# Optimizing a Trainium2 kernel written in Bass

```python
import numpy as np
import jax
import jax.numpy as jnp

def _softmax(x, axis=-1):
    return jax.nn.softmax(x, axis=axis)

def _gelu(x):
    return jax.nn.gelu(x, approximate=True)

def _silu(x):
    return jax.nn.silu(x)

def _sigmoid(x):
    return jax.nn.sigmoid(x)

def _layernorm(x, axis=-1, eps=1e-05):
    m = jnp.mean(x, axis=axis, keepdims=True)
    v = jnp.var(x, axis=axis, keepdims=True)
    return (x - m) / jnp.sqrt(v + eps)

def _scatter_add(tgt, idx, src, axis=0):
    return tgt.at[idx].add(src)

def _segment_sum(src, seg, n):
    return jax.ops.segment_sum(src, seg, n)
kernel_name = 'mk_gnn_resnorm_d4_gnn_r64_7f4fcd'

def setup_inputs(seed: int=0):
    np.random.seed(seed)
    _w = jnp.asarray

    def _rec_inputs():
        import jax
        import jax.numpy as jnp
        _gk = jax.random.key(seed)
        x = -0.000202 + 1 * jax.random.normal(jax.random.fold_in(_gk, 1), (50000, 128), jnp.float32)
        src = jax.random.randint(jax.random.fold_in(_gk, 2), (25000,), 0, 50000, jnp.int32)
        dst = jnp.minimum((50000 * jax.random.uniform(jax.random.fold_in(_gk, 3), (25000,)) ** 2.0).astype(jnp.int32), 49999)
        _o = jnp.argsort(dst, stable=True)
        src = src[_o]
        dst = dst[_o]
        edge_weight = jax.random.uniform(jax.random.fold_in(_gk, 13), (25000,), jnp.float32, 0.0, 0.999999)
        return (x, src, dst, edge_weight)
    x, src, dst, edge_weight = _rec_inputs()

    def _L0_gnn_setup():
        import jax, jax.numpy as jnp
        import numpy as np
        N_NODES = 50000
        N_HEDGES = 10000
        NNZ = 9375
        D = 128

        def _hconv(x, W, b, src, dst):
            x = x @ W
            ones = jnp.ones(src.shape, x.dtype)
            deg_n = jax.ops.segment_sum(ones, src, num_segments=N_NODES)
            deg_e = jax.ops.segment_sum(ones, dst, num_segments=N_HEDGES)
            Dinv = jnp.where(deg_n > 0, 1.0 / deg_n, 0.0)
            Binv = jnp.where(deg_e > 0, 1.0 / deg_e, 0.0)
            he = Binv[:, None] * jax.ops.segment_sum(x[src], dst, num_segments=N_HEDGES)
            out = Dinv[:, None] * jax.ops.segment_sum(he[dst], src, num_segments=N_NODES)
            return out + b
        key = jax.random.key(seed)
        k = jax.random.split(key, 6)
        x = jax.random.normal(k[0], (N_NODES, D), jnp.float32)
        src = jax.random.randint(k[1], (NNZ,), 0, N_NODES, dtype=jnp.int32)
        dst = jax.random.randint(k[2], (NNZ,), 0, N_HEDGES, dtype=jnp.int32)
        edge_index = jnp.stack([src, dst], axis=0)
        scale = 1.0 / np.sqrt(D)
        W1 = jax.random.normal(k[3], (D, D), jnp.float32) * scale
        W2 = jax.random.normal(k[4], (D, D), jnp.float32) * scale
        b1 = jnp.zeros((D,), jnp.float32)
        b2 = jnp.zeros((D,), jnp.float32)
        return {'x': x, 'edge_index': edge_index, 'W1': W1, 'b1': b1, 'W2': W2, 'b2': b2}
    _L0_gnn_all = _L0_gnn_setup()
    _L0_gnn_in = {k: v for k, v in _L0_gnn_all.items() if k in ('W1', 'b1', 'W2', 'b2')}
    del _L0_gnn_all

    def _L1_gnn_setup():
        import jax, jax.numpy as jnp
        import numpy as np
        N_NODES = 100000
        key = jax.random.key(seed)
        k1, k2, k3 = jax.random.split(key, 3)
        x = jax.random.normal(k1, (N_NODES, 128), dtype=jnp.float32)
        src_idx = jax.random.randint(k2, (31250,), 0, N_NODES, dtype=jnp.int64)
        dst_idx = jax.random.randint(k3, (31250,), 0, N_NODES, dtype=jnp.int64)
        return {'x': x, 'src_idx': src_idx, 'dst_idx': dst_idx}
    _L1_gnn_all = _L1_gnn_setup()
    _L1_gnn_in = {k: v for k, v in _L1_gnn_all.items() if k in ()}
    del _L1_gnn_all

    def _L2_gnn_setup():
        import jax, jax.numpy as jnp
        import numpy as np
        N, E, D, H, HD, L = (50000, 12500, 128, 4, 32, 5)

        def _layernorm(x, g, b):
            mu = jnp.mean(x, axis=-1, keepdims=True)
            var = jnp.mean(jnp.square(x - mu), axis=-1, keepdims=True)
            return (x - mu) * jax.lax.rsqrt(var + 1e-05) * g + b

        def _conv(x, src, dst, Wq, bq, Wk, bk, Wv, bv, Ws, bs):
            n = x.shape[0]
            q = (x @ Wq + bq).reshape(n, H, HD)
            k = (x @ Wk + bk).reshape(n, H, HD)
            v = (x @ Wv + bv).reshape(n, H, HD)
            alpha = jnp.sum(q[dst] * k[src], axis=-1) / jnp.sqrt(jnp.float32(HD))
            amax = jax.ops.segment_max(alpha, dst, num_segments=n)
            ex = jnp.exp(alpha - amax[dst])
            denom = jax.ops.segment_sum(ex, dst, num_segments=n)
            attn = ex / (denom[dst] + 1e-16)
            msg = v[src] * attn[:, :, None]
            out = jax.ops.segment_sum(msg, dst, num_segments=n).reshape(n, H * HD)
            return out + x @ Ws + bs
        key = jax.random.key(seed)
        ks = jax.random.split(key, 8)
        w = 0.05
        return {'x': jax.random.normal(ks[0], (N, D), jnp.float32), 'edge_index': jax.random.randint(ks[1], (2, E), 0, N, jnp.int64), 'Wq': jax.random.normal(ks[2], (L, D, D), jnp.float32) * w, 'bq': jnp.zeros((L, D), jnp.float32), 'Wk': jax.random.normal(ks[3], (L, D, D), jnp.float32) * w, 'bk': jnp.zeros((L, D), jnp.float32), 'Wv': jax.random.normal(ks[4], (L, D, D), jnp.float32) * w, 'bv': jnp.zeros((L, D), jnp.float32), 'Ws': jax.random.normal(ks[5], (L, D, D), jnp.float32) * w, 'bs': jnp.zeros((L, D), jnp.float32), 'ln_g': jnp.ones((4, D), jnp.float32), 'ln_b': jnp.zeros((4, D), jnp.float32)}
    _L2_gnn_all = _L2_gnn_setup()
    _L2_gnn_in = {k: v for k, v in _L2_gnn_all.items() if k in ('Wq', 'bq', 'Wk', 'bk', 'Wv', 'bv', 'Ws', 'bs', 'ln_g', 'ln_b')}
    del _L2_gnn_all

    def _L3_gnn_setup():
        import jax, jax.numpy as jnp
        import numpy as np
        N_NODES = 50000
        N_EDGES = 12500
        HIDDEN = 128
        key = jax.random.key(seed)
        k1, k2, k3, k4, k5, k6 = jax.random.split(key, 6)
        stdv = 1.0 / np.sqrt(HIDDEN)
        h = jax.random.normal(k1, (N_NODES, HIDDEN), dtype=jnp.float32)
        edge_src = jax.random.randint(k2, (N_EDGES,), 0, N_NODES, dtype=jnp.int32)
        edge_dst = jax.random.randint(k3, (N_EDGES,), 0, N_NODES, dtype=jnp.int32)
        edge_val = jax.random.uniform(k4, (N_EDGES,), dtype=jnp.float32)
        weight = jax.random.uniform(k5, (HIDDEN, HIDDEN), dtype=jnp.float32, minval=-stdv, maxval=stdv)
        bias = jax.random.uniform(k6, (HIDDEN,), dtype=jnp.float32, minval=-stdv, maxval=stdv)
        return {'h': h, 'edge_src': edge_src, 'edge_dst': edge_dst, 'edge_val': edge_val, 'weight': weight, 'bias': bias}
    _L3_gnn_all = _L3_gnn_setup()
    _L3_gnn_in = {k: v for k, v in _L3_gnn_all.items() if k in ('weight', 'bias')}
    del _L3_gnn_all
    return {'x': x, 'src': src, 'dst': dst, 'edge_weight': edge_weight, 'L0_gnn_W1': _L0_gnn_in['W1'], 'L0_gnn_b1': _L0_gnn_in['b1'], 'L0_gnn_W2': _L0_gnn_in['W2'], 'L0_gnn_b2': _L0_gnn_in['b2'], 'L2_gnn_Wq': _L2_gnn_in['Wq'], 'L2_gnn_bq': _L2_gnn_in['bq'], 'L2_gnn_Wk': _L2_gnn_in['Wk'], 'L2_gnn_bk': _L2_gnn_in['bk'], 'L2_gnn_Wv': _L2_gnn_in['Wv'], 'L2_gnn_bv': _L2_gnn_in['bv'], 'L2_gnn_Ws': _L2_gnn_in['Ws'], 'L2_gnn_bs': _L2_gnn_in['bs'], 'L2_gnn_ln_g': _L2_gnn_in['ln_g'], 'L2_gnn_ln_b': _L2_gnn_in['ln_b'], 'L3_gnn_weight': _L3_gnn_in['weight'], 'L3_gnn_bias': _L3_gnn_in['bias']}

def reference(x, src, dst, edge_weight, L0_gnn_W1, L0_gnn_b1, L0_gnn_W2, L0_gnn_b2, L2_gnn_Wq, L2_gnn_bq, L2_gnn_Wk, L2_gnn_bk, L2_gnn_Wv, L2_gnn_bv, L2_gnn_Ws, L2_gnn_bs, L2_gnn_ln_g, L2_gnn_ln_b, L3_gnn_weight, L3_gnn_bias):
    import jax
    import jax.numpy as jnp

    def _L0_gnn_ref(x, edge_index, W1, b1, W2, b2):
        import jax, jax.numpy as jnp
        import numpy as np
        N_NODES = 50000
        N_HEDGES = 10000
        NNZ = 9375
        D = 128

        def _hconv(x, W, b, src, dst):
            x = x @ W
            ones = jnp.ones(src.shape, x.dtype)
            deg_n = jax.ops.segment_sum(ones, src, num_segments=N_NODES)
            deg_e = jax.ops.segment_sum(ones, dst, num_segments=N_HEDGES)
            Dinv = jnp.where(deg_n > 0, 1.0 / deg_n, 0.0)
            Binv = jnp.where(deg_e > 0, 1.0 / deg_e, 0.0)
            he = Binv[:, None] * jax.ops.segment_sum(x[src], dst, num_segments=N_HEDGES)
            out = Dinv[:, None] * jax.ops.segment_sum(he[dst], src, num_segments=N_NODES)
            return out + b
        src, dst = (edge_index[0], edge_index[1])
        h = _hconv(x, W1, b1, src, dst)
        h = jax.nn.relu(h)
        return _hconv(h, W2, b2, src, dst)

    def _L1_gnn_ref(x, src_idx, dst_idx):
        import jax, jax.numpy as jnp
        import numpy as np
        N_NODES = 100000
        x_j = x[src_idx]
        agg = jax.ops.segment_sum(x_j, dst_idx, num_segments=x.shape[0])
        return x + agg

    def _L2_gnn_ref(x, edge_index, Wq, bq, Wk, bk, Wv, bv, Ws, bs, ln_g, ln_b):
        import jax, jax.numpy as jnp
        import numpy as np
        N, E, D, H, HD, L = (50000, 12500, 128, 4, 32, 5)

        def _layernorm(x, g, b):
            mu = jnp.mean(x, axis=-1, keepdims=True)
            var = jnp.mean(jnp.square(x - mu), axis=-1, keepdims=True)
            return (x - mu) * jax.lax.rsqrt(var + 1e-05) * g + b

        def _conv(x, src, dst, Wq, bq, Wk, bk, Wv, bv, Ws, bs):
            n = x.shape[0]
            q = (x @ Wq + bq).reshape(n, H, HD)
            k = (x @ Wk + bk).reshape(n, H, HD)
            v = (x @ Wv + bv).reshape(n, H, HD)
            alpha = jnp.sum(q[dst] * k[src], axis=-1) / jnp.sqrt(jnp.float32(HD))
            amax = jax.ops.segment_max(alpha, dst, num_segments=n)
            ex = jnp.exp(alpha - amax[dst])
            denom = jax.ops.segment_sum(ex, dst, num_segments=n)
            attn = ex / (denom[dst] + 1e-16)
            msg = v[src] * attn[:, :, None]
            out = jax.ops.segment_sum(msg, dst, num_segments=n).reshape(n, H * HD)
            return out + x @ Ws + bs
        src, dst = (edge_index[0], edge_index[1])
        gelu = lambda t: jax.nn.gelu(t, approximate=False)
        res = x
        h = _conv(x, src, dst, Wq[0], bq[0], Wk[0], bk[0], Wv[0], bv[0], Ws[0], bs[0])
        h = gelu(_layernorm(h, ln_g[0], ln_b[0])) + res
        for i in range(1, 4):
            res = h
            h = _conv(h, src, dst, Wq[i], bq[i], Wk[i], bk[i], Wv[i], bv[i], Ws[i], bs[i])
            h = gelu(_layernorm(h, ln_g[i], ln_b[i])) + res
        h = _conv(h, src, dst, Wq[4], bq[4], Wk[4], bk[4], Wv[4], bv[4], Ws[4], bs[4])
        return gelu(h)

    def _L3_gnn_ref(h, edge_src, edge_dst, edge_val, weight, bias):
        import jax, jax.numpy as jnp
        import numpy as np
        N_NODES = 50000
        N_EDGES = 12500
        HIDDEN = 128
        support = jnp.matmul(h, weight)
        msgs = edge_val[:, None] * support[edge_src]
        out = jax.ops.segment_sum(msgs, edge_dst, num_segments=N_NODES)
        out = out + bias
        out = jax.nn.relu(out)
        return out
    edge_index = jnp.stack([src, dst])
    x = _layernorm(x + _L0_gnn_ref(x, edge_index, L0_gnn_W1, L0_gnn_b1, L0_gnn_W2, L0_gnn_b2), axis=-1)
    x = _layernorm(x + _L1_gnn_ref(x, src, dst), axis=-1)
    x = _layernorm(x + _L2_gnn_ref(x, edge_index, L2_gnn_Wq, L2_gnn_bq, L2_gnn_Wk, L2_gnn_bk, L2_gnn_Wv, L2_gnn_bv, L2_gnn_Ws, L2_gnn_bs, L2_gnn_ln_g, L2_gnn_ln_b), axis=-1)
    x = _layernorm(x + _L3_gnn_ref(x, src, dst, edge_weight, L3_gnn_weight, L3_gnn_bias), axis=-1)
    return x

_drawn_inputs = setup_inputs


def setup_inputs(seed=0):
    import zlib

    import numpy as np

    out = dict(_drawn_inputs(seed))
    spreads = {'L0_gnn_b1': (0.0, 0.269),
     'L0_gnn_b2': (0.0, 0.1),
     'L2_gnn_bq': (0.0, 0.8),
     'L2_gnn_bk': (0.0, 0.8),
     'L2_gnn_bv': (0.0, 0.1),
     'L2_gnn_bs': (0.0, 0.1),
     'L2_gnn_ln_g': (1.0, 0.2),
     'L2_gnn_ln_b': (0.0, 0.1)}
    factors = {}
    for name, (base, spread) in spreads.items():
        noise = np.random.default_rng([zlib.crc32(name.encode()), seed]).standard_normal(out[name].shape)
        drawn = base * np.exp(spread * noise) if base else spread * noise
        out[name] = jnp.asarray(drawn.astype(out[name].dtype))
    for name, factor in factors.items():
        out[name] = (out[name] * factor).astype(out[name].dtype)
    return out
```

```python
from contextlib import ExitStack

import concourse.bass as bass
from concourse import mybir

F32 = mybir.dt.float32
I32 = mybir.dt.int32
BF16 = mybir.dt.bfloat16
ALU = mybir.AluOpType
ACT = mybir.ActivationFunctionType

P = 128
D = 128
HEADS = 4
HD = D // HEADS
N = 50000
NH = 10000
E = 25000
LAYERS = 5
EPS = 1e-5

T = -(-E // P)
EP = T * P
FULL = E // T
REST = E - FULL * T
U = 4
C = U * P
NC = T // U
DIG = 256
HALF = T // 2
PADKEY = N
TRASH = N + 1
BIG = 1e30
FILL = 5000

NP = 125
RP = N // NP
G = 8
NG = RP // G
SPLIT = 112

assert T % U == 0 and NC % 2 == 1 and NG % 2 == 0 and NP * RP == N

SRC_D, DST_D, OUT_D, OUT_HE, WEIGHT, HE_S, OUT_S, CNT_D, CNT_S = range(9)
NCOL = 9


class Program:
    pass


def chunks(eng, body):
    for c in range(2):
        body(c, 0, c, False)
    with eng.Fori(1, NC // 2) as i:
        body(2 * i, i, 0, True)
        body(2 * i + 1, i, 1, True)
    body(NC - 1, NC // 2, 0, True)


def signals(nc, ctx):
    taken = []

    def clear():
        nc.clear_and_free_semaphores(taken)
        nc.all_engine_barrier()

    def sem(name):
        taken.append(nc.alloc_semaphore(name))
        return taken[-1]

    ctx.callback(clear)
    return sem


def constants(nc, life, g):
    def sb(name, shape, dt):
        return life.enter_context(nc.sbuf_tensor(name, shape, dt))

    g.ident = sb("ident", [P, P], F32)
    g.before = sb("before", [P, P], BF16)
    g.notbefore = sb("notbefore", [P, P], BF16)
    g.ones = sb("ones", [P, P], BF16)
    g.heads = sb("heads", [P, P], F32)
    g.digits = sb("digits", [P, DIG], BF16)
    g.col = sb("col", [P, NCOL, T], F32)
    g.idx = sb("idx", [P, NCOL, T], I32)
    g.same_d = sb("same_d", [P, EP], BF16)
    g.same_s = sb("same_s", [P, EP], BF16)
    with ExitStack() as ctx:
        sem = signals(nc, ctx)
        digits_i = ctx.enter_context(nc.sbuf_tensor("digits_i", [P, DIG], I32))
        set_up = sem("set_up")
        iota_done = sem("iota_done")
        all_done = sem("all_done")
        block = ctx.enter_context(nc.Block())
        @block.vector
        def _(dve):
            nc.vector.memset(g.ident[:, :], 0.0).then_inc(set_up, 1)
            nc.vector.memset(g.before[:, :], 1.0).then_inc(set_up, 1)
            nc.vector.memset(g.notbefore[:, :], 1.0).then_inc(set_up, 1)
            nc.vector.memset(g.ones[:, :], 1.0).then_inc(all_done, 1)
            nc.vector.memset(g.heads[:, :], 0.0).then_inc(set_up, 1)
            dve.wait_ge(set_up, 4)
            for h in range(HEADS):
                s = slice(h * HD, h * HD + HD)
                nc.vector.memset(g.heads[s, s], 1.0).then_inc(all_done, 1)
            dve.wait_ge(iota_done, 1)
            nc.vector.tensor_copy(g.digits[:, :], digits_i[:, :]).then_inc(all_done, 1)
            dve.wait_ge(all_done, HEADS + 2)

        @block.gpsimd
        def _(pool):
            nc.gpsimd.iota(digits_i[:, :], pattern=[[1, DIG]], base=0, channel_multiplier=0).then_inc(iota_done, 1)
            pool.wait_ge(set_up, 4)
            nc.gpsimd.affine_select(out=g.ident[:, :], in_=g.ident[:, :], compare_op=ALU.not_equal, fill=1.0,
                                    base=0, pattern=[[-1, P]], channel_multiplier=1)
            nc.gpsimd.affine_select(out=g.before[:, :], in_=g.before[:, :], compare_op=ALU.is_gt, fill=0.0,
                                    base=0, pattern=[[1, P]], channel_multiplier=-1)
            nc.gpsimd.affine_select(out=g.notbefore[:, :], in_=g.notbefore[:, :], compare_op=ALU.is_ge, fill=0.0,
                                    base=0, pattern=[[-1, P]], channel_multiplier=1).then_inc(iota_done, 1)
            pool.wait_ge(iota_done, 2)


def count_digits(nc, g, dst, src, weight, pay, digit, counts):
    with ExitStack() as ctx:
        sem = signals(nc, ctx)
        raw = ctx.enter_context(nc.sbuf_tensor("raw", [P, 2, T], I32))
        low = ctx.enter_context(nc.sbuf_tensor("low", [P, 4, T], I32))
        smaller = ctx.enter_context(nc.sbuf_tensor("smaller", [P, 4, U, DIG], BF16))
        nothing = ctx.enter_context(nc.sbuf_tensor("nothing", [P, DIG], BF16))
        zero = ctx.enter_context(nc.sbuf_tensor("zero", [NP, FILL * D // NP], F32))
        cleared = sem("cleared")
        loaded = sem("loaded")
        nothing_ready = sem("nothing_ready")
        zero_ready = sem("zero_ready")
        zeros_stored = sem("zeros_stored")
        copied = sem("copied")
        masked = sem("masked")
        digits_ready = sem("digits_ready")
        smaller_ready = sem("smaller_ready")
        smaller_used = sem("smaller_used")
        block = ctx.enter_context(nc.Block())
        zero_fills = [(t, r) for t, rows in ((g.agg_s, N), (g.agg_d, N), (g.he, NH))
                      for r in range(0, rows, FILL)]

        @block.sync
        def _(sp):
            sp.wait_ge(cleared, 2)
            for k, x in enumerate((dst, src)):
                sp.dma_start(raw[0:FULL, k, :], x[0:FULL * T].rearrange("(p t) -> p t", t=T)).then_inc(loaded, 16)
                sp.dma_start(raw[FULL:FULL + 1, k, 0:REST],
                             x[FULL * T:E].rearrange("(a t) -> a t", a=1)).then_inc(loaded, 16)
            sp.dma_start(g.idx[0:FULL, WEIGHT, :].bitcast(F32),
                         weight[0:FULL * T].rearrange("(p t) -> p t", t=T)).then_inc(loaded, 16)
            sp.dma_start(g.idx[FULL:FULL + 1, WEIGHT, 0:REST].bitcast(F32),
                         weight[FULL * T:E].rearrange("(a t) -> a t", a=1)).then_inc(loaded, 16)
            sp.wait_ge(zero_ready, 1)
            for t, r in zero_fills:
                sp.dma_start(t[r:r + FILL, :].rearrange("(p a) f -> p (a f)", p=NP),
                             zero[:, :]).then_inc(zeros_stored, 16)
            sp.wait_ge(zeros_stored, 16 * len(zero_fills))

        @block.vector
        def _(dve):
            nc.vector.memset(raw[:, :, :], PADKEY).then_inc(cleared, 1)
            nc.vector.memset(g.idx[:, WEIGHT, :].bitcast(F32), 0.0).then_inc(cleared, 1)
            nc.vector.memset(pay[:, :, 3], 0.0)
            nc.vector.memset(nothing[:, :], 0.0).then_inc(nothing_ready, 1)
            dve.wait_ge(loaded, 6 * 16)
            nc.vector.tensor_copy(pay[:, :, 0], raw[:, 0, :]).then_inc(copied, 1)
            nc.vector.tensor_copy(pay[:, :, 1], raw[:, 1, :]).then_inc(copied, 1)
            nc.vector.tensor_copy(pay[:, :, 2], g.idx[:, WEIGHT, :].bitcast(F32)).then_inc(copied, 1)
            for k in range(2):
                nc.vector.tensor_scalar(low[:, 2 * k, :], raw[:, k, :], DIG - 1, None,
                                        ALU.bitwise_and).then_inc(masked, 1)
                nc.vector.tensor_scalar(low[:, 2 * k + 1, :], raw[:, k, :], 8, None,
                                        ALU.arith_shift_right).then_inc(masked, 1)
            dve.wait_ge(masked, 4)
            nc.vector.tensor_copy(digit[:, :, :], low[:, :, :]).then_inc(digits_ready, 1)
            dve.wait_ge(digits_ready, 1)

            def compare(c, i, par, steady):
                for u in range(U):
                    for k in range(4):
                        if u == 0 and k == 0 and (steady or par):
                            dve.wait_ge(smaller_used, c)
                        nc.vector.tensor_scalar(smaller[:, k, u, :], g.digits[:, :],
                                                digit[:, k, bass.ds(c * U + u, 1)], None,
                                                ALU.is_gt).then_inc(smaller_ready, 1)

            chunks(dve, compare)

        @block.gpsimd
        def _(pool):
            nc.gpsimd.memset(zero[:, :], 0.0).then_inc(zero_ready, 1)

        @block.tensor
        def _(pe):
            pe.wait_ge(nothing_ready, 1)
            for k in range(4):
                nc.tensor.matmul(counts[:, k, 0:DIG], g.ones[:, :], nothing[:, :], start=True, stop=False,
                                 skip_group_check=True)

            def add(c, i, par, steady):
                for u in range(U):
                    pe.wait_ge(smaller_ready, 4 * U * c + 4 * u + 4)
                    for k in range(4):
                        last = nc.tensor.matmul(counts[:, k, 0:DIG], g.ones[:, :], smaller[:, k, u, :],
                                                start=False, stop=False, skip_group_check=True)
                last.then_inc(smaller_used, 1)

            chunks(pe, add)


def rank_pass(nc, g, which, digit, pay, counts, tables, shift):
    with ExitStack() as ctx:
        sem = signals(nc, ctx)
        equal = ctx.enter_context(nc.sbuf_tensor(f"equal_{which}", [P, 2, U, DIG], BF16))
        unused = ctx.enter_context(nc.sbuf_tensor(f"unused_{which}", [P, 2, DIG], F32))
        place = ctx.enter_context(nc.sbuf_tensor(f"place_{which}", [P, 2, 2, U], F32))
        place_i = ctx.enter_context(nc.sbuf_tensor(f"place_i_{which}", [P, 2, 2, U], I32))
        row = ctx.enter_context(nc.sbuf_tensor(f"row_{which}", [P, 2, 2, U, 4], F32))
        er0 = sem(f"equal_ready0_{which}")
        er1 = sem(f"equal_ready1_{which}")
        rk0 = sem(f"ranked0_{which}")
        rk1 = sem(f"ranked1_{which}")
        rd0 = sem(f"read0_{which}")
        rd1 = sem(f"read1_{which}")
        mo0 = sem(f"moved_on0_{which}")
        mo1 = sem(f"moved_on1_{which}")
        rows_ready = sem(f"rows_ready_{which}")
        st0 = sem(f"stored0_{which}")
        st1 = sem(f"stored1_{which}")
        block = ctx.enter_context(nc.Block())
        equal_ready, ranked, read, moved_on, stored = (er0, er1), (rk0, rk1), (rd0, rd1), (mo0, mo1), (st0, st1)

        @block.vector
        def _(dve):
            def body(c, i, par, steady):
                def one_hot(u):
                    for k in range(2):
                        if steady or par:
                            dve.wait_ge(moved_on[k], U * c - U + u + 1)
                        nc.vector.tensor_scalar(equal[:, k, u, :], g.digits[:, :],
                                                digit[k][:, bass.ds(c * U + u, 1)], None,
                                                ALU.is_equal).then_inc(equal_ready[k], 1)

                one_hot(0)
                if steady:
                    dve.wait_ge(stored[par], 2 * U * 16 * i)
                for k in range(2):
                    nc.vector.tensor_copy(row[:, par, k, :, :], pay[k][:, bass.ds(c * U, U), :])
                for u in range(U):
                    if u + 1 < U:
                        one_hot(u + 1)
                    for k in range(2):
                        dve.wait_ge(ranked[k], U * c + u + 1)
                        nc.vector.tensor_tensor_reduce(unused[:, k, :], equal[:, k, u, :],
                                                       counts[:, 2 * k + which, 0:DIG], 1.0, 0.0, ALU.mult,
                                                       ALU.add, place[:, par, k, u:u + 1]).then_inc(read[k], 1)
                for k in range(2):
                    dve.wait_ge(read[k], U * c + U)
                    nc.vector.tensor_scalar(place_i[:, par, k, :], place[:, par, k, :], float(shift), None,
                                            ALU.add).then_inc(rows_ready, 1)

            chunks(dve, body)

        @block.tensor
        def _(pe):
            def body(c, i, par, steady):
                for u in range(U):
                    for k in range(2):
                        pe.wait_ge(equal_ready[k], U * c + u + 1)
                        nc.tensor.matmul(counts[:, 2 * k + which, 0:DIG], g.before[:, :], equal[:, k, u, :],
                                         start=False, stop=False, skip_group_check=True).then_inc(ranked[k], 1)
                    for k in range(2):
                        pe.wait_ge(read[k], U * c + u + 1)
                        nc.tensor.matmul(counts[:, 2 * k + which, 0:DIG], g.notbefore[:, :], equal[:, k, u, :],
                                         start=False, stop=False, skip_group_check=True).then_inc(moved_on[k], 1)

            chunks(pe, body)

        @block.gpsimd
        def _(pool):
            def body(c, i, par, steady):
                pool.wait_ge(rows_ready, 2 * c + 2)
                pool.nop(nofuse=True)
                for k in range(2):
                    for u in range(U):
                        nc.gpsimd.indirect_dma_start(
                            out=tables[k][:, :],
                            out_offset=bass.IndirectOffsetOnAxis(ap=place_i[:, par, k, u:u + 1], axis=0),
                            in_=row[:, par, k, u, :], in_offset=None).then_inc(stored[par], 16)

            chunks(pool, body)
            pool.wait_ge(st0, (NC // 2 + 1) * 2 * U * 16)
            pool.wait_ge(st1, (NC // 2) * 2 * U * 16)


def second_digit(nc, g, tables, digit, pay):
    with ExitStack() as ctx:
        sem = signals(nc, ctx)
        rows = ctx.enter_context(nc.sbuf_tensor("rows", [HALF, 2, 2, P * 4], F32))
        key_i = ctx.enter_context(nc.sbuf_tensor("key_i", [P, 2, T], I32))
        high_i = ctx.enter_context(nc.sbuf_tensor("high_i", [P, 2, T], I32))
        turned = ctx.enter_context(nc.psum_tensor("turned", [P, 2, 4, P], F32))
        rows_loaded = sem("rows_loaded")
        turned_ready = sem("turned_ready")
        turned_read = sem("turned_read")
        keys_ready = sem("keys_ready")
        high_ready = sem("high_ready")
        high_done = sem("high_done")
        block = ctx.enter_context(nc.Block())
        @block.sync
        def _(sp):
            for k in range(2):
                sp.dma_start(rows[:, k, :, :], tables[k][0:EP, :].rearrange("(h q p) f -> q h (p f)", h=2, p=P)
                             ).then_inc(rows_loaded, 16)

        @block.tensor
        def _(pe):
            pe.wait_ge(rows_loaded, 32)
            for n, (k, h) in enumerate([(k, h) for k in range(2) for h in range(2)]):
                if n >= 2:
                    pe.wait_ge(turned_read, n - 1)
                for f in range(3):
                    part = rows[:, k, h, :].rearrange("q (p f) -> q f p", f=4)[:, f, :]
                    last = nc.tensor.transpose(turned[:, n % 2, f, 0:HALF], part, g.ident[0:HALF, 0:HALF])
                last.then_inc(turned_ready, 1)

        @block.vector
        def _(dve):
            nc.vector.memset(pay[0][:, :, 3], 0.0)
            nc.vector.memset(pay[1][:, :, 3], 0.0)
            for n, (k, h) in enumerate([(k, h) for k in range(2) for h in range(2)]):
                dve.wait_ge(turned_ready, n + 1)
                nc.vector.tensor_copy(key_i[:, k, h * HALF:h * HALF + HALF],
                                      turned[:, n % 2, k, 0:HALF]).then_inc(keys_ready, 1)
                for f in range(3):
                    last = nc.vector.tensor_copy(pay[k][:, h * HALF:h * HALF + HALF, f],
                                                 turned[:, n % 2, f, 0:HALF])
                last.then_inc(turned_read, 1)
            dve.wait_ge(keys_ready, 4)
            nc.vector.tensor_scalar(high_i[:, :, :], key_i[:, :, :], 8, None,
                                    ALU.arith_shift_right).then_inc(high_ready, 1)
            dve.wait_ge(high_ready, 1)
            for k in range(2):
                nc.vector.tensor_copy(digit[k], high_i[:, k, :]).then_inc(high_done, 1)
            dve.wait_ge(high_done, 2)
            dve.wait_ge(turned_read, 4)


def describe(nc, g, tables, cols, same_rows):
    with ExitStack() as ctx:
        sem = signals(nc, ctx)
        ends = ctx.enter_context(nc.sbuf_tensor("ends", [1, 4], F32))
        win = ctx.enter_context(nc.sbuf_tensor("win", [P, 2, T + 2, 4], F32))
        number = ctx.enter_context(nc.sbuf_tensor("number", [P, T], F32))
        number_i = ctx.enter_context(nc.sbuf_tensor("number_i", [P, T], I32))
        same = ctx.enter_context(nc.sbuf_tensor("same", [P, 2, T], BF16))
        last = ctx.enter_context(nc.sbuf_tensor("last", [P, 3, T], F32))
        small = ctx.enter_context(nc.sbuf_tensor("small", [P, T], F32))
        away = ctx.enter_context(nc.sbuf_tensor("away", [P, 3, T], F32))
        made = ctx.enter_context(nc.sbuf_tensor("made", [P, NCOL, T], F32))
        tmp = ctx.enter_context(nc.sbuf_tensor("tmp", [P, 3, T], F32))
        one = ctx.enter_context(nc.sbuf_tensor("one", [2, EP // 8], F32))
        count = ctx.enter_context(nc.sbuf_tensor("count", [2, 2, EP // 8], F32))
        lines = ctx.enter_context(nc.sbuf_tensor("lines", [HALF, NCOL, 2, P], F32))
        turned = ctx.enter_context(nc.psum_tensor("turned2", [P, 2, 4, P], F32))
        numbered = sem("numbered")
        ends_set = sem("ends_set")
        ends_stored = sem("ends_stored")
        win_loaded = sem("win_loaded")
        step = sem("step")
        same_ready = sem("same_ready")
        same_stored = sem("same_stored")
        flags_loaded = sem("flags_loaded")
        spread_loaded = sem("spread_loaded")
        made_ready = sem("made_ready")
        made_stored = sem("made_stored")
        counted = sem("counted")
        cs0 = sem("count_stored0")
        cs1 = sem("count_stored1")
        lines_loaded = sem("lines_loaded")
        turned_ready = sem("turned_ready2")
        turned_read = sem("turned_read2")
        block = ctx.enter_context(nc.Block())
        S = EP // 8
        count_stored = (cs0, cs1)
        flags = g.same_s[0:2, :]

        @block.sync
        def _(sp):
            sp.wait_ge(ends_set, 1)
            for k in range(2):
                for r in (0, EP + 1):
                    sp.dma_start(tables[k][r:r + 1, :], ends[:, :]).then_inc(ends_stored, 16)
            sp.wait_ge(ends_stored, 64)
            for k in range(2):
                t = tables[k][0:1, :]
                src = bass.AP(t.tensor, 0, [[T * 4, P], [1, (T + 2) * 4]])
                sp.dma_start(win[:, k, :, :].rearrange("p t f -> p (t f)"), src).then_inc(win_loaded, 16)
            sp.wait_ge(same_ready, 2)
            for k in range(2):
                sp.dma_start(same_rows[k:k + 1, :].rearrange("a (p t) -> (a p) t", t=T),
                             same[:, k, :]).then_inc(same_stored, 16)
            sp.wait_ge(same_stored, 32)
            sp.dma_start(flags[:, :], same_rows[:, :]).then_inc(flags_loaded, 16)
            sp.dma_start(g.same_d[:, :], same_rows[0:1, :].to_broadcast([P, EP])).then_inc(spread_loaded, 16)
            sp.wait_ge(made_ready, 1)
            for k in range(NCOL - 2):
                sp.dma_start(cols[k:k + 1, :].rearrange("a (p t) -> (a p) t", t=T),
                             made[:, k, :]).then_inc(made_stored, 16)
            for n in range(8):
                sp.wait_ge(counted, n + 1)
                sp.dma_start(cols[CNT_D:CNT_S + 1, n * S:n * S + S], count[:, n % 2, :]).then_inc(count_stored[n % 2], 16)
            sp.dma_start(g.same_s[:, :], same_rows[1:2, :].to_broadcast([P, EP])).then_inc(spread_loaded, 16)
            sp.wait_ge(cs0, 64)
            sp.wait_ge(cs1, 64)
            sp.wait_ge(made_stored, 16 * (NCOL - 2))
            for k in range(NCOL):
                sp.dma_start(lines[:, k, :, :], cols[k:k + 1, :].rearrange("a (h q p) -> (a q) h p", h=2, p=P)
                             ).then_inc(lines_loaded, 16)
            sp.wait_ge(spread_loaded, 32)

        @block.gpsimd
        def _(pool):
            nc.gpsimd.iota(number_i[:, :], pattern=[[1, T]], base=0, channel_multiplier=T).then_inc(numbered, 1)

        @block.vector
        def _(dve):
            at = [0]

            def link(ins):
                at[0] += 1
                ins.then_inc(step, 1)
                dve.wait_ge(step, at[0])

            nc.vector.memset(ends[:, :], -1.0).then_inc(ends_set, 1)
            link(nc.vector.memset(one[:, :], 1.0))
            dve.wait_ge(numbered, 1)
            link(nc.vector.tensor_copy(number[:, :], number_i[:, :]))
            dve.wait_ge(win_loaded, 32)
            for k in range(2):
                key = win[:, k, 1:T + 1, k]
                nc.vector.tensor_tensor(same[:, k, :], key, win[:, k, 0:T, k], ALU.is_equal).then_inc(same_ready, 1)
                nc.vector.tensor_tensor(last[:, k, :], key, win[:, k, 2:T + 2, k], ALU.not_equal)
            nc.vector.tensor_scalar(away[:, 0, :], number[:, :], float(TRASH), None, ALU.add)
            nc.vector.tensor_scalar(away[:, 1, :], number[:, :], float(TRASH), None, ALU.add)
            nc.vector.tensor_scalar(away[:, 2, :], number[:, :], float(NH), None, ALU.add)
            link(nc.vector.tensor_scalar(small[:, :], win[:, 0, 1:T + 1, 0], float(NH), None, ALU.is_lt))
            link(nc.vector.tensor_tensor(last[:, 2, :], last[:, 0, :], small[:, :], ALU.mult))
            for n, (k, to) in enumerate(((0, OUT_D), (1, OUT_S), (0, OUT_HE))):
                link(nc.vector.tensor_tensor(tmp[:, n, :], win[:, k, 1:T + 1, k], away[:, n, :], ALU.subtract))
                link(nc.vector.tensor_tensor(tmp[:, n, :], tmp[:, n, :], last[:, n, :], ALU.mult))
                link(nc.vector.tensor_tensor(made[:, to, :], tmp[:, n, :], away[:, n, :], ALU.add))
            nc.vector.tensor_scalar(made[:, SRC_D, :], win[:, 0, 1:T + 1, 1], float(N - 1), None, ALU.min)
            nc.vector.tensor_scalar(made[:, DST_D, :], win[:, 0, 1:T + 1, 0], float(N - 1), None, ALU.min)
            nc.vector.tensor_scalar(made[:, HE_S, :], win[:, 1, 1:T + 1, 0], float(NH - 1), None, ALU.min)
            nc.vector.tensor_copy(made[:, WEIGHT, :], win[:, 0, 1:T + 1, 2]).then_inc(made_ready, 1)
            dve.wait_ge(flags_loaded, 16)
            for n in range(8):
                if n >= 2:
                    dve.wait_ge(count_stored[n % 2], 16 * (n // 2))
                if n:
                    dve.wait_ge(counted, n)
                nc.vector.tensor_tensor_scan(count[:, n % 2, :], flags[:, n * S:n * S + S], one[:, :],
                                             count[:, 1 - n % 2, S - 1:S] if n else 0.0,
                                             ALU.mult, ALU.add).then_inc(counted, 1)
            for n in range(NCOL):
                dve.wait_ge(turned_ready, n + 1)
                link(nc.vector.tensor_copy(g.col[:, n, :].rearrange("p (h q) -> p h q", h=2),
                                           turned[:, n % 2, 0:2, 0:HALF]))
                nc.vector.tensor_copy(g.idx[:, n, :], g.col[:, n, :]).then_inc(turned_read, 1)
            dve.wait_ge(turned_read, NCOL)
            link(nc.vector.reciprocal(g.col[:, CNT_D:CNT_S + 1, :], g.col[:, CNT_D:CNT_S + 1, :]))

        @block.tensor
        def _(pe):
            pe.wait_ge(lines_loaded, 16 * NCOL)
            for n in range(NCOL):
                if n >= 2:
                    pe.wait_ge(turned_read, n - 1)
                for h in range(2):
                    t = nc.tensor.transpose(turned[:, n % 2, h, 0:HALF], lines[:, n, h, :], g.ident[0:HALF, 0:HALF])
                t.then_inc(turned_ready, 1)


def sum_segments(nc, g, name, table, same, source, target, out, weight=None, relu_bias=None, w=None, scale=None):
    with ExitStack() as ctx:
        def sb(n, shape, dt):
            return ctx.enter_context(nc.sbuf_tensor(name + n, shape, dt))

        signal = signals(nc, ctx)

        def sem(n):
            return signal(name + n)

        rows = sb("rows", [P, 2, U, D], F32)
        weighted = sb("weighted", [P, 2, U, D], F32)
        message = sb("message", [P, 2, C], F32)
        total = sb("total", [P, 2, C], F32)
        done = sb("done", [P, 2, U, D], F32)
        source_rows = sb("source_rows", [P, 2, U], I32)
        target_rows = sb("target_rows", [P, 2, U], I32)
        w_sb = sb("w", [D, D], F32)
        bias_sb = sb("bias", [D, 1], F32)
        turned = ctx.enter_context(nc.psum_tensor(name + "turned", [P, 2, C], F32))
        back = ctx.enter_context(nc.psum_tensor(name + "back", [P, 2, U, D], F32))

        at_copied = sem("at_copied")
        gathered = (sem("gathered0"), sem("gathered1"))
        scattered = (sem("scattered0"), sem("scattered1"))
        weights_loaded = sem("weights_loaded")
        rows_weighted = sem("rows_weighted")
        message_turned = sem("message_turned")
        message_ready = sem("message_ready")
        summed = sem("summed")
        turned_back = sem("turned_back")
        rows_ready = sem("rows_ready")
        block = ctx.enter_context(nc.Block())
        n_loads = (w is not None) + (relu_bias is not None)

        @block.sync
        def _(sp):
            if w is not None:
                sp.dma_start(w_sb[:, :], w).then_inc(weights_loaded, 16)
            if relu_bias is not None:
                sp.dma_start(bias_sb[:, :], relu_bias.rearrange("(p a) -> p a", a=1)).then_inc(weights_loaded, 16)

        @block.gpsimd
        def _(pool):
            def fetch(c, i, par, steady):
                if steady:
                    pool.wait_ge(rows_weighted if weight is not None else message_turned, c - 1)
                nc.gpsimd.tensor_copy(source_rows[:, par, :], g.idx[:, source, bass.ds(c * U, U)]).then_inc(at_copied, 1)
                pool.wait_ge(at_copied, 2 * c - 1 if steady else c + 1)
                pool.nop(nofuse=True)
                for u in range(U):
                    nc.gpsimd.indirect_dma_start(
                        out=rows[:, par, u, :], out_offset=None, in_=table,
                        in_offset=bass.IndirectOffsetOnAxis(ap=source_rows[:, par, u:u + 1], axis=0)
                    ).then_inc(gathered[par], 16)

            def send(c, i, par, steady, copies):
                if steady:
                    pool.wait_ge(scattered[par], 16 * U * i)
                nc.gpsimd.tensor_copy(target_rows[:, par, :], g.idx[:, target, bass.ds(c * U, U)]).then_inc(at_copied, 1)
                pool.wait_ge(at_copied, copies)
                pool.wait_ge(rows_ready, c + 1)
                pool.nop(nofuse=True)
                for u in range(U):
                    nc.gpsimd.indirect_dma_start(
                        out=out, out_offset=bass.IndirectOffsetOnAxis(ap=target_rows[:, par, u:u + 1], axis=0),
                        in_=done[:, par, u, :], in_offset=None).then_inc(scattered[par], 16)

            fetch(0, 0, 0, False)
            fetch(1, 0, 1, False)
            for c in (2, 3):
                fetch(c, 1, c % 2, True)
                send(c - 2, 0, c % 2, False, 2 * c)
            with pool.Fori(2, NC // 2) as i:
                for par in range(2):
                    fetch(2 * i + par, i, par, True)
                    send(2 * i + par - 2, i - 1, par, True, 4 * i + 2 * par)
            fetch(NC - 1, NC // 2, 0, True)
            send(NC - 3, NC // 2 - 1, 0, True, 2 * NC - 2)
            send(NC - 2, NC // 2 - 1, 1, True, 2 * NC - 1)
            send(NC - 1, NC // 2, 0, True, 2 * NC)
            pool.wait_ge(scattered[0], 16 * U * (NC // 2 + 1))
            pool.wait_ge(scattered[1], 16 * U * (NC // 2))

        @block.tensor
        def _(pe):
            if n_loads:
                pe.wait_ge(weights_loaded, 16 * n_loads)
            turn = g.ident if w is None else w_sb

            def body(c, i, par, steady):
                if weight is not None:
                    pe.wait_ge(rows_weighted, c + 1)
                else:
                    pe.wait_ge(gathered[par], 16 * U * (i + 1))
                if steady:
                    pe.wait_ge(message_ready if relu_bias is not None else summed, c - 1)
                for u in range(U):
                    x = (rows if weight is None else weighted)[:, par, u, :]
                    t = nc.tensor.transpose(turned[:, par, u * P:u * P + P], x, g.ident[:, :])
                t.then_inc(message_turned, 1)

            def finish(c, i, par, steady):
                pe.wait_ge(summed, c + 1)
                if steady:
                    pe.wait_ge(rows_ready, c - 1)
                for u in range(U):
                    t = nc.tensor.matmul(back[:, par, u, :], total[:, par, u * P:u * P + P], turn[:, :],
                                         start=True, stop=True)
                t.then_inc(turned_back, 1)

            body(0, 0, 0, False)
            body(1, 0, 1, False)
            finish(0, 0, 0, False)
            body(2, 1, 0, True)
            finish(1, 0, 1, False)
            with pe.Fori(1, NC // 2) as i:
                body(2 * i + 1, i, 1, True)
                finish(2 * i, i, 0, True)
                body(2 * i + 2, i + 1, 0, True)
                finish(2 * i + 1, i, 1, True)
            finish(NC - 1, NC // 2, 0, True)

        @block.vector
        def _(dve):
            def body(c, i, par, steady):
                if weight is not None:
                    dve.wait_ge(gathered[par], 16 * U * (i + 1))
                    if steady:
                        dve.wait_ge(message_turned, c - 1)
                    for u in range(U):
                        t = nc.vector.tensor_scalar(weighted[:, par, u, :], rows[:, par, u, :],
                                                    g.col[:, weight, bass.ds(c * U + u, 1)], None, ALU.mult)
                    t.then_inc(rows_weighted, 1)
                if relu_bias is not None:
                    dve.wait_ge(message_ready, c + 1)
                else:
                    dve.wait_ge(message_turned, c + 1)
                if steady:
                    dve.wait_ge(turned_back, c - 1)
                if steady or par:
                    dve.wait_ge(summed, c)
                x = message[:, par, :] if relu_bias is not None else turned[:, par, :]
                nc.vector.tensor_tensor_scan(total[:, par, :], same[:, bass.ds(c * C, C)], x,
                                             total[:, 1 - par, C - 1:C] if steady or par else 0.0,
                                             ALU.mult, ALU.add).then_inc(summed, 1)

            chunks(dve, body)

        @block.scalar
        def _(act):
            if relu_bias is not None:
                act.wait_ge(weights_loaded, 16 * n_loads)

            def relu(c, i, par, steady):
                act.wait_ge(message_turned, c + 1)
                if steady:
                    act.wait_ge(summed, c - 1)
                nc.scalar.activation(message[:, par, :], turned[:, par, :], ACT.Relu,
                                     bias=bias_sb[:, 0:1]).then_inc(message_ready, 1)

            def body(c, i, par, steady):
                act.wait_ge(turned_back, c + 1)
                if steady:
                    act.wait_ge(scattered[par], 16 * U * i)
                if scale is None:
                    nc.scalar.activation(done[:, par, :, :], back[:, par, :, :], ACT.Copy).then_inc(rows_ready, 1)
                else:
                    for u in range(U):
                        t = nc.scalar.activation(done[:, par, u, :], back[:, par, u, :], ACT.Copy,
                                                 scale=g.col[:, scale, bass.ds(c * U + u, 1)])
                    t.then_inc(rows_ready, 1)

            if relu_bias is None:
                chunks(act, body)
            else:
                relu(0, 0, 0, False)
                relu(1, 0, 1, False)
                body(0, 0, 0, False)
                relu(2, 1, 0, True)
                body(1, 0, 1, False)
                with act.Fori(1, NC // 2) as i:
                    relu(2 * i + 1, i, 1, True)
                    body(2 * i, i, 0, True)
                    relu(2 * i + 2, i + 1, 0, True)
                    body(2 * i + 1, i, 1, True)
                body(NC - 1, NC // 2, 0, True)


def make_penalties(nc, g):
    with ExitStack() as ctx:
        made_penalties = signals(nc, ctx)("made_penalties")
        block = ctx.enter_context(nc.Block())

        @block.vector
        def _(dve):
            nc.vector.tensor_scalar(g.same_s[:, :], g.same_d[:, :], BIG, -BIG, ALU.mult,
                                    ALU.add).then_inc(made_penalties, 1)
            dve.wait_ge(made_penalties, 1)


def attend(nc, g, name, table, wq, bq, wk, bk, wv, bv, out):
    with ExitStack() as ctx:
        def sb(n, shape, dt):
            return ctx.enter_context(nc.sbuf_tensor(name + n, shape, dt))

        signal = signals(nc, ctx)

        def sem(n):
            return signal(name + n)

        def ps(n, shape):
            return ctx.enter_context(nc.psum_tensor(name + n, shape, F32))

        rows = sb("rows", [P, 2, 2, U, D], F32)
        x_src = sb("x_src", [P, 2, C], F32)
        x_dst = sb("x_dst", [P, 2, C], F32)
        query = sb("query", [P, 2, C], F32)
        qk = sb("qk", [P, C], F32)
        top = sb("top", [P, 2, C + 1], F32)
        enter = sb("enter", [P, 2, C], F32)
        keep = sb("keep", [P, 2, C], F32)
        mass = sb("mass", [P, 2, C], F32)
        message = sb("message", [P, C], F32)
        total = sb("total", [P, 2, C], F32)
        result = sb("result", [P, 2, C], F32)
        share = sb("share", [P, C], F32)
        done = sb("done", [P, 2, U, D], F32)
        at = sb("at", [P, 2, 3, U], I32)
        w_sb = sb("w", [D, 3, D], F32)
        b_sb = sb("b", [D, 3], F32)
        bq_scaled = sb("bq_scaled", [D, 1], F32)
        t_src = ps("t_src", [P, C])
        t_dst = ps("t_dst", [P, C])
        key = ps("key", [P, C])
        raw_query = ps("raw_query", [P, C])
        value = ps("value", [P, 2, C])
        score = ps("score", [P, C])
        back = ps("back", [P, U, D])

        weights_loaded = sem("weights_loaded")
        bias_scaled = sem("bias_scaled")
        at_copied = sem("at_copied")
        gathered = (sem("gathered0"), sem("gathered1"))
        scattered = (sem("scattered0"), sem("scattered1"))
        turned = sem("turned")
        turned_read = sem("turned_read")
        projected = sem("projected")
        query_ready = sem("query_ready")
        qk_ready = sem("qk_ready")
        scored = sem("scored")
        top_ready = sem("top_ready")
        shifted = sem("shifted")
        keep_step = sem("keep_step")
        enter_ready = sem("enter_ready")
        keep_ready = sem("keep_ready")
        mass_ready = sem("mass_ready")
        message_ready = sem("message_ready")
        total_ready = sem("total_ready")
        share_step = sem("share_step")
        result_ready = sem("result_ready")
        turned_back = sem("turned_back")
        rows_ready = sem("rows_ready")
        first_top = sem("first_top")
        block = ctx.enter_context(nc.Block())
        SCALE = HD ** -0.5

        @block.sync
        def _(sp):
            for n, (w, b) in enumerate(((wk, bk), (wv, bv), (wq, bq))):
                sp.dma_start(w_sb[:, n, :], w).then_inc(weights_loaded, 16)
                sp.dma_start(b_sb[:, n:n + 1], b.rearrange("(p a) -> p a", a=1)).then_inc(weights_loaded, 16)

        @block.gpsimd
        def _(pool):
            def fetch(c, i, par, steady):
                if steady:
                    pool.wait_ge(turned, c - 1)
                for k, n in enumerate((SRC_D, DST_D)):
                    nc.gpsimd.tensor_copy(at[:, par, k, :], g.idx[:, n, bass.ds(c * U, U)]).then_inc(at_copied, 1)
                pool.wait_ge(at_copied, 3 * c if steady else 2 * c + 2)
                pool.nop(nofuse=True)
                for k in range(2):
                    for u in range(U):
                        nc.gpsimd.indirect_dma_start(
                            out=rows[:, par, k, u, :], out_offset=None, in_=table,
                            in_offset=bass.IndirectOffsetOnAxis(ap=at[:, par, k, u:u + 1], axis=0)
                        ).then_inc(gathered[par], 16)

            def send(c, i, par, steady, copies):
                if steady:
                    pool.wait_ge(scattered[par], 16 * U * i)
                nc.gpsimd.tensor_copy(at[:, par, 2, :], g.idx[:, OUT_D, bass.ds(c * U, U)]).then_inc(at_copied, 1)
                pool.wait_ge(at_copied, copies)
                pool.wait_ge(rows_ready, c + 1)
                pool.nop(nofuse=True)
                for u in range(U):
                    nc.gpsimd.indirect_dma_start(
                        out=out, out_offset=bass.IndirectOffsetOnAxis(ap=at[:, par, 2, u:u + 1], axis=0),
                        in_=done[:, par, u, :], in_offset=None).then_inc(scattered[par], 16)

            fetch(0, 0, 0, False)
            fetch(1, 0, 1, False)
            for c in (2, 3):
                fetch(c, 1, c % 2, True)
                send(c - 2, 0, c % 2, False, 3 * c + 1)
            with pool.Fori(2, NC // 2) as i:
                for par in range(2):
                    fetch(2 * i + par, i, par, True)
                    send(2 * i + par - 2, i - 1, par, True, 6 * i + 3 * par + 1)
            fetch(NC - 1, NC // 2, 0, True)
            send(NC - 3, NC // 2 - 1, 0, True, 3 * NC - 2)
            send(NC - 2, NC // 2 - 1, 1, True, 3 * NC - 1)
            send(NC - 1, NC // 2, 0, True, 3 * NC)
            pool.wait_ge(scattered[0], 16 * U * (NC // 2 + 1))
            pool.wait_ge(scattered[1], 16 * U * (NC // 2))

        @block.tensor
        def _(pe):
            def turn(c, i, par, steady):
                pe.wait_ge(gathered[par], 2 * U * 16 * (i + 1))
                if steady or par:
                    pe.wait_ge(turned_read, c)
                for k, to in enumerate((t_src, t_dst)):
                    for u in range(U):
                        t = nc.tensor.transpose(to[:, u * P:u * P + P], rows[:, par, k, u, :], g.ident[:, :])
                t.then_inc(turned, 1)

            def project(c, i, par, steady):
                pe.wait_ge(turned_read, c + 1)
                if steady or par:
                    pe.wait_ge(qk_ready, c)
                if steady:
                    pe.wait_ge(message_ready, c - 1)
                nc.tensor.matmul(raw_query[:, :], w_sb[:, 2, :], x_dst[:, par, :], start=True, stop=True)
                nc.tensor.matmul(key[:, :], w_sb[:, 0, :], x_src[:, par, :], start=True, stop=True)
                nc.tensor.matmul(value[:, par, :], w_sb[:, 1, :], x_src[:, par, :], start=True,
                                 stop=True).then_inc(projected, 1)

            def rate(c, i, par, steady):
                pe.wait_ge(qk_ready, c + 1)
                if steady or par:
                    pe.wait_ge(shifted, c)
                nc.tensor.matmul(score[:, :], g.heads[:, :], qk[:, :], start=True, stop=True).then_inc(scored, 1)

            def finish(c, i, par, steady):
                pe.wait_ge(result_ready, c + 1)
                if steady or par:
                    pe.wait_ge(rows_ready, c)
                for u in range(U):
                    t = nc.tensor.transpose(back[:, u, :], result[:, par, u * P:u * P + P], g.ident[:, :])
                t.then_inc(turned_back, 1)

            pe.wait_ge(weights_loaded, 16 * 6)
            turn(0, 0, 0, False)
            project(0, 0, 0, False)
            turn(1, 0, 1, False)
            rate(0, 0, 0, False)
            project(1, 0, 1, False)
            turn(2, 1, 0, True)
            rate(1, 0, 1, False)
            finish(0, 0, 0, False)
            with pe.Fori(1, NC // 2) as i:
                project(2 * i, i, 0, True)
                turn(2 * i + 1, i, 1, True)
                rate(2 * i, i, 0, True)
                finish(2 * i - 1, i - 1, 1, True)
                project(2 * i + 1, i, 1, True)
                turn(2 * i + 2, i + 1, 0, True)
                rate(2 * i + 1, i, 1, True)
                finish(2 * i, i, 0, True)
            project(NC - 1, NC // 2, 0, True)
            rate(NC - 1, NC // 2, 0, True)
            finish(NC - 2, NC // 2 - 1, 1, True)
            finish(NC - 1, NC // 2, 0, True)

        @block.scalar
        def _(act):
            def fetch(c, i, par, steady):
                act.wait_ge(turned, c + 1)
                if steady:
                    act.wait_ge(projected, c - 1)
                nc.scalar.activation(x_src[:, par, :], t_src[:, :], ACT.Copy)
                nc.scalar.activation(x_dst[:, par, :], t_dst[:, :], ACT.Copy).then_inc(turned_read, 1)

            def ask(c, i, par, steady):
                act.wait_ge(projected, c + 1)
                nc.scalar.activation(query[:, par, :], raw_query[:, :], ACT.Identity, bias=bq_scaled[:, 0:1],
                                     scale=SCALE).then_inc(query_ready, 1)

            def exps(c, i, par, steady):
                act.wait_ge(shifted, c + 1)
                nc.scalar.activation(enter[:, par, :], enter[:, par, :], ACT.Exp).then_inc(enter_ready, 1)
                act.wait_ge(keep_step, 2 * c + 2)
                nc.scalar.activation(keep[:, par, :], keep[:, par, :], ACT.Exp).then_inc(keep_ready, 1)

            def finish(c, i, par, steady):
                act.wait_ge(turned_back, c + 1)
                if steady:
                    act.wait_ge(scattered[par], 16 * U * i)
                nc.scalar.activation(done[:, par, :, :], back[:, :, :], ACT.Copy).then_inc(rows_ready, 1)

            act.wait_ge(bias_scaled, 1)
            fetch(0, 0, 0, False)
            ask(0, 0, 0, False)
            fetch(1, 0, 1, False)
            exps(0, 0, 0, False)
            ask(1, 0, 1, False)
            fetch(2, 1, 0, True)
            exps(1, 0, 1, False)
            finish(0, 0, 0, False)
            with act.Fori(1, NC // 2) as i:
                ask(2 * i, i, 0, True)
                fetch(2 * i + 1, i, 1, True)
                exps(2 * i, i, 0, True)
                finish(2 * i - 1, i - 1, 1, True)
                ask(2 * i + 1, i, 1, True)
                fetch(2 * i + 2, i + 1, 0, True)
                exps(2 * i + 1, i, 1, True)
                finish(2 * i, i, 0, True)
            ask(NC - 1, NC // 2, 0, True)
            exps(NC - 1, NC // 2, 0, True)
            finish(NC - 2, NC // 2 - 1, 1, True)
            finish(NC - 1, NC // 2, 0, True)

        @block.vector
        def _(dve):
            def multiply(c, i, par, steady):
                dve.wait_ge(query_ready, c + 1)
                if steady or par:
                    dve.wait_ge(scored, c)
                nc.vector.scalar_tensor_tensor(out=qk[:, :], in0=key[:, :], scalar=b_sb[:, 0:1],
                                               in1=query[:, par, :], op0=ALU.add, op1=ALU.mult
                                               ).then_inc(qk_ready, 1)

            def shift(c, i, par, steady):
                if steady or par:
                    dve.wait_ge(top_ready, c)
                    nc.vector.tensor_copy(top[:, par, 0:1], top[:, 1 - par, C:C + 1]).then_inc(first_top, 1)
                else:
                    nc.vector.memset(top[:, 0, 0:1], 0.0).then_inc(first_top, 1)
                dve.wait_ge(first_top, c + 1)
                dve.wait_ge(scored, c + 1)
                pen = g.same_s[:, bass.ds(c * C, C)]
                nc.vector.tensor_tensor_scan(top[:, par, 1:C + 1], pen, score[:, :], top[:, par, 0:1],
                                             ALU.add, ALU.max).then_inc(top_ready, 1)
                dve.wait_ge(top_ready, c + 1)
                if steady:
                    dve.wait_ge(total_ready, c - 1)
                nc.vector.tensor_tensor(keep[:, par, :], top[:, par, 0:C], pen, ALU.add).then_inc(keep_step, 1)
                nc.vector.tensor_tensor(enter[:, par, :], score[:, :], top[:, par, 1:C + 1], ALU.subtract
                                        ).then_inc(shifted, 1)
                dve.wait_ge(keep_step, 2 * c + 1)
                nc.vector.tensor_tensor(keep[:, par, :], keep[:, par, :], top[:, par, 1:C + 1], ALU.subtract
                                        ).then_inc(keep_step, 1)

            def add_up(c, i, par, steady):
                dve.wait_ge(enter_ready, c + 1)
                if steady or par:
                    dve.wait_ge(total_ready, c)
                nc.vector.scalar_tensor_tensor(out=message[:, :], in0=value[:, par, :], scalar=b_sb[:, 1:2],
                                               in1=enter[:, par, :], op0=ALU.add, op1=ALU.mult
                                               ).then_inc(message_ready, 1)
                dve.wait_ge(keep_ready, c + 1)
                if steady or par:
                    dve.wait_ge(result_ready, c)
                nc.vector.tensor_tensor_scan(mass[:, par, :], keep[:, par, :], enter[:, par, :],
                                             mass[:, 1 - par, C - 1:C] if steady or par else 0.0,
                                             ALU.mult, ALU.add).then_inc(mass_ready, 1)
                dve.wait_ge(message_ready, c + 1)
                nc.vector.tensor_tensor_scan(total[:, par, :], keep[:, par, :], message[:, :],
                                             total[:, 1 - par, C - 1:C] if steady or par else 0.0,
                                             ALU.mult, ALU.add).then_inc(total_ready, 1)
                dve.wait_ge(mass_ready, c + 1)
                nc.vector.tensor_scalar(share[:, :], mass[:, par, :], 1e-16, None, ALU.add).then_inc(share_step, 1)
                dve.wait_ge(share_step, 2 * c + 1)
                nc.vector.reciprocal(share[:, :], share[:, :]).then_inc(share_step, 1)
                dve.wait_ge(share_step, 2 * c + 2)
                dve.wait_ge(total_ready, c + 1)
                if steady:
                    dve.wait_ge(turned_back, c - 1)
                nc.vector.tensor_tensor(result[:, par, :], total[:, par, :], share[:, :], ALU.mult
                                        ).then_inc(result_ready, 1)

            dve.wait_ge(weights_loaded, 16 * 6)
            nc.vector.tensor_scalar(bq_scaled[:, :], b_sb[:, 2:3], SCALE, None, ALU.mult).then_inc(bias_scaled, 1)
            multiply(0, 0, 0, False)
            shift(0, 0, 0, False)
            multiply(1, 0, 1, False)
            add_up(0, 0, 0, False)
            shift(1, 0, 1, False)
            with dve.Fori(1, NC // 2) as i:
                multiply(2 * i, i, 0, True)
                add_up(2 * i - 1, i - 1, 1, True)
                shift(2 * i, i, 0, True)
                multiply(2 * i + 1, i, 1, True)
                add_up(2 * i, i, 0, True)
                shift(2 * i + 1, i, 1, True)
            multiply(NC - 1, NC // 2, 0, True)
            add_up(NC - 2, NC // 2 - 1, 1, True)
            shift(NC - 1, NC // 2, 0, True)
            add_up(NC - 1, NC // 2, 0, True)


def after(eng, sem, value):
    if not isinstance(value, int) or value > 0:
        eng.wait_ge(sem, value)


def groups(eng, body, lag=0):
    for n in range(6):
        body(n // 4, n % 4)
    with eng.Fori(1, (NG - 6) // 4 + 1) as i:
        for r in range(4):
            body(i + (2 + r) // 4, (2 + r) % 4)
    for n in range(NG, NG + lag):
        body(n // 4, n % 4)


def back_by(q, m, lag):
    if isinstance(q, int) and 4 * q + m < lag:
        return None
    return (q, m - lag) if m >= lag else (q - 1, m + 4 - lag)


def inside(q, m):
    return not isinstance(q, int) or 4 * q + m < NG


ADD, TWICE, CONV, LAST, RELU = range(5)


def update_nodes(nc, g, name, kind, h, agg, out, bias=None, ws=None, gain=None, offset=None, outer=None):
    with ExitStack() as ctx:
        def sb(n, shape, dt=F32):
            return ctx.enter_context(nc.sbuf_tensor(name + n, shape, dt))

        signal = signals(nc, ctx)

        def sem(n):
            return signal(name + n)

        conv = kind in (CONV, LAST)
        node = sb("node", [NP, 4, G, D])
        agg_in = sb("agg_in", [NP, 2, G, D])
        y = sb("y", [NP, 2, G, D])
        z = sb("z", [NP, 2, G, D]) if kind == CONV else None
        outer_in = sb("outer_in", [NP, 4, G, D]) if kind == LAST else None
        turned_sb = sb("turned_sb", [D, 2, G, P]) if conv else None
        w_sb = sb("w_sb", [D, D])
        rows3 = sb("rows3", [NP, 3, D])
        stats = sb("stats", [NP, G, 6])
        mv = sb("mv", [NP, G, 2])
        var = sb("var", [NP, G])
        half = sb("half", [NP, G], I32)
        root = sb("root", [NP, G])
        t1 = sb("t1", [NP, G])
        rstd = sb("rstd", [NP, 2, G])
        shift = sb("shift", [NP, 2, G])
        if conv:
            turned = ctx.enter_context(nc.psum_tensor(name + "turned", [D, 2, G, P], F32))
            product = ctx.enter_context(nc.psum_tensor(name + "product", [P, 2, G, D], F32))

        consts_loaded = sem("consts_loaded")
        node_loaded = [sem(f"node_loaded{m}") for m in range(4)]
        agg_loaded = [sem(f"agg_loaded{m}") for m in range(2)]
        stored = [sem(f"stored{m}") for m in range(4)]
        bias_added = sem("bias_added")
        turned_ready = sem("turned_ready")
        turned_copied = sem("turned_copied")
        product_ready = sem("product_ready")
        sum_ready = sem("sum_ready")
        activated = sem("activated")
        outer_added = sem("outer_added")
        stats_ready = sem("stats_ready")
        mv_ready = sem("mv_ready")
        step = sem("step")
        norm_ready = sem("norm_ready")
        normed = sem("normed")
        scaled = sem("scaled")
        offset_added = sem("offset_added")
        result_ready = sem("result_ready")
        block = ctx.enter_context(nc.Block())

        parts = (slice(0, SPLIT), slice(SPLIT, NP))
        rowvecs = [v for v in (bias, gain, offset) if v is not None]
        n_const = len(rowvecs) + (ws is not None)

        def of_group(table, s, grp):
            return table[0:N, :].rearrange("(p r) f -> p (r f)", r=RP)[s, bass.ds(grp * G * D, G * D)]

        def bc(row):
            return rows3[:, row:row + 1, :].to_broadcast([NP, G, D])

        @block.sync
        def _(sp):
            for n, v in enumerate((bias, gain, offset)):
                if v is not None:
                    sp.dma_start(rows3[:, n, :], v.rearrange("(a f) -> a f", a=1).to_broadcast([NP, D])
                                 ).then_inc(consts_loaded, 16)
            if ws is not None:
                sp.dma_start(w_sb[:, :], ws).then_inc(consts_loaded, 16)

            def load(q, m):
                grp = 4 * q + m
                after(sp, stored[m], 32 * q)
                for s in parts:
                    sp.dma_start(node[s, m, :, :].rearrange("p a f -> p (a f)"), of_group(h, s, grp)
                                 ).then_inc(node_loaded[m], 16)
                if kind == LAST:
                    for s in parts:
                        sp.dma_start(outer_in[s, m, :, :].rearrange("p a f -> p (a f)"), of_group(outer, s, grp)
                                     ).then_inc(node_loaded[m], 16)
                after(sp, sum_ready, grp - 1)
                for s in parts:
                    sp.dma_start(agg_in[s, m % 2, :, :].rearrange("p a f -> p (a f)"), of_group(agg, s, grp)
                                 ).then_inc(agg_loaded[m % 2], 16)

            groups(sp, load)

        n_node = 64 if kind == LAST else 32

        def node_in(eng, q, m):
            eng.wait_ge(node_loaded[m], n_node * (q + 1))

        def agg_in_ready(eng, q, m):
            eng.wait_ge(agg_loaded[m % 2], 32 * (2 * q + m // 2 + 1))

        @block.gpsimd
        def _(pool):
            if n_const:
                pool.wait_ge(consts_loaded, 16 * n_const)

            def body(q, m):
                grp = 4 * q + m
                if bias is not None and inside(q, m):
                    agg_in_ready(pool, q, m)
                    nc.gpsimd.tensor_tensor(agg_in[:, m % 2, :, :], agg_in[:, m % 2, :, :], bc(0),
                                            ALU.add).then_inc(bias_added, 1)
                if kind == CONV and (was := back_by(q, m, 1)):
                    p = was[1] % 2
                    pool.wait_ge(normed, grp)
                    nc.gpsimd.tensor_tensor(z[:, p, :, :], z[:, p, :, :], bc(1), ALU.mult).then_inc(scaled, 1)
                    pool.wait_ge(scaled, grp)
                    nc.gpsimd.tensor_tensor(z[:, p, :, :], z[:, p, :, :], bc(2), ALU.add).then_inc(offset_added, 1)

            groups(pool, body, 1)

        @block.tensor
        def _(pe):
            if not conv:
                return
            pe.wait_ge(consts_loaded, 16 * n_const)

            def body(q, m):
                grp = 4 * q + m
                p = m % 2
                if inside(q, m):
                    node_in(pe, q, m)
                    after(pe, turned_copied, grp - 1)
                    for j in range(G):
                        t = nc.tensor.transpose(turned[:, p, j, 0:NP], node[:, m, j, :], g.ident[0:NP, 0:NP])
                    t.then_inc(turned_ready, 1)
                if was := back_by(q, m, 1):
                    p = was[1] % 2
                    pe.wait_ge(turned_copied, grp)
                    after(pe, sum_ready, grp - 2)
                    for j in range(G):
                        t = nc.tensor.matmul(product[0:NP, p, j, :], turned_sb[:, p, j, 0:NP], w_sb[:, :],
                                             start=True, stop=True)
                    t.then_inc(product_ready, 1)

            groups(pe, body, 1)

        @block.scalar
        def _(act):
            def normalize(q, m, to):
                grp = 4 * q + m
                act.wait_ge(norm_ready, grp + 1)
                for j in range(G):
                    t = nc.scalar.activation(to[:, j, :], y[:, m % 2, j, :], ACT.Identity,
                                             bias=shift[:, m % 2, j:j + 1], scale=rstd[:, m % 2, j:j + 1])
                t.then_inc(normed, 1)

            def store(q, m):
                grp = 4 * q + m
                act.wait_ge(result_ready if kind == CONV else normed, grp + 1)
                for s in parts:
                    act.dma_start(of_group(out, s, grp), node[s, m, :, :].rearrange("p a f -> p (a f)")
                                  ).then_inc(stored[m], 16)

            def copy(q, m):
                grp = 4 * q + m
                act.wait_ge(turned_ready, grp + 1)
                after(act, product_ready, grp - 1)
                nc.scalar.activation(turned_sb[:, m % 2, :, 0:NP], turned[:, m % 2, :, 0:NP],
                                     ACT.Copy).then_inc(turned_copied, 1)

            def gelu(q, m, x):
                grp = 4 * q + m
                act.wait_ge(offset_added if kind == CONV else sum_ready, grp + 1)
                nc.scalar.activation(x[:, m % 2, :, :], x[:, m % 2, :, :], ACT.Gelu).then_inc(activated, 1)

            def body(q, m):
                if conv and inside(q, m):
                    copy(q, m)
                if kind == CONV:
                    if (was := back_by(q, m, 1)) and inside(*was):
                        after(act, result_ready, 4 * q + m - 2)
                        normalize(*was, z[:, was[1] % 2, :, :])
                    if (was := back_by(q, m, 2)) and inside(*was):
                        gelu(*was, z)
                    if was := back_by(q, m, 3):
                        store(*was)
                elif kind == LAST:
                    if (was := back_by(q, m, 1)) and inside(*was):
                        gelu(*was, y)
                    if (was := back_by(q, m, 2)) and inside(*was):
                        normalize(*was, node[:, was[1], :, :])
                    if was := back_by(q, m, 3):
                        store(*was)
                else:
                    if inside(q, m):
                        normalize(q, m, node[:, m, :, :])
                    if was := back_by(q, m, 1):
                        store(*was)

            groups(act, body, 3 if conv else 1)
            for m in range(4):
                act.wait_ge(stored[m], 32 * len(range(m, NG, 4)))

        @block.vector
        def _(dve):
            STEPS = 12

            def add(q, m):
                grp = 4 * q + m
                p = m % 2
                if conv:
                    dve.wait_ge(product_ready, grp + 1)
                else:
                    node_in(dve, q, m)
                if bias is not None:
                    dve.wait_ge(bias_added, grp + 1)
                else:
                    agg_in_ready(dve, q, m)
                after(dve, normed, grp - 1)
                a = agg_in[:, p, :, :]
                if conv:
                    ins = nc.vector.tensor_tensor(y[:, p, :, :], product[0:NP, p, :, :], a, ALU.add)
                elif kind == ADD:
                    ins = nc.vector.tensor_tensor(y[:, p, :, :], node[:, m, :, :], a, ALU.add)
                elif kind == TWICE:
                    ins = nc.vector.scalar_tensor_tensor(out=y[:, p, :, :], in0=node[:, m, :, :], scalar=2.0,
                                                         in1=a, op0=ALU.mult, op1=ALU.add)
                else:
                    ins = nc.vector.scalar_tensor_tensor(out=y[:, p, :, :], in0=a, scalar=0.0,
                                                         in1=node[:, m, :, :], op0=ALU.max, op1=ALU.add)
                ins.then_inc(sum_ready, 1)

            def measure(q, m):
                grp = 4 * q + m
                p = m % 2
                if kind == LAST:
                    dve.wait_ge(activated, grp + 1)
                    nc.vector.tensor_tensor(y[:, p, :, :], y[:, p, :, :], outer_in[:, m, :, :],
                                            ALU.add).then_inc(outer_added, 1)
                    dve.wait_ge(outer_added, grp + 1)
                else:
                    dve.wait_ge(sum_ready, grp + 1)
                for j in range(G):
                    t = nc.vector.bn_stats(stats[:, j, :], y[:, p, j, :])
                t.then_inc(stats_ready, 1)
                dve.wait_ge(stats_ready, grp + 1)
                dve.nop(nofuse=True)
                for j in range(G):
                    t = nc.vector.bn_aggr(mv[:, j, :], stats[:, j, :])
                t.then_inc(mv_ready, 1)
                dve.wait_ge(mv_ready, grp + 1)
                n = [0]

                def link(ins):
                    n[0] += 1
                    ins.then_inc(step, 1)
                    dve.wait_ge(step, STEPS * grp + n[0])

                link(nc.vector.tensor_scalar(var[:, :], mv[:, :, 1], EPS, None, ALU.add))
                link(nc.vector.tensor_scalar(half[:, :], var[:, :].bitcast(I32), 1, None, ALU.arith_shift_right))
                link(nc.vector.tensor_scalar(root[:, :].bitcast(I32), half[:, :], -1.0, float(0x5F3759DF),
                                             ALU.mult, ALU.add))
                for turn in range(3):
                    link(nc.vector.tensor_tensor(t1[:, :], root[:, :], root[:, :], ALU.mult))
                    link(nc.vector.scalar_tensor_tensor(out=t1[:, :], in0=t1[:, :], scalar=-0.5, in1=var[:, :],
                                                        op0=ALU.mult, op1=ALU.mult))
                    to = rstd[:, p, :] if turn == 2 else root[:, :]
                    link(nc.vector.scalar_tensor_tensor(out=to, in0=t1[:, :], scalar=1.5, in1=root[:, :],
                                                        op0=ALU.add, op1=ALU.mult))
                assert n[0] == STEPS
                nc.vector.scalar_tensor_tensor(out=shift[:, p, :], in0=mv[:, :, 0], scalar=-1.0,
                                               in1=rstd[:, p, :], op0=ALU.mult, op1=ALU.mult
                                               ).then_inc(norm_ready, 1)
                dve.wait_ge(norm_ready, grp + 1)

            def keep_on(q, m):
                grp = 4 * q + m
                dve.wait_ge(activated, grp + 1)
                nc.vector.tensor_tensor(node[:, m, :, :], node[:, m, :, :], z[:, m % 2, :, :],
                                        ALU.add).then_inc(result_ready, 1)

            def body(q, m):
                if inside(q, m):
                    add(q, m)
                    if kind != LAST:
                        measure(q, m)
                if kind == LAST and (was := back_by(q, m, 1)):
                    measure(*was)
                if kind == CONV and (was := back_by(q, m, 2)):
                    keep_on(*was)

            groups(dve, body, {CONV: 2, LAST: 1}.get(kind, 0))


def build(nc, x, src, dst, edge_weight, w1, b1, w2, b2, wq, bq, wk, bk, wv, bv, ws, bs, ln_g, ln_b, w3, b3, out):
    def dram(name, shape, dt=F32):
        return nc.dram_tensor(name, shape, dt).ap()

    g = Program()
    g.agg_s = dram("agg_s", [TRASH + EP, D])
    g.agg_d = dram("agg_d", [TRASH + EP, D])
    g.he = dram("he", [NH + EP, D])
    by_low = [dram(f"by_low{k}", [EP, 4]) for k in range(2)]
    by_key = [dram(f"by_key{k}", [EP + 2, 4]) for k in range(2)]
    cols = dram("cols", [NCOL, EP])
    same_rows = dram("same_rows", [2, EP], BF16)
    h = [dram(f"h{n}", [N, D]) for n in range(3)]

    with ExitStack() as ctx:
        constants(nc, ctx, g)
        with (
            nc.sbuf_tensor("pay0", [P, T, 4], F32) as pay0,
            nc.sbuf_tensor("pay1", [P, T, 4], F32) as pay1,
            nc.sbuf_tensor("digit", [P, 4, T], F32) as digit,
            nc.psum_tensor("counts", [P, 4, 512], F32) as counts,
        ):
            count_digits(nc, g, dst, src, edge_weight, pay0, digit, counts)
            rank_pass(nc, g, 0, (digit[:, 0, :], digit[:, 2, :]), (pay0, pay0), counts, by_low, 0)
            second_digit(nc, g, by_low, (digit[:, 1, :], digit[:, 3, :]), (pay0, pay1))
            rank_pass(nc, g, 1, (digit[:, 1, :], digit[:, 3, :]), (pay0, pay1), counts, by_key, 1)
        describe(nc, g, by_key, cols, same_rows)

        sum_segments(nc, g, "a", x, g.same_d, SRC_D, OUT_HE, g.he, w=w1, scale=CNT_D)
        sum_segments(nc, g, "b", g.he[0:NH, :], g.same_s, HE_S, OUT_S, g.agg_s, scale=CNT_S)
        sum_segments(nc, g, "c", g.agg_s[0:N, :], g.same_d, SRC_D, OUT_HE, g.he, relu_bias=b1, w=w2, scale=CNT_D)
        sum_segments(nc, g, "d", g.he[0:NH, :], g.same_s, HE_S, OUT_S, g.agg_s, scale=CNT_S)
        update_nodes(nc, g, "e", ADD, x, g.agg_s, h[0], bias=b2)

        sum_segments(nc, g, "f", h[0], g.same_d, SRC_D, OUT_D, g.agg_d)
        update_nodes(nc, g, "g", TWICE, h[0], g.agg_d, h[1])

        make_penalties(nc, g)
        at = 1
        for n in range(LAYERS):
            attend(nc, g, f"h{n}", h[at], wq[n], bq[n], wk[n], bk[n], wv[n], bv[n], g.agg_d)
            to = 2 if at == 0 else 0
            if n < LAYERS - 1:
                update_nodes(nc, g, f"i{n}", CONV, h[at], g.agg_d, h[to], bias=bs[n], ws=ws[n], gain=ln_g[n],
                             offset=ln_b[n])
            else:
                update_nodes(nc, g, f"i{n}", LAST, h[at], g.agg_d, h[to], bias=bs[n], ws=ws[n], outer=h[1])
            at = to

        sum_segments(nc, g, "j", h[at], g.same_d, SRC_D, OUT_D, g.agg_d, weight=WEIGHT, w=w3)
        update_nodes(nc, g, "k", RELU, h[at], g.agg_d, out, bias=b3)


_INS = ["x", "src", "dst", "edge_weight", "L0_gnn_W1", "L0_gnn_b1", "L0_gnn_W2", "L0_gnn_b2", "L2_gnn_Wq",
        "L2_gnn_bq", "L2_gnn_Wk", "L2_gnn_bk", "L2_gnn_Wv", "L2_gnn_bv", "L2_gnn_Ws", "L2_gnn_bs", "L2_gnn_ln_g",
        "L2_gnn_ln_b", "L3_gnn_weight", "L3_gnn_bias"]


def kernel(**inputs):
    import numpy as np
    import concourse.bacc as bacc
    from concourse.bass_utils import run_bass_kernel_spmd

    nc = bacc.Bacc("TRN2", target_bir_lowering=False, num_devices=1)
    arrays, args = {}, []
    for name in _INS:
        a = np.ascontiguousarray(inputs[name])
        arrays[f"in_{name}"] = a
        args.append(nc.dram_tensor(f"in_{name}", a.shape, mybir.dt.from_np(a.dtype), kind="ExternalInput").ap())
    args.append(nc.dram_tensor("out", (N, D), F32, kind="ExternalOutput").ap())
    build(nc, *args)
    r = run_bass_kernel_spmd(nc, [arrays], core_ids=[0])
    return r.results[0]["out"]
```

```python
from contextlib import ExitStack

import concourse.bass as bass
from concourse import mybir

F32 = mybir.dt.float32
I32 = mybir.dt.int32
BF16 = mybir.dt.bfloat16
ALU = mybir.AluOpType
ACT = mybir.ActivationFunctionType

P = 128
D = 128
HEADS = 4
HD = D // HEADS
N = 50000
NH = 10000
E = 25000
LAYERS = 5
EPS = 1e-5

T = -(-E // P)
EP = T * P
FULL = E // T
REST = E - FULL * T
U = 4
C = U * P
NC = T // U
DIG = 256
HALF = T // 2
PADKEY = N
TRASH = N + 1
BIG = 1e30
FILL = 5000

NP = 125
RP = N // NP
G = 8
NG = RP // G
SPLIT = 112

assert T % U == 0 and NC % 2 == 1 and NG % 2 == 0 and NP * RP == N

SRC_D, DST_D, OUT_D, OUT_HE, WEIGHT, HE_S, OUT_S, CNT_D, CNT_S = range(9)
NCOL = 9


class Program:
    pass


def chunks(eng, body):
    for c in range(2):
        body(c, 0, c, False)
    with eng.Fori(1, NC // 2) as i:
        body(2 * i, i, 0, True)
        body(2 * i + 1, i, 1, True)
    body(NC - 1, NC // 2, 0, True)


def signals(nc, ctx):
    taken = []

    def clear():
        nc.clear_and_free_semaphores(taken)
        nc.all_engine_barrier()

    def sem(name):
        taken.append(nc.alloc_semaphore(name))
        return taken[-1]

    ctx.callback(clear)
    return sem


def constants(nc, life, g):
    def sb(name, shape, dt):
        return life.enter_context(nc.sbuf_tensor(name, shape, dt))

    g.ident = sb("ident", [P, P], F32)
    g.before = sb("before", [P, P], BF16)
    g.notbefore = sb("notbefore", [P, P], BF16)
    g.ones = sb("ones", [P, P], BF16)
    g.heads = sb("heads", [P, P], F32)
    g.digits = sb("digits", [P, DIG], BF16)
    g.col = sb("col", [P, NCOL, T], F32)
    g.idx = sb("idx", [P, NCOL, T], I32)
    g.same_d = sb("same_d", [P, EP], BF16)
    g.same_s = sb("same_s", [P, EP], BF16)
    with ExitStack() as ctx:
        sem = signals(nc, ctx)
        digits_i = ctx.enter_context(nc.sbuf_tensor("digits_i", [P, DIG], I32))
        set_up = sem("set_up")
        iota_done = sem("iota_done")
        all_done = sem("all_done")
        block = ctx.enter_context(nc.Block())
        @block.vector
        def _(dve):
            nc.vector.memset(g.ident[:, :], 0.0).then_inc(set_up, 1)
            nc.vector.memset(g.before[:, :], 1.0).then_inc(set_up, 1)
            nc.vector.memset(g.notbefore[:, :], 1.0).then_inc(set_up, 1)
            nc.vector.memset(g.ones[:, :], 1.0).then_inc(all_done, 1)
            nc.vector.memset(g.heads[:, :], 0.0).then_inc(set_up, 1)
            dve.wait_ge(set_up, 4)
            for h in range(HEADS):
                s = slice(h * HD, h * HD + HD)
                nc.vector.memset(g.heads[s, s], 1.0).then_inc(all_done, 1)
            dve.wait_ge(iota_done, 1)
            nc.vector.tensor_copy(g.digits[:, :], digits_i[:, :]).then_inc(all_done, 1)
            dve.wait_ge(all_done, HEADS + 2)

        @block.gpsimd
        def _(pool):
            nc.gpsimd.iota(digits_i[:, :], pattern=[[1, DIG]], base=0, channel_multiplier=0).then_inc(iota_done, 1)
            pool.wait_ge(set_up, 4)
            nc.gpsimd.affine_select(out=g.ident[:, :], in_=g.ident[:, :], compare_op=ALU.not_equal, fill=1.0,
                                    base=0, pattern=[[-1, P]], channel_multiplier=1)
            nc.gpsimd.affine_select(out=g.before[:, :], in_=g.before[:, :], compare_op=ALU.is_gt, fill=0.0,
                                    base=0, pattern=[[1, P]], channel_multiplier=-1)
            nc.gpsimd.affine_select(out=g.notbefore[:, :], in_=g.notbefore[:, :], compare_op=ALU.is_ge, fill=0.0,
                                    base=0, pattern=[[-1, P]], channel_multiplier=1).then_inc(iota_done, 1)
            pool.wait_ge(iota_done, 2)


def count_digits(nc, g, dst, src, weight, pay, digit, counts):
    with ExitStack() as ctx:
        sem = signals(nc, ctx)
        raw = ctx.enter_context(nc.sbuf_tensor("raw", [P, 2, T], I32))
        low = ctx.enter_context(nc.sbuf_tensor("low", [P, 4, T], I32))
        smaller = ctx.enter_context(nc.sbuf_tensor("smaller", [P, 4, U, DIG], BF16))
        nothing = ctx.enter_context(nc.sbuf_tensor("nothing", [P, DIG], BF16))
        zero = ctx.enter_context(nc.sbuf_tensor("zero", [NP, FILL * D // NP], F32))
        cleared = sem("cleared")
        loaded = sem("loaded")
        nothing_ready = sem("nothing_ready")
        zero_ready = sem("zero_ready")
        zeros_stored = sem("zeros_stored")
        copied = sem("copied")
        masked = sem("masked")
        digits_ready = sem("digits_ready")
        smaller_ready = sem("smaller_ready")
        smaller_used = sem("smaller_used")
        block = ctx.enter_context(nc.Block())
        zero_fills = [(t, r) for t, rows in ((g.agg_s, N), (g.agg_d, N), (g.he, NH))
                      for r in range(0, rows, FILL)]

        @block.sync
        def _(sp):
            sp.wait_ge(cleared, 2)
            for k, x in enumerate((dst, src)):
                sp.dma_start(raw[0:FULL, k, :], x[0:FULL * T].rearrange("(p t) -> p t", t=T)).then_inc(loaded, 16)
                sp.dma_start(raw[FULL:FULL + 1, k, 0:REST],
                             x[FULL * T:E].rearrange("(a t) -> a t", a=1)).then_inc(loaded, 16)
            sp.dma_start(g.idx[0:FULL, WEIGHT, :].bitcast(F32),
                         weight[0:FULL * T].rearrange("(p t) -> p t", t=T)).then_inc(loaded, 16)
            sp.dma_start(g.idx[FULL:FULL + 1, WEIGHT, 0:REST].bitcast(F32),
                         weight[FULL * T:E].rearrange("(a t) -> a t", a=1)).then_inc(loaded, 16)
            sp.wait_ge(zero_ready, 1)
            for t, r in zero_fills:
                sp.dma_start(t[r:r + FILL, :].rearrange("(p a) f -> p (a f)", p=NP),
                             zero[:, :]).then_inc(zeros_stored, 16)
            sp.wait_ge(zeros_stored, 16 * len(zero_fills))

        @block.vector
        def _(dve):
            nc.vector.memset(raw[:, :, :], PADKEY).then_inc(cleared, 1)
            nc.vector.memset(g.idx[:, WEIGHT, :].bitcast(F32), 0.0).then_inc(cleared, 1)
            nc.vector.memset(pay[:, :, 3], 0.0)
            nc.vector.memset(nothing[:, :], 0.0).then_inc(nothing_ready, 1)
            dve.wait_ge(loaded, 6 * 16)
            nc.vector.tensor_copy(pay[:, :, 0], raw[:, 0, :]).then_inc(copied, 1)
            nc.vector.tensor_copy(pay[:, :, 1], raw[:, 1, :]).then_inc(copied, 1)
            nc.vector.tensor_copy(pay[:, :, 2], g.idx[:, WEIGHT, :].bitcast(F32)).then_inc(copied, 1)
            for k in range(2):
                nc.vector.tensor_scalar(low[:, 2 * k, :], raw[:, k, :], DIG - 1, None,
                                        ALU.bitwise_and).then_inc(masked, 1)
                nc.vector.tensor_scalar(low[:, 2 * k + 1, :], raw[:, k, :], 8, None,
                                        ALU.arith_shift_right).then_inc(masked, 1)
            dve.wait_ge(masked, 4)
            nc.vector.tensor_copy(digit[:, :, :], low[:, :, :]).then_inc(digits_ready, 1)
            dve.wait_ge(digits_ready, 1)

            def compare(c, i, par, steady):
                for u in range(U):
                    for k in range(4):
                        if u == 0 and k == 0 and (steady or par):
                            dve.wait_ge(smaller_used, c)
                        nc.vector.tensor_scalar(smaller[:, k, u, :], g.digits[:, :],
                                                digit[:, k, bass.ds(c * U + u, 1)], None,
                                                ALU.is_gt).then_inc(smaller_ready, 1)

            chunks(dve, compare)

        @block.gpsimd
        def _(pool):
            nc.gpsimd.memset(zero[:, :], 0.0).then_inc(zero_ready, 1)

        @block.tensor
        def _(pe):
            pe.wait_ge(nothing_ready, 1)
            for k in range(4):
                nc.tensor.matmul(counts[:, k, 0:DIG], g.ones[:, :], nothing[:, :], start=True, stop=False,
                                 skip_group_check=True)

            def add(c, i, par, steady):
                for u in range(U):
                    pe.wait_ge(smaller_ready, 4 * U * c + 4 * u + 4)
                    for k in range(4):
                        last = nc.tensor.matmul(counts[:, k, 0:DIG], g.ones[:, :], smaller[:, k, u, :],
                                                start=False, stop=False, skip_group_check=True)
                last.then_inc(smaller_used, 1)

            chunks(pe, add)


def rank_pass(nc, g, which, digit, pay, counts, tables, shift):
    with ExitStack() as ctx:
        sem = signals(nc, ctx)
        equal = ctx.enter_context(nc.sbuf_tensor(f"equal_{which}", [P, 2, U, DIG], BF16))
        unused = ctx.enter_context(nc.sbuf_tensor(f"unused_{which}", [P, 2, DIG], F32))
        place = ctx.enter_context(nc.sbuf_tensor(f"place_{which}", [P, 2, 2, U], F32))
        place_i = ctx.enter_context(nc.sbuf_tensor(f"place_i_{which}", [P, 2, 2, U], I32))
        row = ctx.enter_context(nc.sbuf_tensor(f"row_{which}", [P, 2, 2, U, 4], F32))
        er0 = sem(f"equal_ready0_{which}")
        er1 = sem(f"equal_ready1_{which}")
        rk0 = sem(f"ranked0_{which}")
        rk1 = sem(f"ranked1_{which}")
        rd0 = sem(f"read0_{which}")
        rd1 = sem(f"read1_{which}")
        mo0 = sem(f"moved_on0_{which}")
        mo1 = sem(f"moved_on1_{which}")
        rows_ready = sem(f"rows_ready_{which}")
        st0 = sem(f"stored0_{which}")
        st1 = sem(f"stored1_{which}")
        block = ctx.enter_context(nc.Block())
        equal_ready, ranked, read, moved_on, stored = (er0, er1), (rk0, rk1), (rd0, rd1), (mo0, mo1), (st0, st1)

        @block.vector
        def _(dve):
            def body(c, i, par, steady):
                def one_hot(u):
                    for k in range(2):
                        if steady or par:
                            dve.wait_ge(moved_on[k], U * c - U + u + 1)
                        nc.vector.tensor_scalar(equal[:, k, u, :], g.digits[:, :],
                                                digit[k][:, bass.ds(c * U + u, 1)], None,
                                                ALU.is_equal).then_inc(equal_ready[k], 1)

                one_hot(0)
                if steady:
                    dve.wait_ge(stored[par], 2 * U * 16 * i)
                for k in range(2):
                    nc.vector.tensor_copy(row[:, par, k, :, :], pay[k][:, bass.ds(c * U, U), :])
                for u in range(U):
                    if u + 1 < U:
                        one_hot(u + 1)
                    for k in range(2):
                        dve.wait_ge(ranked[k], U * c + u + 1)
                        nc.vector.tensor_tensor_reduce(unused[:, k, :], equal[:, k, u, :],
                                                       counts[:, 2 * k + which, 0:DIG], 1.0, 0.0, ALU.mult,
                                                       ALU.add, place[:, par, k, u:u + 1]).then_inc(read[k], 1)
                for k in range(2):
                    dve.wait_ge(read[k], U * c + U)
                    nc.vector.tensor_scalar(place_i[:, par, k, :], place[:, par, k, :], float(shift), None,
                                            ALU.add).then_inc(rows_ready, 1)

            chunks(dve, body)

        @block.tensor
        def _(pe):
            def body(c, i, par, steady):
                for u in range(U):
                    for k in range(2):
                        pe.wait_ge(equal_ready[k], U * c + u + 1)
                        nc.tensor.matmul(counts[:, 2 * k + which, 0:DIG], g.before[:, :], equal[:, k, u, :],
                                         start=False, stop=False, skip_group_check=True).then_inc(ranked[k], 1)
                    for k in range(2):
                        pe.wait_ge(read[k], U * c + u + 1)
                        nc.tensor.matmul(counts[:, 2 * k + which, 0:DIG], g.notbefore[:, :], equal[:, k, u, :],
                                         start=False, stop=False, skip_group_check=True).then_inc(moved_on[k], 1)

            chunks(pe, body)

        @block.gpsimd
        def _(pool):
            def body(c, i, par, steady):
                pool.wait_ge(rows_ready, 2 * c + 2)
                pool.nop(nofuse=True)
                for k in range(2):
                    for u in range(U):
                        nc.gpsimd.indirect_dma_start(
                            out=tables[k][:, :],
                            out_offset=bass.IndirectOffsetOnAxis(ap=place_i[:, par, k, u:u + 1], axis=0),
                            in_=row[:, par, k, u, :], in_offset=None).then_inc(stored[par], 16)

            chunks(pool, body)
            pool.wait_ge(st0, (NC // 2 + 1) * 2 * U * 16)
            pool.wait_ge(st1, (NC // 2) * 2 * U * 16)


def second_digit(nc, g, tables, digit, pay):
    with ExitStack() as ctx:
        sem = signals(nc, ctx)
        rows = ctx.enter_context(nc.sbuf_tensor("rows", [HALF, 2, 2, P * 4], F32))
        key_i = ctx.enter_context(nc.sbuf_tensor("key_i", [P, 2, T], I32))
        high_i = ctx.enter_context(nc.sbuf_tensor("high_i", [P, 2, T], I32))
        turned = ctx.enter_context(nc.psum_tensor("turned", [P, 2, 4, P], F32))
        rows_loaded = sem("rows_loaded")
        turned_ready = sem("turned_ready")
        turned_read = sem("turned_read")
        keys_ready = sem("keys_ready")
        high_ready = sem("high_ready")
        high_done = sem("high_done")
        block = ctx.enter_context(nc.Block())
        @block.sync
        def _(sp):
            for k in range(2):
                sp.dma_start(rows[:, k, :, :], tables[k][0:EP, :].rearrange("(h q p) f -> q h (p f)", h=2, p=P)
                             ).then_inc(rows_loaded, 16)

        @block.tensor
        def _(pe):
            pe.wait_ge(rows_loaded, 32)
            for n, (k, h) in enumerate([(k, h) for k in range(2) for h in range(2)]):
                if n >= 2:
                    pe.wait_ge(turned_read, n - 1)
                for f in range(3):
                    part = rows[:, k, h, :].rearrange("q (p f) -> q f p", f=4)[:, f, :]
                    last = nc.tensor.transpose(turned[:, n % 2, f, 0:HALF], part, g.ident[0:HALF, 0:HALF])
                last.then_inc(turned_ready, 1)

        @block.vector
        def _(dve):
            nc.vector.memset(pay[0][:, :, 3], 0.0)
            nc.vector.memset(pay[1][:, :, 3], 0.0)
            for n, (k, h) in enumerate([(k, h) for k in range(2) for h in range(2)]):
                dve.wait_ge(turned_ready, n + 1)
                nc.vector.tensor_copy(key_i[:, k, h * HALF:h * HALF + HALF],
                                      turned[:, n % 2, k, 0:HALF]).then_inc(keys_ready, 1)
                for f in range(3):
                    last = nc.vector.tensor_copy(pay[k][:, h * HALF:h * HALF + HALF, f],
                                                 turned[:, n % 2, f, 0:HALF])
                last.then_inc(turned_read, 1)
            dve.wait_ge(keys_ready, 4)
            nc.vector.tensor_scalar(high_i[:, :, :], key_i[:, :, :], 8, None,
                                    ALU.arith_shift_right).then_inc(high_ready, 1)
            dve.wait_ge(high_ready, 1)
            for k in range(2):
                nc.vector.tensor_copy(digit[k], high_i[:, k, :]).then_inc(high_done, 1)
            dve.wait_ge(high_done, 2)
            dve.wait_ge(turned_read, 4)


def describe(nc, g, tables, cols, same_rows):
    with ExitStack() as ctx:
        sem = signals(nc, ctx)
        ends = ctx.enter_context(nc.sbuf_tensor("ends", [1, 4], F32))
        win = ctx.enter_context(nc.sbuf_tensor("win", [P, 2, T + 2, 4], F32))
        number = ctx.enter_context(nc.sbuf_tensor("number", [P, T], F32))
        number_i = ctx.enter_context(nc.sbuf_tensor("number_i", [P, T], I32))
        same = ctx.enter_context(nc.sbuf_tensor("same", [P, 2, T], BF16))
        last = ctx.enter_context(nc.sbuf_tensor("last", [P, 3, T], F32))
        small = ctx.enter_context(nc.sbuf_tensor("small", [P, T], F32))
        away = ctx.enter_context(nc.sbuf_tensor("away", [P, 3, T], F32))
        made = ctx.enter_context(nc.sbuf_tensor("made", [P, NCOL, T], F32))
        tmp = ctx.enter_context(nc.sbuf_tensor("tmp", [P, 3, T], F32))
        one = ctx.enter_context(nc.sbuf_tensor("one", [2, EP // 8], F32))
        count = ctx.enter_context(nc.sbuf_tensor("count", [2, 2, EP // 8], F32))
        lines = ctx.enter_context(nc.sbuf_tensor("lines", [HALF, NCOL, 2, P], F32))
        turned = ctx.enter_context(nc.psum_tensor("turned2", [P, 2, 4, P], F32))
        numbered = sem("numbered")
        ends_set = sem("ends_set")
        ends_stored = sem("ends_stored")
        win_loaded = sem("win_loaded")
        step = sem("step")
        same_ready = sem("same_ready")
        same_stored = sem("same_stored")
        flags_loaded = sem("flags_loaded")
        spread_loaded = sem("spread_loaded")
        made_ready = sem("made_ready")
        made_stored = sem("made_stored")
        counted = sem("counted")
        cs0 = sem("count_stored0")
        cs1 = sem("count_stored1")
        lines_loaded = sem("lines_loaded")
        turned_ready = sem("turned_ready2")
        turned_read = sem("turned_read2")
        block = ctx.enter_context(nc.Block())
        S = EP // 8
        count_stored = (cs0, cs1)
        flags = g.same_s[0:2, :]

        @block.sync
        def _(sp):
            sp.wait_ge(ends_set, 1)
            for k in range(2):
                for r in (0, EP + 1):
                    sp.dma_start(tables[k][r:r + 1, :], ends[:, :]).then_inc(ends_stored, 16)
            sp.wait_ge(ends_stored, 64)
            for k in range(2):
                t = tables[k][0:1, :]
                src = bass.AP(t.tensor, 0, [[T * 4, P], [1, (T + 2) * 4]])
                sp.dma_start(win[:, k, :, :].rearrange("p t f -> p (t f)"), src).then_inc(win_loaded, 16)
            sp.wait_ge(same_ready, 2)
            for k in range(2):
                sp.dma_start(same_rows[k:k + 1, :].rearrange("a (p t) -> (a p) t", t=T),
                             same[:, k, :]).then_inc(same_stored, 16)
            sp.wait_ge(same_stored, 32)
            sp.dma_start(flags[:, :], same_rows[:, :]).then_inc(flags_loaded, 16)
            sp.dma_start(g.same_d[:, :], same_rows[0:1, :].to_broadcast([P, EP])).then_inc(spread_loaded, 16)
            sp.wait_ge(made_ready, 1)
            for k in range(NCOL - 2):
                sp.dma_start(cols[k:k + 1, :].rearrange("a (p t) -> (a p) t", t=T),
                             made[:, k, :]).then_inc(made_stored, 16)
            for n in range(8):
                sp.wait_ge(counted, n + 1)
                sp.dma_start(cols[CNT_D:CNT_S + 1, n * S:n * S + S], count[:, n % 2, :]).then_inc(count_stored[n % 2], 16)
            sp.dma_start(g.same_s[:, :], same_rows[1:2, :].to_broadcast([P, EP])).then_inc(spread_loaded, 16)
            sp.wait_ge(cs0, 64)
            sp.wait_ge(cs1, 64)
            sp.wait_ge(made_stored, 16 * (NCOL - 2))
            for k in range(NCOL):
                sp.dma_start(lines[:, k, :, :], cols[k:k + 1, :].rearrange("a (h q p) -> (a q) h p", h=2, p=P)
                             ).then_inc(lines_loaded, 16)
            sp.wait_ge(spread_loaded, 32)

        @block.gpsimd
        def _(pool):
            nc.gpsimd.iota(number_i[:, :], pattern=[[1, T]], base=0, channel_multiplier=T).then_inc(numbered, 1)

        @block.vector
        def _(dve):
            at = [0]

            def link(ins):
                at[0] += 1
                ins.then_inc(step, 1)
                dve.wait_ge(step, at[0])

            nc.vector.memset(ends[:, :], -1.0).then_inc(ends_set, 1)
            link(nc.vector.memset(one[:, :], 1.0))
            dve.wait_ge(numbered, 1)
            link(nc.vector.tensor_copy(number[:, :], number_i[:, :]))
            dve.wait_ge(win_loaded, 32)
            for k in range(2):
                key = win[:, k, 1:T + 1, k]
                nc.vector.tensor_tensor(same[:, k, :], key, win[:, k, 0:T, k], ALU.is_equal).then_inc(same_ready, 1)
                nc.vector.tensor_tensor(last[:, k, :], key, win[:, k, 2:T + 2, k], ALU.not_equal)
            nc.vector.tensor_scalar(away[:, 0, :], number[:, :], float(TRASH), None, ALU.add)
            nc.vector.tensor_scalar(away[:, 1, :], number[:, :], float(TRASH), None, ALU.add)
            nc.vector.tensor_scalar(away[:, 2, :], number[:, :], float(NH), None, ALU.add)
            link(nc.vector.tensor_scalar(small[:, :], win[:, 0, 1:T + 1, 0], float(NH), None, ALU.is_lt))
            link(nc.vector.tensor_tensor(last[:, 2, :], last[:, 0, :], small[:, :], ALU.mult))
            for n, (k, to) in enumerate(((0, OUT_D), (1, OUT_S), (0, OUT_HE))):
                link(nc.vector.tensor_tensor(tmp[:, n, :], win[:, k, 1:T + 1, k], away[:, n, :], ALU.subtract))
                link(nc.vector.tensor_tensor(tmp[:, n, :], tmp[:, n, :], last[:, n, :], ALU.mult))
                link(nc.vector.tensor_tensor(made[:, to, :], tmp[:, n, :], away[:, n, :], ALU.add))
            nc.vector.tensor_scalar(made[:, SRC_D, :], win[:, 0, 1:T + 1, 1], float(N - 1), None, ALU.min)
            nc.vector.tensor_scalar(made[:, DST_D, :], win[:, 0, 1:T + 1, 0], float(N - 1), None, ALU.min)
            nc.vector.tensor_scalar(made[:, HE_S, :], win[:, 1, 1:T + 1, 0], float(NH - 1), None, ALU.min)
            nc.vector.tensor_copy(made[:, WEIGHT, :], win[:, 0, 1:T + 1, 2]).then_inc(made_ready, 1)
            dve.wait_ge(flags_loaded, 16)
            for n in range(8):
                if n >= 2:
                    dve.wait_ge(count_stored[n % 2], 16 * (n // 2))
                if n:
                    dve.wait_ge(counted, n)
                nc.vector.tensor_tensor_scan(count[:, n % 2, :], flags[:, n * S:n * S + S], one[:, :],
                                             count[:, 1 - n % 2, S - 1:S] if n else 0.0,
                                             ALU.mult, ALU.add).then_inc(counted, 1)
            for n in range(NCOL):
                dve.wait_ge(turned_ready, n + 1)
                link(nc.vector.tensor_copy(g.col[:, n, :].rearrange("p (h q) -> p h q", h=2),
                                           turned[:, n % 2, 0:2, 0:HALF]))
                nc.vector.tensor_copy(g.idx[:, n, :], g.col[:, n, :]).then_inc(turned_read, 1)
            dve.wait_ge(turned_read, NCOL)
            link(nc.vector.reciprocal(g.col[:, CNT_D:CNT_S + 1, :], g.col[:, CNT_D:CNT_S + 1, :]))

        @block.tensor
        def _(pe):
            pe.wait_ge(lines_loaded, 16 * NCOL)
            for n in range(NCOL):
                if n >= 2:
                    pe.wait_ge(turned_read, n - 1)
                for h in range(2):
                    t = nc.tensor.transpose(turned[:, n % 2, h, 0:HALF], lines[:, n, h, :], g.ident[0:HALF, 0:HALF])
                t.then_inc(turned_ready, 1)


def sum_segments(nc, g, name, table, same, source, target, out, weight=None, relu_bias=None, w=None, scale=None):
    with ExitStack() as ctx:
        def sb(n, shape, dt):
            return ctx.enter_context(nc.sbuf_tensor(name + n, shape, dt))

        signal = signals(nc, ctx)

        def sem(n):
            return signal(name + n)

        rows = sb("rows", [P, 2, U, D], F32)
        weighted = sb("weighted", [P, 2, U, D], F32)
        message = sb("message", [P, 2, C], F32)
        total = sb("total", [P, 2, C], F32)
        done = sb("done", [P, 2, U, D], F32)
        source_rows = sb("source_rows", [P, 2, U], I32)
        target_rows = sb("target_rows", [P, 2, U], I32)
        w_sb = sb("w", [D, D], F32)
        bias_sb = sb("bias", [D, 1], F32)
        turned = ctx.enter_context(nc.psum_tensor(name + "turned", [P, 2, C], F32))
        back = ctx.enter_context(nc.psum_tensor(name + "back", [P, 2, U, D], F32))

        at_copied = sem("at_copied")
        gathered = (sem("gathered0"), sem("gathered1"))
        scattered = (sem("scattered0"), sem("scattered1"))
        weights_loaded = sem("weights_loaded")
        rows_weighted = sem("rows_weighted")
        message_turned = sem("message_turned")
        message_ready = sem("message_ready")
        summed = sem("summed")
        turned_back = sem("turned_back")
        rows_ready = sem("rows_ready")
        block = ctx.enter_context(nc.Block())
        n_loads = (w is not None) + (relu_bias is not None)

        @block.sync
        def _(sp):
            if w is not None:
                sp.dma_start(w_sb[:, :], w).then_inc(weights_loaded, 16)
            if relu_bias is not None:
                sp.dma_start(bias_sb[:, :], relu_bias.rearrange("(p a) -> p a", a=1)).then_inc(weights_loaded, 16)

        @block.gpsimd
        def _(pool):
            def fetch(c, i, par, steady):
                if steady:
                    pool.wait_ge(rows_weighted if weight is not None else message_turned, c - 1)
                nc.gpsimd.tensor_copy(source_rows[:, par, :], g.idx[:, source, bass.ds(c * U, U)]).then_inc(at_copied, 1)
                pool.wait_ge(at_copied, 2 * c - 1 if steady else c + 1)
                pool.nop(nofuse=True)
                for u in range(U):
                    nc.gpsimd.indirect_dma_start(
                        out=rows[:, par, u, :], out_offset=None, in_=table,
                        in_offset=bass.IndirectOffsetOnAxis(ap=source_rows[:, par, u:u + 1], axis=0)
                    ).then_inc(gathered[par], 16)

            def send(c, i, par, steady, copies):
                if steady:
                    pool.wait_ge(scattered[par], 16 * U * i)
                nc.gpsimd.tensor_copy(target_rows[:, par, :], g.idx[:, target, bass.ds(c * U, U)]).then_inc(at_copied, 1)
                pool.wait_ge(at_copied, copies)
                pool.wait_ge(rows_ready, c + 1)
                pool.nop(nofuse=True)
                for u in range(U):
                    nc.gpsimd.indirect_dma_start(
                        out=out, out_offset=bass.IndirectOffsetOnAxis(ap=target_rows[:, par, u:u + 1], axis=0),
                        in_=done[:, par, u, :], in_offset=None).then_inc(scattered[par], 16)

            fetch(0, 0, 0, False)
            fetch(1, 0, 1, False)
            for c in (2, 3):
                fetch(c, 1, c % 2, True)
                send(c - 2, 0, c % 2, False, 2 * c)
            with pool.Fori(2, NC // 2) as i:
                for par in range(2):
                    fetch(2 * i + par, i, par, True)
                    send(2 * i + par - 2, i - 1, par, True, 4 * i + 2 * par)
            fetch(NC - 1, NC // 2, 0, True)
            send(NC - 3, NC // 2 - 1, 0, True, 2 * NC - 2)
            send(NC - 2, NC // 2 - 1, 1, True, 2 * NC - 1)
            send(NC - 1, NC // 2, 0, True, 2 * NC)
            pool.wait_ge(scattered[0], 16 * U * (NC // 2 + 1))
            pool.wait_ge(scattered[1], 16 * U * (NC // 2))

        @block.tensor
        def _(pe):
            if n_loads:
                pe.wait_ge(weights_loaded, 16 * n_loads)
            turn = g.ident if w is None else w_sb

            def body(c, i, par, steady):
                if weight is not None:
                    pe.wait_ge(rows_weighted, c + 1)
                else:
                    pe.wait_ge(gathered[par], 16 * U * (i + 1))
                if steady:
                    pe.wait_ge(message_ready if relu_bias is not None else summed, c - 1)
                for u in range(U):
                    x = (rows if weight is None else weighted)[:, par, u, :]
                    t = nc.tensor.transpose(turned[:, par, u * P:u * P + P], x, g.ident[:, :])
                t.then_inc(message_turned, 1)

            def finish(c, i, par, steady):
                pe.wait_ge(summed, c + 1)
                if steady:
                    pe.wait_ge(rows_ready, c - 1)
                for u in range(U):
                    t = nc.tensor.matmul(back[:, par, u, :], total[:, par, u * P:u * P + P], turn[:, :],
                                         start=True, stop=True)
                t.then_inc(turned_back, 1)

            body(0, 0, 0, False)
            body(1, 0, 1, False)
            finish(0, 0, 0, False)
            body(2, 1, 0, True)
            finish(1, 0, 1, False)
            with pe.Fori(1, NC // 2) as i:
                body(2 * i + 1, i, 1, True)
                finish(2 * i, i, 0, True)
                body(2 * i + 2, i + 1, 0, True)
                finish(2 * i + 1, i, 1, True)
            finish(NC - 1, NC // 2, 0, True)

        @block.vector
        def _(dve):
            def body(c, i, par, steady):
                if weight is not None:
                    dve.wait_ge(gathered[par], 16 * U * (i + 1))
                    if steady:
                        dve.wait_ge(message_turned, c - 1)
                    for u in range(U):
                        t = nc.vector.tensor_scalar(weighted[:, par, u, :], rows[:, par, u, :],
                                                    g.col[:, weight, bass.ds(c * U + u, 1)], None, ALU.mult)
                    t.then_inc(rows_weighted, 1)
                if relu_bias is not None:
                    dve.wait_ge(message_ready, c + 1)
                else:
                    dve.wait_ge(message_turned, c + 1)
                if steady:
                    dve.wait_ge(turned_back, c - 1)
                if steady or par:
                    dve.wait_ge(summed, c)
                x = message[:, par, :] if relu_bias is not None else turned[:, par, :]
                nc.vector.tensor_tensor_scan(total[:, par, :], same[:, bass.ds(c * C, C)], x,
                                             total[:, 1 - par, C - 1:C] if steady or par else 0.0,
                                             ALU.mult, ALU.add).then_inc(summed, 1)

            chunks(dve, body)

        @block.scalar
        def _(act):
            if relu_bias is not None:
                act.wait_ge(weights_loaded, 16 * n_loads)

            def relu(c, i, par, steady):
                act.wait_ge(message_turned, c + 1)
                if steady:
                    act.wait_ge(summed, c - 1)
                nc.scalar.activation(message[:, par, :], turned[:, par, :], ACT.Relu,
                                     bias=bias_sb[:, 0:1]).then_inc(message_ready, 1)

            def body(c, i, par, steady):
                act.wait_ge(turned_back, c + 1)
                if steady:
                    act.wait_ge(scattered[par], 16 * U * i)
                if scale is None:
                    nc.scalar.activation(done[:, par, :, :], back[:, par, :, :], ACT.Copy).then_inc(rows_ready, 1)
                else:
                    for u in range(U):
                        t = nc.scalar.activation(done[:, par, u, :], back[:, par, u, :], ACT.Copy,
                                                 scale=g.col[:, scale, bass.ds(c * U + u, 1)])
                    t.then_inc(rows_ready, 1)

            if relu_bias is None:
                chunks(act, body)
            else:
                relu(0, 0, 0, False)
                relu(1, 0, 1, False)
                body(0, 0, 0, False)
                relu(2, 1, 0, True)
                body(1, 0, 1, False)
                with act.Fori(1, NC // 2) as i:
                    relu(2 * i + 1, i, 1, True)
                    body(2 * i, i, 0, True)
                    relu(2 * i + 2, i + 1, 0, True)
                    body(2 * i + 1, i, 1, True)
                body(NC - 1, NC // 2, 0, True)


def make_penalties(nc, g):
    with ExitStack() as ctx:
        made_penalties = signals(nc, ctx)("made_penalties")
        block = ctx.enter_context(nc.Block())

        @block.vector
        def _(dve):
            nc.vector.tensor_scalar(g.same_s[:, :], g.same_d[:, :], BIG, -BIG, ALU.mult,
                                    ALU.add).then_inc(made_penalties, 1)
            dve.wait_ge(made_penalties, 1)


def attend(nc, g, name, table, wq, bq, wk, bk, wv, bv, out):
    with ExitStack() as ctx:
        def sb(n, shape, dt=F32):
            return ctx.enter_context(nc.sbuf_tensor(name + n, shape, dt))

        signal = signals(nc, ctx)

        def sem(n):
            return signal(name + n)

        def ps(n, shape):
            return ctx.enter_context(nc.psum_tensor(name + n, shape, F32))

        rows = sb("rows", [P, 2, 2, U, D])
        x_src = sb("x_src", [P, 2, C])
        x_dst = sb("x_dst", [P, 2, C])
        query = sb("query", [P, C])
        qk = sb("qk", [P, C])
        top = sb("top", [P, 2, C + 1])
        enter = sb("enter", [P, 2, C])
        keep = sb("keep", [P, 2, C])
        mass = sb("mass", [P, 2, C])
        message = sb("message", [P, C])
        total = sb("total", [P, 2, C])
        share = sb("share", [P, U * HEADS])
        done = sb("done", [P, 2, U, D])
        source_rows = sb("source_rows", [P, 2, 2, U], I32)
        target_rows = sb("target_rows", [P, 2, U], I32)
        w_sb = sb("w", [D, 3, D])
        b_sb = sb("b", [D, 3])
        bq_scaled = sb("bq_scaled", [D, 1])
        t_src = ps("t_src", [P, C])
        t_dst = ps("t_dst", [P, C])
        key = ps("key", [P, C])
        raw_query = ps("raw_query", [P, C])
        value = ps("value", [P, C])
        score = ps("score", [P, C])
        back = ps("back", [P, U, D])
        mass_back = ps("mass_back", [P, U * HEADS])

        weights_loaded = sem("weights_loaded")
        bias_scaled = sem("bias_scaled")
        source_rows_copied = sem("source_rows_copied")
        target_rows_copied = sem("target_rows_copied")
        gathered = (sem("gathered0"), sem("gathered1"))
        scattered = (sem("scattered0"), sem("scattered1"))
        turned = sem("turned")
        turned_copied = sem("turned_copied")
        keys_ready = sem("keys_ready")
        values_ready = sem("values_ready")
        query_ready = sem("query_ready")
        qk_ready = sem("qk_ready")
        scored = sem("scored")
        first_top = sem("first_top")
        top_ready = sem("top_ready")
        enter_shifted = sem("enter_shifted")
        keep_step = sem("keep_step")
        enter_ready = sem("enter_ready")
        keep_ready = sem("keep_ready")
        mass_ready = sem("mass_ready")
        message_ready = sem("message_ready")
        total_ready = sem("total_ready")
        turned_back = sem("turned_back")
        share_step = sem("share_step")
        rows_ready = sem("rows_ready")
        block = ctx.enter_context(nc.Block())
        SCALE = HD ** -0.5
        LAG = 3

        @block.sync
        def _(sp):
            for n, (w, b) in enumerate(((wk, bk), (wv, bv), (wq, bq))):
                sp.dma_start(w_sb[:, n, :], w).then_inc(weights_loaded, 16)
                sp.dma_start(b_sb[:, n:n + 1], b.rearrange("(p a) -> p a", a=1)).then_inc(weights_loaded, 16)

        @block.gpsimd
        def _(pool):
            def fetch(c, i, par):
                after(pool, turned, c - 1)
                for k, n in enumerate((SRC_D, DST_D)):
                    nc.gpsimd.tensor_copy(source_rows[:, par, k, :], g.idx[:, n, bass.ds(c * U, U)]
                                          ).then_inc(source_rows_copied, 1)
                pool.wait_ge(source_rows_copied, 2 * c + 2)
                pool.nop(nofuse=True)
                for k in range(2):
                    for u in range(U):
                        nc.gpsimd.indirect_dma_start(
                            out=rows[:, par, k, u, :], out_offset=None, in_=table,
                            in_offset=bass.IndirectOffsetOnAxis(ap=source_rows[:, par, k, u:u + 1], axis=0)
                        ).then_inc(gathered[par], 16)

            def send(c, i, par):
                after(pool, scattered[par], 16 * U * i)
                nc.gpsimd.tensor_copy(target_rows[:, par, :], g.idx[:, OUT_D, bass.ds(c * U, U)]
                                      ).then_inc(target_rows_copied, 1)
                pool.wait_ge(target_rows_copied, c + 1)
                pool.wait_ge(rows_ready, c + 1)
                pool.nop(nofuse=True)
                for u in range(U):
                    nc.gpsimd.indirect_dma_start(
                        out=out, out_offset=bass.IndirectOffsetOnAxis(ap=target_rows[:, par, u:u + 1], axis=0),
                        in_=done[:, par, u, :], in_offset=None).then_inc(scattered[par], 16)

            def step(c, i, par):
                if now := chunk_before(c, i, par, 0):
                    fetch(*now)
                if was := chunk_before(c, i, par, LAG):
                    send(*was)

            steps(pool, step, LAG)
            pool.wait_ge(scattered[0], 16 * U * (NC // 2 + 1))
            pool.wait_ge(scattered[1], 16 * U * (NC // 2))

        @block.tensor
        def _(pe):
            def turn(c, i, par):
                pe.wait_ge(gathered[par], 2 * U * 16 * (i + 1))
                after(pe, turned_copied, c)
                for k, to in enumerate((t_src, t_dst)):
                    for u in range(U):
                        t = nc.tensor.transpose(to[:, u * P:u * P + P], rows[:, par, k, u, :], g.ident[:, :])
                t.then_inc(turned, 1)

            def keys(c, i, par):
                pe.wait_ge(turned_copied, c + 1)
                after(pe, qk_ready, c)
                nc.tensor.matmul(raw_query[:, :], w_sb[:, 2, :], x_dst[:, par, :], start=True, stop=True)
                nc.tensor.matmul(key[:, :], w_sb[:, 0, :], x_src[:, par, :], start=True,
                                 stop=True).then_inc(keys_ready, 1)

            def rate(c, i, par):
                pe.wait_ge(qk_ready, c + 1)
                after(pe, enter_shifted, c)
                nc.tensor.matmul(score[:, :], g.heads[:, :], qk[:, :], start=True, stop=True).then_inc(scored, 1)

            def values(c, i, par):
                after(pe, message_ready, c)
                nc.tensor.matmul(value[:, :], w_sb[:, 1, :], x_src[:, par, :], start=True,
                                 stop=True).then_inc(values_ready, 1)

            def finish(c, i, par):
                pe.wait_ge(total_ready, c + 1)
                pe.wait_ge(mass_ready, c + 1)
                after(pe, rows_ready, c)
                for u in range(U):
                    nc.tensor.matmul(mass_back[:, u * HEADS:u * HEADS + HEADS], mass[:, par, u * P:u * P + P],
                                     g.ident[:, 0:D:HD], start=True, stop=True)
                for u in range(U):
                    t = nc.tensor.transpose(back[:, u, :], total[:, par, u * P:u * P + P], g.ident[:, :])
                t.then_inc(turned_back, 1)

            pe.wait_ge(weights_loaded, 16 * 6)

            def step(c, i, par):
                if now := chunk_before(c, i, par, 0):
                    turn(*now)
                if was := chunk_before(c, i, par, 1):
                    rate(*was)
                    values(*was)
                if now := chunk_before(c, i, par, 0):
                    keys(*now)
                if was := chunk_before(c, i, par, 2):
                    finish(*was)

            steps(pe, step, 2)

        @block.scalar
        def _(act):
            def copy(c, i, par):
                act.wait_ge(turned, c + 1)
                after(act, values_ready, c - 1)
                nc.scalar.activation(x_dst[:, par, :], t_dst[:, :], ACT.Copy)
                nc.scalar.activation(x_src[:, par, :], t_src[:, :], ACT.Copy).then_inc(turned_copied, 1)

            def ask(c, i, par):
                act.wait_ge(keys_ready, c + 1)
                after(act, qk_ready, c)
                nc.scalar.activation(query[:, :], raw_query[:, :], ACT.Identity, bias=bq_scaled[:, 0:1],
                                     scale=SCALE).then_inc(query_ready, 1)

            def exps(c, i, par):
                act.wait_ge(enter_shifted, c + 1)
                nc.scalar.activation(enter[:, par, :], enter[:, par, :], ACT.Exp).then_inc(enter_ready, 1)
                act.wait_ge(keep_step, 2 * c + 2)
                nc.scalar.activation(keep[:, par, :], keep[:, par, :], ACT.Exp).then_inc(keep_ready, 1)

            act.wait_ge(bias_scaled, 1)

            def step(c, i, par):
                if now := chunk_before(c, i, par, 0):
                    copy(*now)
                    ask(*now)
                if was := chunk_before(c, i, par, 1):
                    exps(*was)

            steps(act, step, 1)

        @block.vector
        def _(dve):
            def multiply(c, i, par):
                dve.wait_ge(query_ready, c + 1)
                after(dve, scored, c)
                nc.vector.scalar_tensor_tensor(out=qk[:, :], in0=key[:, :], scalar=b_sb[:, 0:1],
                                               in1=query[:, :], op0=ALU.add, op1=ALU.mult
                                               ).then_inc(qk_ready, 1)

            def shift(c, i, par):
                if isinstance(c, int) and c == 0:
                    nc.vector.memset(top[:, 0, 0:1], 0.0).then_inc(first_top, 1)
                else:
                    dve.wait_ge(top_ready, c)
                    nc.vector.tensor_copy(top[:, par, 0:1], top[:, 1 - par, C:C + 1]).then_inc(first_top, 1)
                dve.wait_ge(first_top, c + 1)
                dve.wait_ge(scored, c + 1)
                penalty = g.same_s[:, bass.ds(c * C, C)]
                nc.vector.tensor_tensor_scan(top[:, par, 1:C + 1], penalty, score[:, :], top[:, par, 0:1],
                                             ALU.add, ALU.max).then_inc(top_ready, 1)
                after(dve, total_ready, c - 1)
                dve.wait_ge(top_ready, c + 1)
                nc.vector.tensor_tensor(keep[:, par, :], top[:, par, 0:C], penalty, ALU.add).then_inc(keep_step, 1)
                nc.vector.tensor_tensor(enter[:, par, :], score[:, :], top[:, par, 1:C + 1], ALU.subtract
                                        ).then_inc(enter_shifted, 1)
                dve.wait_ge(keep_step, 2 * c + 1)
                nc.vector.tensor_tensor(keep[:, par, :], keep[:, par, :], top[:, par, 1:C + 1], ALU.subtract
                                        ).then_inc(keep_step, 1)

            def add_up(c, i, par):
                first = isinstance(c, int) and c == 0
                dve.wait_ge(enter_ready, c + 1)
                dve.wait_ge(values_ready, c + 1)
                after(dve, total_ready, c)
                nc.vector.scalar_tensor_tensor(out=message[:, :], in0=value[:, :], scalar=b_sb[:, 1:2],
                                               in1=enter[:, par, :], op0=ALU.add, op1=ALU.mult
                                               ).then_inc(message_ready, 1)
                dve.wait_ge(keep_ready, c + 1)
                after(dve, turned_back, c - 1)
                after(dve, mass_ready, c)
                nc.vector.tensor_tensor_scan(mass[:, par, :], keep[:, par, :], enter[:, par, :],
                                             0.0 if first else mass[:, 1 - par, C - 1:C],
                                             ALU.mult, ALU.add).then_inc(mass_ready, 1)
                dve.wait_ge(message_ready, c + 1)
                nc.vector.tensor_tensor_scan(total[:, par, :], keep[:, par, :], message[:, :],
                                             0.0 if first else total[:, 1 - par, C - 1:C],
                                             ALU.mult, ALU.add).then_inc(total_ready, 1)

            def divide(c, i, par):
                dve.wait_ge(turned_back, c + 1)
                after(dve, rows_ready, c)
                nc.vector.tensor_scalar(share[:, :], mass_back[:, :], 1e-16, None, ALU.add).then_inc(share_step, 1)
                dve.wait_ge(share_step, 2 * c + 1)
                nc.vector.reciprocal(share[:, :], share[:, :]).then_inc(share_step, 1)
                dve.wait_ge(share_step, 2 * c + 2)
                after(dve, scattered[par], 16 * U * i)
                nc.vector.tensor_tensor(done[:, par, :, :].rearrange("p u (h d) -> p (u h) d", h=HEADS),
                                        back[:, :, :].rearrange("p u (h d) -> p (u h) d", h=HEADS),
                                        share[:, :].rearrange("p (a b) -> p a b", b=1).to_broadcast(
                                            [P, U * HEADS, HD]), ALU.mult).then_inc(rows_ready, 1)

            dve.wait_ge(weights_loaded, 16 * 6)
            nc.vector.tensor_scalar(bq_scaled[:, :], b_sb[:, 2:3], SCALE, None, ALU.mult).then_inc(bias_scaled, 1)

            def step(c, i, par):
                if was := chunk_before(c, i, par, 1):
                    shift(*was)
                if now := chunk_before(c, i, par, 0):
                    multiply(*now)
                if was := chunk_before(c, i, par, 2):
                    divide(*was)
                if was := chunk_before(c, i, par, 1):
                    add_up(*was)

            steps(dve, step, 2)


def after(eng, sem, value):
    if not isinstance(value, int) or value > 0:
        eng.wait_ge(sem, value)


def steps(eng, step, lag):
    for c in range(6):
        step(c, c // 2, c % 2)
    with eng.Fori(3, NC // 2) as i:
        step(2 * i, i, 0)
        step(2 * i + 1, i, 1)
    for c in range(NC - 1, NC + lag):
        step(c, c // 2, c % 2)


def chunk_before(c, i, par, lag):
    if isinstance(c, int) and not 0 <= c - lag < NC:
        return None
    p = (par - lag) % 2
    return c - lag, i + (par - lag - p) // 2, p


ADD, TWICE, CONV, LAST, RELU = range(5)
RING = 6


def group_steps(eng, step, lag):
    head = NG % RING + RING
    for n in range(head):
        step(n // RING, n % RING)
    with eng.Fori(1, (NG - head) // RING + 1) as i:
        for r in range(RING):
            step(i + (head % RING + r) // RING, (head % RING + r) % RING)
    for n in range(NG, NG + lag):
        step(n // RING, n % RING)


def group_before(q, m, lag):
    if isinstance(q, int) and not 0 <= RING * q + m - lag < NG:
        return None
    return (q, m - lag) if m >= lag else (q - 1, m + RING - lag)


def update_nodes(nc, g, name, kind, h, agg, out, bias=None, ws=None, gain=None, offset=None, outer=None):
    with ExitStack() as ctx:
        def sb(n, shape, dt=F32):
            return ctx.enter_context(nc.sbuf_tensor(name + n, shape, dt))

        signal = signals(nc, ctx)

        def sem(n):
            return signal(name + n)

        conv = kind in (CONV, LAST)
        R = 6 if kind == CONV else 3
        node = sb("node", [NP, R, G, D])
        agg_in = sb("agg_in", [NP, 3, G, D])
        y = sb("y", [NP, 3, G, D])
        z = sb("z", [NP, 3, G, D]) if conv else None
        outer_in = sb("outer_in", [NP, 3, G, D]) if kind == LAST else None
        result = sb("result", [NP, 2 if conv else 3, G, D])
        turned_sb = sb("turned_sb", [D, 2, G, P]) if conv else None
        w_sb = sb("w_sb", [D, D])
        on_all = sb("on_all", [NP, 3, D])
        stats = sb("stats", [NP, G, 6])
        mean_var = sb("mean_var", [NP, 2, G, 2])
        var = sb("var", [NP, G])
        half = sb("half", [NP, G], I32)
        root = sb("root", [NP, G])
        square = sb("square", [NP, G])
        rstd = sb("rstd", [NP, 2, G])
        shift = sb("shift", [NP, 2, G])
        if conv:
            turned = ctx.enter_context(nc.psum_tensor(name + "turned", [D, 2, G, P], F32))
            product = ctx.enter_context(nc.psum_tensor(name + "product", [P, 2, G, D], F32))

        consts_loaded = sem("consts_loaded")
        node_loaded = [sem(f"node_loaded{m}") for m in range(R)]
        agg_loaded = [sem(f"agg_loaded{m}") for m in range(3)]
        outer_loaded = [sem(f"outer_loaded{m}") for m in range(3)] if kind == LAST else None
        RO = 2 if conv else 3
        stored = [sem(f"stored{m}") for m in range(RO)]
        bias_added = sem("bias_added")
        turned_ready = sem("turned_ready")
        turned_copied = sem("turned_copied")
        product_ready = sem("product_ready")
        sum_ready = sem("sum_ready")
        activated = sem("activated")
        outer_added = sem("outer_added")
        stats_ready = sem("stats_ready")
        mean_var_ready = sem("mean_var_ready")
        newton_step = sem("newton_step")
        norm_ready = sem("norm_ready")
        normed = sem("normed")
        scaled = sem("scaled")
        offset_added = sem("offset_added")
        result_ready = sem("result_ready")
        block = ctx.enter_context(nc.Block())

        parts = (slice(0, SPLIT), slice(SPLIT, NP))
        n_const = len([v for v in (bias, gain, offset, ws) if v is not None])
        ADDED = 1 if conv else 0
        MEASURED = 2 if kind == LAST else ADDED
        NORMED = MEASURED + 1
        ACTIVATED = 3 if kind == CONV else 1
        STORED = {CONV: 5, LAST: 4}.get(kind, 2)

        def number(q, m):
            return RING * q + m

        def uses(q, m, ring):
            return q * (RING // ring) + m // ring + 1

        def of_group(table, s, grp):
            return table[0:N, :].rearrange("(p r) f -> p (r f)", r=RP)[s, bass.ds(grp * G * D, G * D)]

        def row_of(n):
            return on_all[:, n:n + 1, :].to_broadcast([NP, G, D])

        @block.sync
        def _(sp):
            for n, v in enumerate((bias, gain, offset)):
                if v is not None:
                    sp.dma_start(on_all[:, n, :], v.rearrange("(a f) -> a f", a=1).to_broadcast([NP, D])
                                 ).then_inc(consts_loaded, 16)
            if ws is not None:
                sp.dma_start(w_sb[:, :], ws).then_inc(consts_loaded, 16)

            def step(q, m):
                grp = number(q, m)
                after(sp, {CONV: result_ready, LAST: turned_ready}.get(kind, sum_ready), grp + 1 - R)
                for s in parts:
                    sp.dma_start(node[s, m % R, :, :].rearrange("p a f -> p (a f)"), of_group(h, s, grp)
                                 ).then_inc(node_loaded[m % R], 16)
                after(sp, sum_ready, grp - 2)
                for s in parts:
                    sp.dma_start(agg_in[s, m % 3, :, :].rearrange("p a f -> p (a f)"), of_group(agg, s, grp)
                                 ).then_inc(agg_loaded[m % 3], 16)
                if kind == LAST:
                    after(sp, outer_added, grp - 2)
                    for s in parts:
                        sp.dma_start(outer_in[s, m % 3, :, :].rearrange("p a f -> p (a f)"),
                                     of_group(outer, s, grp)).then_inc(outer_loaded[m % 3], 16)

            group_steps(sp, step, 0)

        @block.gpsimd
        def _(pool):
            if n_const:
                pool.wait_ge(consts_loaded, 16 * n_const)

            def add_bias(q, m):
                pool.wait_ge(agg_loaded[m % 3], 32 * uses(q, m, 3))
                nc.gpsimd.tensor_tensor(agg_in[:, m % 3, :, :], agg_in[:, m % 3, :, :], row_of(0),
                                        ALU.add).then_inc(bias_added, 1)

            def affine(q, m):
                grp = number(q, m)
                pool.wait_ge(normed, grp + 1)
                nc.gpsimd.tensor_tensor(z[:, m % 3, :, :], z[:, m % 3, :, :], row_of(1), ALU.mult
                                        ).then_inc(scaled, 1)
                pool.wait_ge(scaled, grp + 1)
                nc.gpsimd.tensor_tensor(z[:, m % 3, :, :], z[:, m % 3, :, :], row_of(2), ALU.add
                                        ).then_inc(offset_added, 1)

            def step(q, m):
                if bias is not None and (now := group_before(q, m, 0)):
                    add_bias(*now)
                if kind == CONV and (was := group_before(q, m, NORMED)):
                    affine(*was)

            group_steps(pool, step, NORMED if kind == CONV else 0)

        @block.tensor
        def _(pe):
            if not conv:
                return
            pe.wait_ge(consts_loaded, 16 * n_const)

            def turn(q, m):
                p = m % 2
                pe.wait_ge(node_loaded[m % R], 32 * uses(q, m, R))
                after(pe, turned_copied, number(q, m) - 1)
                for j in range(G):
                    t = nc.tensor.transpose(turned[:, p, j, 0:NP], node[:, m % R, j, :], g.ident[0:NP, 0:NP])
                t.then_inc(turned_ready, 1)

            def project(q, m):
                grp = number(q, m)
                p = m % 2
                pe.wait_ge(turned_copied, grp + 1)
                after(pe, sum_ready, grp - 1)
                for j in range(G):
                    t = nc.tensor.matmul(product[0:NP, p, j, :], turned_sb[:, p, j, 0:NP], w_sb[:, :],
                                         start=True, stop=True)
                t.then_inc(product_ready, 1)

            def step(q, m):
                if now := group_before(q, m, 0):
                    turn(*now)
                if was := group_before(q, m, 1):
                    project(*was)

            group_steps(pe, step, 1)

        @block.scalar
        def _(act):
            def copy(q, m):
                grp = number(q, m)
                act.wait_ge(turned_ready, grp + 1)
                after(act, product_ready, grp - 1)
                nc.scalar.activation(turned_sb[:, m % 2, :, 0:NP], turned[:, m % 2, :, 0:NP],
                                     ACT.Copy).then_inc(turned_copied, 1)

            def normalize(q, m):
                grp = number(q, m)
                act.wait_ge(norm_ready, grp + 1)
                if kind == CONV:
                    after(act, result_ready, grp - 2)
                    to = z[:, m % 3, :, :]
                else:
                    after(act, stored[m % RO], 32 * (uses(q, m, RO) - 1))
                    to = result[:, m % RO, :, :]
                x = (z if kind == LAST else y)[:, m % 3, :, :]
                for j in range(G):
                    t = nc.scalar.activation(to[:, j, :], x[:, j, :], ACT.Identity,
                                             bias=shift[:, m % 2, j:j + 1], scale=rstd[:, m % 2, j:j + 1])
                t.then_inc(normed, 1)

            def gelu(q, m):
                act.wait_ge(offset_added if kind == CONV else sum_ready, number(q, m) + 1)
                x = (z if kind == CONV else y)[:, m % 3, :, :]
                nc.scalar.activation(x, x, ACT.Gelu).then_inc(activated, 1)

            def store(q, m):
                act.wait_ge(result_ready if kind == CONV else normed, number(q, m) + 1)
                for s in parts:
                    act.dma_start(of_group(out, s, number(q, m)),
                                  result[s, m % RO, :, :].rearrange("p a f -> p (a f)")
                                  ).then_inc(stored[m % RO], 16)

            def step(q, m):
                if conv and (now := group_before(q, m, 0)):
                    copy(*now)
                if kind == LAST and (was := group_before(q, m, ACTIVATED)):
                    gelu(*was)
                if was := group_before(q, m, STORED):
                    store(*was)
                if was := group_before(q, m, NORMED):
                    normalize(*was)
                if kind == CONV and (was := group_before(q, m, ACTIVATED)):
                    gelu(*was)

            group_steps(act, step, STORED)
            for m in range(RO):
                act.wait_ge(stored[m], 32 * len(range(m, NG, RO)))

        @block.vector
        def _(dve):
            NEWTON = 12

            def add(q, m):
                grp = number(q, m)
                if conv:
                    dve.wait_ge(product_ready, grp + 1)
                else:
                    dve.wait_ge(node_loaded[m % R], 32 * uses(q, m, R))
                if bias is not None:
                    dve.wait_ge(bias_added, grp + 1)
                else:
                    dve.wait_ge(agg_loaded[m % 3], 32 * uses(q, m, 3))
                after(dve, outer_added if kind == LAST else normed, grp - 2)
                to = y[:, m % 3, :, :]
                a = agg_in[:, m % 3, :, :]
                if conv:
                    ins = nc.vector.tensor_tensor(to, product[0:NP, m % 2, :, :], a, ALU.add)
                elif kind == ADD:
                    ins = nc.vector.tensor_tensor(to, node[:, m % R, :, :], a, ALU.add)
                elif kind == TWICE:
                    ins = nc.vector.scalar_tensor_tensor(out=to, in0=node[:, m % R, :, :], scalar=2.0,
                                                         in1=a, op0=ALU.mult, op1=ALU.add)
                else:
                    ins = nc.vector.scalar_tensor_tensor(out=to, in0=a, scalar=0.0,
                                                         in1=node[:, m % R, :, :], op0=ALU.max, op1=ALU.add)
                ins.then_inc(sum_ready, 1)

            def add_outer(q, m):
                grp = number(q, m)
                dve.wait_ge(activated, grp + 1)
                dve.wait_ge(outer_loaded[m % 3], 32 * uses(q, m, 3))
                after(dve, normed, grp - 2)
                nc.vector.tensor_tensor(z[:, m % 3, :, :], y[:, m % 3, :, :], outer_in[:, m % 3, :, :],
                                        ALU.add).then_inc(outer_added, 1)

            def measure(q, m, n):
                grp = number(q, m)
                if n == 0:
                    dve.wait_ge(outer_added if kind == LAST else sum_ready, grp + 1)
                    after(dve, mean_var_ready, grp)
                if n == G:
                    after(dve, norm_ready, grp - 1)
                    dve.wait_ge(stats_ready, grp + 1)
                    dve.nop(nofuse=True)
                if n < G:
                    x = (z if kind == LAST else y)[:, m % 3, n, :]
                    ins = nc.vector.bn_stats(stats[:, n, :], x)
                    if n == G - 1:
                        ins.then_inc(stats_ready, 1)
                else:
                    ins = nc.vector.bn_aggr(mean_var[:, m % 2, n - G, :], stats[:, n - G, :])
                    if n == 2 * G - 1:
                        ins.then_inc(mean_var_ready, 1)

            def newton(q, m, n):
                grp = number(q, m)
                if n == 0:
                    dve.wait_ge(mean_var_ready, grp + 1)
                    after(dve, normed, grp - 1)
                    ins = nc.vector.tensor_scalar(var[:, :], mean_var[:, m % 2, :, 1], EPS, None, ALU.add)
                else:
                    dve.wait_ge(newton_step, NEWTON * grp + n)
                if n == 1:
                    ins = nc.vector.tensor_scalar(half[:, :], var[:, :].bitcast(I32), 1, None,
                                                  ALU.arith_shift_right)
                if n == 2:
                    ins = nc.vector.tensor_scalar(root[:, :].bitcast(I32), half[:, :], -1.0, float(0x5F3759DF),
                                                  ALU.mult, ALU.add)
                if n in (3, 6, 9):
                    ins = nc.vector.tensor_tensor(square[:, :], root[:, :], root[:, :], ALU.mult)
                if n in (4, 7, 10):
                    ins = nc.vector.scalar_tensor_tensor(out=square[:, :], in0=square[:, :], scalar=-0.5,
                                                         in1=var[:, :], op0=ALU.mult, op1=ALU.mult)
                if n in (5, 8, 11):
                    to = rstd[:, m % 2, :] if n == 11 else root[:, :]
                    ins = nc.vector.scalar_tensor_tensor(out=to, in0=square[:, :], scalar=1.5, in1=root[:, :],
                                                         op0=ALU.add, op1=ALU.mult)
                if n < NEWTON:
                    ins.then_inc(newton_step, 1)
                else:
                    nc.vector.scalar_tensor_tensor(out=shift[:, m % 2, :], in0=mean_var[:, m % 2, :, 0],
                                                   scalar=-1.0, in1=rstd[:, m % 2, :], op0=ALU.mult,
                                                   op1=ALU.mult).then_inc(norm_ready, 1)

            def keep_on(q, m):
                grp = number(q, m)
                dve.wait_ge(activated, grp + 1)
                after(dve, stored[m % 2], 32 * (uses(q, m, 2) - 1))
                nc.vector.tensor_tensor(result[:, m % 2, :, :], node[:, m % R, :, :], z[:, m % 3, :, :],
                                        ALU.add).then_inc(result_ready, 1)

            def step(q, m):
                if was := group_before(q, m, ADDED):
                    add(*was)
                if kind == LAST and (was := group_before(q, m, MEASURED)):
                    add_outer(*was)
                now, was = group_before(q, m, MEASURED), group_before(q, m, NORMED)
                for n in range(2 * G):
                    if was and n <= NEWTON:
                        newton(*was, n)
                    if now:
                        measure(*now, n)
                if kind == CONV and (was := group_before(q, m, ACTIVATED + 1)):
                    keep_on(*was)

            group_steps(dve, step, ACTIVATED + 1 if kind == CONV else NORMED)


def build(nc, x, src, dst, edge_weight, w1, b1, w2, b2, wq, bq, wk, bk, wv, bv, ws, bs, ln_g, ln_b, w3, b3, out):
    def dram(name, shape, dt=F32):
        return nc.dram_tensor(name, shape, dt).ap()

    g = Program()
    g.agg_s = dram("agg_s", [TRASH + EP, D])
    g.agg_d = dram("agg_d", [TRASH + EP, D])
    g.he = dram("he", [NH + EP, D])
    by_low = [dram(f"by_low{k}", [EP, 4]) for k in range(2)]
    by_key = [dram(f"by_key{k}", [EP + 2, 4]) for k in range(2)]
    cols = dram("cols", [NCOL, EP])
    same_rows = dram("same_rows", [2, EP], BF16)
    h = [dram(f"h{n}", [N, D]) for n in range(3)]

    with ExitStack() as ctx:
        constants(nc, ctx, g)
        with (
            nc.sbuf_tensor("pay0", [P, T, 4], F32) as pay0,
            nc.sbuf_tensor("pay1", [P, T, 4], F32) as pay1,
            nc.sbuf_tensor("digit", [P, 4, T], F32) as digit,
            nc.psum_tensor("counts", [P, 4, 512], F32) as counts,
        ):
            count_digits(nc, g, dst, src, edge_weight, pay0, digit, counts)
            rank_pass(nc, g, 0, (digit[:, 0, :], digit[:, 2, :]), (pay0, pay0), counts, by_low, 0)
            second_digit(nc, g, by_low, (digit[:, 1, :], digit[:, 3, :]), (pay0, pay1))
            rank_pass(nc, g, 1, (digit[:, 1, :], digit[:, 3, :]), (pay0, pay1), counts, by_key, 1)
        describe(nc, g, by_key, cols, same_rows)

        sum_segments(nc, g, "a", x, g.same_d, SRC_D, OUT_HE, g.he, w=w1, scale=CNT_D)
        sum_segments(nc, g, "b", g.he[0:NH, :], g.same_s, HE_S, OUT_S, g.agg_s, scale=CNT_S)
        sum_segments(nc, g, "c", g.agg_s[0:N, :], g.same_d, SRC_D, OUT_HE, g.he, relu_bias=b1, w=w2, scale=CNT_D)
        sum_segments(nc, g, "d", g.he[0:NH, :], g.same_s, HE_S, OUT_S, g.agg_s, scale=CNT_S)
        update_nodes(nc, g, "e", ADD, x, g.agg_s, h[0], bias=b2)

        sum_segments(nc, g, "f", h[0], g.same_d, SRC_D, OUT_D, g.agg_d)
        update_nodes(nc, g, "g", TWICE, h[0], g.agg_d, h[1])

        make_penalties(nc, g)
        at = 1
        for n in range(LAYERS):
            attend(nc, g, f"h{n}", h[at], wq[n], bq[n], wk[n], bk[n], wv[n], bv[n], g.agg_d)
            to = 2 if at == 0 else 0
            if n < LAYERS - 1:
                update_nodes(nc, g, f"i{n}", CONV, h[at], g.agg_d, h[to], bias=bs[n], ws=ws[n], gain=ln_g[n],
                             offset=ln_b[n])
            else:
                update_nodes(nc, g, f"i{n}", LAST, h[at], g.agg_d, h[to], bias=bs[n], ws=ws[n], outer=h[1])
            at = to

        sum_segments(nc, g, "j", h[at], g.same_d, SRC_D, OUT_D, g.agg_d, weight=WEIGHT, w=w3)
        update_nodes(nc, g, "k", RELU, h[at], g.agg_d, out, bias=b3)


_INS = ["x", "src", "dst", "edge_weight", "L0_gnn_W1", "L0_gnn_b1", "L0_gnn_W2", "L0_gnn_b2", "L2_gnn_Wq",
        "L2_gnn_bq", "L2_gnn_Wk", "L2_gnn_bk", "L2_gnn_Wv", "L2_gnn_bv", "L2_gnn_Ws", "L2_gnn_bs", "L2_gnn_ln_g",
        "L2_gnn_ln_b", "L3_gnn_weight", "L3_gnn_bias"]


def kernel(**inputs):
    import numpy as np
    import concourse.bacc as bacc
    from concourse.bass_utils import run_bass_kernel_spmd

    nc = bacc.Bacc("TRN2", target_bir_lowering=False, num_devices=1)
    arrays, args = {}, []
    for name in _INS:
        a = np.ascontiguousarray(inputs[name])
        arrays[f"in_{name}"] = a
        args.append(nc.dram_tensor(f"in_{name}", a.shape, mybir.dt.from_np(a.dtype), kind="ExternalInput").ap())
    args.append(nc.dram_tensor("out", (N, D), F32, kind="ExternalOutput").ap())
    build(nc, *args)
    r = run_bass_kernel_spmd(nc, [arrays], core_ids=[0])
    return r.results[0]["out"]
```

```python
from contextlib import ExitStack

import concourse.bass as bass
from concourse import mybir

F32 = mybir.dt.float32
I32 = mybir.dt.int32
BF16 = mybir.dt.bfloat16
ALU = mybir.AluOpType
ACT = mybir.ActivationFunctionType

P = 128
D = 128
HEADS = 4
HD = D // HEADS
N = 50000
NH = 10000
E = 25000
LAYERS = 5
EPS = 1e-5

T = -(-E // P)
EP = T * P
FULL = E // T
REST = E - FULL * T
U = 4
C = U * P
NC = T // U
DIG = 256
HALF = T // 2
PADKEY = N
TRASH = N + 1
BIG = 1e30
FILL = 1000

NP = 125
RP = N // NP
G = 8
NG = RP // G
SPLIT = 112

assert T % U == 0 and NC % 2 == 1 and NG % 2 == 0 and NP * RP == N

SRC_D, DST_D, OUT_D, OUT_HE, WEIGHT, HE_S, OUT_S, CNT_D, CNT_S = range(9)
NCOL = 9
SAME_D, SAME_S, PENALTY = range(3)


class Program:
    pass


def chunks(eng, body):
    for c in range(2):
        body(c, 0, c, False)
    with eng.Fori(1, NC // 2) as i:
        body(2 * i, i, 0, True)
        body(2 * i + 1, i, 1, True)
    body(NC - 1, NC // 2, 0, True)


def after(eng, sem, value):
    if not isinstance(value, int) or value > 0:
        eng.wait_ge(sem, value)


def steps(eng, step, lag):
    for c in range(6):
        step(c, c // 2, c % 2)
    with eng.Fori(3, NC // 2) as i:
        step(2 * i, i, 0)
        step(2 * i + 1, i, 1)
    for c in range(NC - 1, NC + lag):
        step(c, c // 2, c % 2)


def chunk_before(c, i, par, lag):
    if isinstance(c, int) and not 0 <= c - lag < NC:
        return None
    p = (par - lag) % 2
    return c - lag, i + (par - lag - p) // 2, p


def signals(nc, ctx):
    taken = []

    def clear():
        nc.clear_and_free_semaphores(taken)
        nc.all_engine_barrier()

    def sem(name):
        taken.append(nc.alloc_semaphore(name))
        return taken[-1]

    ctx.callback(clear)
    return sem


def constants(nc, life, g):
    def sb(name, shape, dt):
        return life.enter_context(nc.sbuf_tensor(name, shape, dt))

    g.ident = sb("ident", [P, P], F32)
    g.before = sb("before", [P, P], BF16)
    g.notbefore = sb("notbefore", [P, P], BF16)
    g.ones = sb("ones", [P, P], BF16)
    g.halves = sb("halves", [P, P], BF16)
    g.heads = sb("heads", [P, P], F32)
    g.digits = sb("digits", [P, DIG], BF16)
    g.col = sb("col", [P, NCOL, T], F32)
    g.idx = sb("idx", [P, NCOL, T], I32)
    with ExitStack() as ctx:
        sem = signals(nc, ctx)
        digits_i = ctx.enter_context(nc.sbuf_tensor("digits_i", [P, DIG], I32))
        set_up = sem("set_up")
        iota_done = sem("iota_done")
        all_done = sem("all_done")
        block = ctx.enter_context(nc.Block())

        @block.vector
        def _(dve):
            nc.vector.memset(g.ident[:, :], 0.0).then_inc(set_up, 1)
            nc.vector.memset(g.before[:, :], 1.0).then_inc(set_up, 1)
            nc.vector.memset(g.notbefore[:, :], 1.0).then_inc(set_up, 1)
            nc.vector.memset(g.ones[:, :], 1.0).then_inc(all_done, 1)
            nc.vector.memset(g.halves[:, :], 0.5).then_inc(all_done, 1)
            nc.vector.memset(g.heads[:, :], 0.0).then_inc(set_up, 1)
            dve.wait_ge(set_up, 4)
            for h in range(HEADS):
                s = slice(h * HD, h * HD + HD)
                nc.vector.memset(g.heads[s, s], 1.0).then_inc(all_done, 1)
            dve.wait_ge(iota_done, 1)
            nc.vector.tensor_copy(g.digits[:, :], digits_i[:, :]).then_inc(all_done, 1)
            dve.wait_ge(all_done, HEADS + 3)

        @block.gpsimd
        def _(pool):
            nc.gpsimd.iota(digits_i[:, :], pattern=[[1, DIG]], base=0, channel_multiplier=0).then_inc(iota_done, 1)
            pool.wait_ge(set_up, 4)
            nc.gpsimd.affine_select(out=g.ident[:, :], in_=g.ident[:, :], compare_op=ALU.not_equal, fill=1.0,
                                    base=0, pattern=[[-1, P]], channel_multiplier=1)
            nc.gpsimd.affine_select(out=g.before[:, :], in_=g.before[:, :], compare_op=ALU.is_gt, fill=0.0,
                                    base=0, pattern=[[1, P]], channel_multiplier=-1)
            nc.gpsimd.affine_select(out=g.notbefore[:, :], in_=g.notbefore[:, :], compare_op=ALU.is_ge, fill=0.0,
                                    base=0, pattern=[[-1, P]], channel_multiplier=1).then_inc(iota_done, 1)
            pool.wait_ge(iota_done, 2)


def count_digits(nc, g, dst, src, weight, pay, digit, border, counts):
    with ExitStack() as ctx:
        sem = signals(nc, ctx)
        raw = ctx.enter_context(nc.sbuf_tensor("raw", [P, 2, T], I32))
        low = ctx.enter_context(nc.sbuf_tensor("low", [P, 4, T], I32))
        smaller = ctx.enter_context(nc.sbuf_tensor("smaller", [P, 2, U, DIG], BF16))
        signs = ctx.enter_context(nc.sbuf_tensor("signs", [P, 2, U, DIG], BF16))
        start = ctx.enter_context(nc.sbuf_tensor("start", [P, 2, DIG], BF16))
        zero = ctx.enter_context(nc.sbuf_tensor("zero", [NP, FILL * D // NP], F32))
        cleared = sem("cleared")
        loaded = sem("loaded")
        start_ready = sem("start_ready")
        borders_ready = sem("borders_ready")
        zero_ready = sem("zero_ready")
        zeros_stored = sem("zeros_stored")
        signs_ready = sem("signs_ready")
        signs_used = sem("signs_used")
        copied = sem("copied")
        masked = sem("masked")
        digits_ready = sem("digits_ready")
        smaller_ready = sem("smaller_ready")
        smaller_used = sem("smaller_used")
        block = ctx.enter_context(nc.Block())

        @block.sync
        def _(sp):
            sp.wait_ge(cleared, 2)
            for k, x in enumerate((dst, src)):
                sp.dma_start(raw[0:FULL, k, :], x[0:FULL * T].rearrange("(p t) -> p t", t=T)).then_inc(loaded, 16)
                sp.dma_start(raw[FULL:FULL + 1, k, 0:REST],
                             x[FULL * T:E].rearrange("(a t) -> a t", a=1)).then_inc(loaded, 16)
            sp.dma_start(g.idx[0:FULL, WEIGHT, :].bitcast(F32),
                         weight[0:FULL * T].rearrange("(p t) -> p t", t=T)).then_inc(loaded, 16)
            sp.dma_start(g.idx[FULL:FULL + 1, WEIGHT, 0:REST].bitcast(F32),
                         weight[FULL * T:E].rearrange("(a t) -> a t", a=1)).then_inc(loaded, 16)
            sp.wait_ge(zero_ready, 1)
            for n in range(NH // FILL):
                sp.dma_start(g.he[n * FILL:n * FILL + FILL, :].rearrange("(p a) f -> p (a f)", p=NP),
                             zero[:, :]).then_inc(zeros_stored, 16)
            sp.wait_ge(zeros_stored, 16 * NH // FILL)

        @block.gpsimd
        def _(pool):
            nc.gpsimd.memset(zero[:, :], 0.0).then_inc(zero_ready, 1)

        @block.vector
        def _(dve):
            nc.vector.memset(raw[:, :, :], PADKEY).then_inc(cleared, 1)
            nc.vector.memset(g.idx[:, WEIGHT, :].bitcast(F32), 0.0).then_inc(cleared, 1)
            nc.vector.memset(pay[:, :, 3], 0.0)
            nc.vector.memset(start[:, 0, :], 0.0).then_inc(start_ready, 1)
            nc.vector.memset(start[:, 1, :], float(HALF)).then_inc(start_ready, 1)
            dve.wait_ge(loaded, 6 * 16)
            nc.vector.tensor_copy(pay[:, :, 0], raw[:, 0, :]).then_inc(copied, 1)
            nc.vector.tensor_copy(pay[:, :, 1], raw[:, 1, :]).then_inc(copied, 1)
            nc.vector.tensor_copy(pay[:, :, 2], g.idx[:, WEIGHT, :].bitcast(F32)).then_inc(copied, 1)
            for k in range(2):
                nc.vector.tensor_scalar(low[:, 2 * k, :], raw[:, k, :], DIG - 1, None,
                                        ALU.bitwise_and).then_inc(masked, 1)
                nc.vector.tensor_scalar(low[:, 2 * k + 1, :], raw[:, k, :], 8, None,
                                        ALU.arith_shift_right).then_inc(masked, 1)
            dve.wait_ge(masked, 4)
            nc.vector.tensor_copy(digit[:, :, :], low[:, :, :]).then_inc(digits_ready, 1)
            dve.wait_ge(digits_ready, 1)
            nc.vector.tensor_scalar(border[:, :, :], digit[:, :, :], -1.0, -0.5, ALU.mult, ALU.add
                                    ).then_inc(borders_ready, 1)

            def compare(c, i, par, steady):
                if steady:
                    dve.wait_ge(smaller_used, c - 1)
                for u in range(U):
                    ins = nc.vector.tensor_scalar(smaller[:, par, u, :], g.digits[:, :],
                                                  digit[:, 0, bass.ds(c * U + u, 1)], None, ALU.is_gt)
                ins.then_inc(smaller_ready, 1)

            chunks(dve, compare)

        @block.scalar
        def _(act):
            act.wait_ge(borders_ready, 1)

            def compare(c, i, par, steady):
                if steady:
                    act.wait_ge(signs_used, c - 1)
                    act.nop(nofuse=True)
                for u in range(U):
                    ins = nc.scalar.activation(signs[:, par, u, :], g.digits[:, :], ACT.Sign,
                                               bias=border[:, 2, bass.ds(c * U + u, 1)])
                ins.then_inc(signs_ready, 1)

            chunks(act, compare)

        @block.tensor
        def _(pe):
            pe.wait_ge(start_ready, 2)
            for k in range(4):
                nc.tensor.matmul(counts[:, k, 0:DIG], g.ones[:, :], start[:, int(k > 0), :], start=True, stop=False,
                                 skip_group_check=True)

            def add(c, i, par, steady):
                pe.wait_ge(smaller_ready, c + 1)
                for u in range(U):
                    last = nc.tensor.matmul(counts[:, 0, 0:DIG], g.ones[:, :], smaller[:, par, u, :],
                                            start=False, stop=False, skip_group_check=True)
                last.then_inc(smaller_used, 1)
                pe.wait_ge(signs_ready, c + 1)
                for u in range(U):
                    last = nc.tensor.matmul(counts[:, 2, 0:DIG], g.halves[:, :], signs[:, par, u, :],
                                            start=False, stop=False, skip_group_check=True)
                last.then_inc(signs_used, 1)

            chunks(pe, add)


def rank_pass(nc, g, which, digit, pay, counts, tables, shift, fill_table, next_border=None):
    with ExitStack() as ctx:
        sem = signals(nc, ctx)
        equal = ctx.enter_context(nc.sbuf_tensor(f"equal_{which}", [P, 2, U, DIG], BF16))
        unused = ctx.enter_context(nc.sbuf_tensor(f"unused_{which}", [P, 2, DIG], F32))
        place = ctx.enter_context(nc.sbuf_tensor(f"place_{which}", [P, 2, 2, U], F32))
        place_i = ctx.enter_context(nc.sbuf_tensor(f"place_i_{which}", [P, 2, 2, U], I32))
        row = ctx.enter_context(nc.sbuf_tensor(f"row_{which}", [P, 2, 2, U, 4], F32))
        er0 = sem(f"equal_ready0_{which}")
        er1 = sem(f"equal_ready1_{which}")
        rk0 = sem(f"ranked0_{which}")
        rk1 = sem(f"ranked1_{which}")
        rd0 = sem(f"read0_{which}")
        rd1 = sem(f"read1_{which}")
        mo0 = sem(f"moved_on0_{which}")
        mo1 = sem(f"moved_on1_{which}")
        rows_ready = sem(f"rows_ready_{which}")
        st0 = sem(f"stored0_{which}")
        st1 = sem(f"stored1_{which}")
        zero = ctx.enter_context(nc.sbuf_tensor(f"zero_{which}", [NP, FILL * D // NP], F32))
        zero_ready = sem(f"zero_ready_{which}")
        zeros_stored = sem(f"zeros_stored_{which}")
        first = next_border is not None
        if first:
            signs = ctx.enter_context(nc.sbuf_tensor("signs_next", [P, 2, 2, U, DIG], BF16))
            signs_ready = sem("signs_next_ready")
            signs_used = sem("signs_next_used")
        block = ctx.enter_context(nc.Block())
        equal_ready, ranked, rank_read, moved_on, stored = (er0, er1), (rk0, rk1), (rd0, rd1), (mo0, mo1), (st0, st1)

        @block.sync
        def _(sp):
            def fill(n):
                sp.dma_start(fill_table.rearrange("(n p a) f -> n p (a f)", p=NP, a=FILL // NP)[n],
                             zero[:, :]).then_inc(zeros_stored, 16)

            def body(c, i, par, steady):
                sp.wait_ge(rows_ready, 2 * c + 2)
                fill(c)

            sp.wait_ge(zero_ready, 1)
            chunks(sp, body)
            for n in range(NC, N // FILL):
                fill(n)
            sp.wait_ge(zeros_stored, 16 * N // FILL)

        @block.vector
        def _(dve):
            nc.vector.memset(zero[:, :], 0.0).then_inc(zero_ready, 1)

            def body(c, i, par, steady):
                def one_hot(u):
                    for k in range(2):
                        if steady or par:
                            dve.wait_ge(moved_on[k], U * c - U + u + 1)
                        nc.vector.tensor_scalar(equal[:, k, u, :], g.digits[:, :],
                                                digit[k][:, bass.ds(c * U + u, 1)], None,
                                                ALU.is_equal).then_inc(equal_ready[k], 1)

                one_hot(0)
                if steady:
                    dve.wait_ge(stored[par], 2 * U * 16 * i)
                for k in range(2):
                    nc.vector.tensor_copy(row[:, par, k, :, :], pay[k][:, bass.ds(c * U, U), :])
                for u in range(U):
                    if u + 1 < U:
                        one_hot(u + 1)
                    for k in range(2):
                        dve.wait_ge(ranked[k], U * c + u + 1)
                        nc.vector.tensor_tensor_reduce(unused[:, k, :], equal[:, k, u, :],
                                                       counts[:, 2 * k + which, 0:DIG], 1.0, 0.0, ALU.mult,
                                                       ALU.add, place[:, par, k, u:u + 1]).then_inc(rank_read[k], 1)
                for k in range(2):
                    dve.wait_ge(rank_read[k], U * c + U)
                    nc.vector.tensor_scalar(place_i[:, par, k, :], place[:, par, k, :], float(shift), None,
                                            ALU.add).then_inc(rows_ready, 1)

            chunks(dve, body)

        @block.scalar
        def _(act):
            def body(c, i, par, steady):
                if steady:
                    act.wait_ge(signs_used, U * c - U)
                    act.nop(nofuse=True)
                for u in range(U):
                    for k in range(2):
                        ins = nc.scalar.activation(signs[:, par, k, u, :], g.digits[:, :], ACT.Sign,
                                                   bias=next_border[k][:, bass.ds(c * U + u, 1)])
                    ins.then_inc(signs_ready, 1)

            if first:
                chunks(act, body)

        @block.tensor
        def _(pe):
            def count(c, par, u):
                pe.wait_ge(signs_ready, U * c + u + 1)
                for k in range(2):
                    last = nc.tensor.matmul(counts[:, 2 * k + 1, 0:DIG], g.halves[:, :], signs[:, par, k, u, :],
                                            start=False, stop=False, skip_group_check=True)
                last.then_inc(signs_used, 1)

            def body(c, i, par, steady):
                for u in range(U):
                    for k in range(2):
                        pe.wait_ge(equal_ready[k], U * c + u + 1)
                        nc.tensor.matmul(counts[:, 2 * k + which, 0:DIG], g.before[:, :], equal[:, k, u, :],
                                         start=False, stop=False, skip_group_check=True).then_inc(ranked[k], 1)
                    if first and u:
                        count(c, par, u - 1)
                    elif first and (steady or par):
                        count(c - 1, 1 - par, U - 1)
                    for k in range(2):
                        pe.wait_ge(rank_read[k], U * c + u + 1)
                        nc.tensor.matmul(counts[:, 2 * k + which, 0:DIG], g.notbefore[:, :], equal[:, k, u, :],
                                         start=False, stop=False, skip_group_check=True).then_inc(moved_on[k], 1)

            chunks(pe, body)
            if first:
                count(NC - 1, 0, U - 1)

        @block.gpsimd
        def _(pool):
            def body(c, i, par, steady):
                pool.wait_ge(rows_ready, 2 * c + 2)
                pool.nop(nofuse=True)
                for k in range(2):
                    for u in range(U):
                        nc.gpsimd.indirect_dma_start(
                            out=tables[k][:, :],
                            out_offset=bass.IndirectOffsetOnAxis(ap=place_i[:, par, k, u:u + 1], axis=0),
                            in_=row[:, par, k, u, :], in_offset=None).then_inc(stored[par], 16)

            chunks(pool, body)
            pool.wait_ge(st0, (NC // 2 + 1) * 2 * U * 16)
            pool.wait_ge(st1, (NC // 2) * 2 * U * 16)


def second_digit(nc, g, tables, digit, pay):
    with ExitStack() as ctx:
        sem = signals(nc, ctx)
        rows = ctx.enter_context(nc.sbuf_tensor("rows", [HALF, 2, 2, P * 4], F32))
        key_i = ctx.enter_context(nc.sbuf_tensor("key_i", [P, 2, T], I32))
        high_i = ctx.enter_context(nc.sbuf_tensor("high_i", [P, 2, T], I32))
        turned = ctx.enter_context(nc.psum_tensor("turned", [P, 2, 4, P], F32))
        rows_loaded = sem("rows_loaded")
        turned_ready = sem("turned_ready")
        turned_read = sem("turned_read")
        keys_ready = sem("keys_ready")
        high_ready = sem("high_ready")
        high_done = sem("high_done")
        block = ctx.enter_context(nc.Block())

        @block.sync
        def _(sp):
            for k in range(2):
                sp.dma_start(rows[:, k, :, :], tables[k][0:EP, :].rearrange("(h q p) f -> q h (p f)", h=2, p=P)
                             ).then_inc(rows_loaded, 16)

        @block.tensor
        def _(pe):
            pe.wait_ge(rows_loaded, 32)
            for n, (k, h) in enumerate([(k, h) for k in range(2) for h in range(2)]):
                if n >= 2:
                    pe.wait_ge(turned_read, n - 1)
                for f in range(3):
                    part = rows[:, k, h, :].rearrange("q (p f) -> q f p", f=4)[:, f, :]
                    last = nc.tensor.transpose(turned[:, n % 2, f, 0:HALF], part, g.ident[0:HALF, 0:HALF])
                last.then_inc(turned_ready, 1)

        @block.vector
        def _(dve):
            nc.vector.memset(pay[0][:, :, 3], 0.0)
            nc.vector.memset(pay[1][:, :, 3], 0.0)
            for n, (k, h) in enumerate([(k, h) for k in range(2) for h in range(2)]):
                dve.wait_ge(turned_ready, n + 1)
                nc.vector.tensor_copy(key_i[:, k, h * HALF:h * HALF + HALF],
                                      turned[:, n % 2, k, 0:HALF]).then_inc(keys_ready, 1)
                for f in range(3):
                    last = nc.vector.tensor_copy(pay[k][:, h * HALF:h * HALF + HALF, f],
                                                 turned[:, n % 2, f, 0:HALF])
                last.then_inc(turned_read, 1)
            dve.wait_ge(keys_ready, 4)
            nc.vector.tensor_scalar(high_i[:, :, :], key_i[:, :, :], 8, None,
                                    ALU.arith_shift_right).then_inc(high_ready, 1)
            dve.wait_ge(high_ready, 1)
            for k in range(2):
                nc.vector.tensor_copy(digit[k], high_i[:, k, :]).then_inc(high_done, 1)
            dve.wait_ge(high_done, 2)
            dve.wait_ge(turned_read, 4)


def describe(nc, g, tables, cols):
    with ExitStack() as ctx:
        sem = signals(nc, ctx)
        ends = ctx.enter_context(nc.sbuf_tensor("ends", [1, 4], F32))
        win = ctx.enter_context(nc.sbuf_tensor("win", [P, 2, T + 2, 4], F32))
        number = ctx.enter_context(nc.sbuf_tensor("number", [P, T], F32))
        number_i = ctx.enter_context(nc.sbuf_tensor("number_i", [P, T], I32))
        same = ctx.enter_context(nc.sbuf_tensor("same", [P, 3, T], BF16))
        last = ctx.enter_context(nc.sbuf_tensor("last", [P, 3, T], F32))
        small = ctx.enter_context(nc.sbuf_tensor("small", [P, T], F32))
        away = ctx.enter_context(nc.sbuf_tensor("away", [P, 3, T], F32))
        made = ctx.enter_context(nc.sbuf_tensor("made", [P, NCOL, T], F32))
        tmp = ctx.enter_context(nc.sbuf_tensor("tmp", [P, 3, T], F32))
        one = ctx.enter_context(nc.sbuf_tensor("one", [P, T], F32))
        count = ctx.enter_context(nc.sbuf_tensor("count", [P, 2, T], F32))
        goes_on = ctx.enter_context(nc.sbuf_tensor("goes_on", [P, 2, T], F32))
        whole = ctx.enter_context(nc.sbuf_tensor("whole", [2, P], F32))
        carry = ctx.enter_context(nc.sbuf_tensor("carry", [2, P + 1], F32))
        carry_col = ctx.enter_context(nc.sbuf_tensor("carry_col", [P, 2], F32))
        ends_turned = ctx.enter_context(nc.psum_tensor("ends_turned", [2, 2, P], F32))
        carry_turned = ctx.enter_context(nc.psum_tensor("carry_turned", [P, 2], F32))
        lines = ctx.enter_context(nc.sbuf_tensor("lines", [HALF, NCOL, 2, P], F32))
        turned = ctx.enter_context(nc.psum_tensor("turned2", [P, 2, 4, P], F32))
        numbered = sem("numbered")
        ends_set = sem("ends_set")
        ends_stored = sem("ends_stored")
        win_loaded = sem("win_loaded")
        step = sem("step")
        same_ready = sem("same_ready")
        same_stored = sem("same_stored")
        counts_ready = sem("counts_ready")
        carried = sem("carried")
        ends_ready = sem("ends_ready")
        carry_turned_ready = sem("carry_turned_ready")
        penalties_ready = sem("penalties_ready")
        made_ready = sem("made_ready")
        made_stored = sem("made_stored")
        lines_loaded = sem("lines_loaded")
        turned_ready = sem("turned_ready2")
        turned_read = sem("turned_read2")
        block = ctx.enter_context(nc.Block())

        @block.sync
        def _(sp):
            sp.wait_ge(ends_set, 1)
            for k in range(2):
                for r in (0, EP + 1):
                    sp.dma_start(tables[k][r:r + 1, :], ends[:, :]).then_inc(ends_stored, 16)
            sp.wait_ge(ends_stored, 64)
            for k in range(2):
                t = tables[k][0:1, :]
                src = bass.AP(t.tensor, 0, [[T * 4, P], [1, (T + 2) * 4]])
                sp.dma_start(win[:, k, :, :].rearrange("p t f -> p (t f)"), src).then_inc(win_loaded, 16)
            sp.wait_ge(same_ready, 2)
            for k in range(2):
                sp.dma_start(g.flags[k:k + 1, :].rearrange("a (p t) -> (a p) t", t=T),
                             same[:, k, :]).then_inc(same_stored, 16)
            sp.wait_ge(penalties_ready, 1)
            sp.dma_start(g.flags[PENALTY:PENALTY + 1, :].rearrange("a (p t) -> (a p) t", t=T),
                         same[:, PENALTY, :]).then_inc(same_stored, 16)
            for k in range(NCOL):
                if k in (0, NCOL - 2):
                    sp.wait_ge(made_ready, 1 if k == 0 else 2)
                sp.dma_start(cols[k:k + 1, :].rearrange("a (p t) -> (a p) t", t=T),
                             made[:, k, :]).then_inc(made_stored, 16)
            sp.wait_ge(made_stored, 16 * NCOL)
            for k in range(NCOL):
                sp.dma_start(lines[:, k, :, :], cols[k:k + 1, :].rearrange("a (h q p) -> (a q) h p", h=2, p=P)
                             ).then_inc(lines_loaded, 16)
            sp.wait_ge(same_stored, 48)

        @block.gpsimd
        def _(pool):
            nc.gpsimd.iota(number_i[:, :], pattern=[[1, T]], base=0, channel_multiplier=T).then_inc(numbered, 1)

        @block.vector
        def _(dve):
            at = [0]

            def link(ins):
                at[0] += 1
                ins.then_inc(step, 1)
                dve.wait_ge(step, at[0])

            nc.vector.memset(ends[:, :], -1.0).then_inc(ends_set, 1)
            link(nc.vector.memset(one[:, :], 1.0))
            dve.wait_ge(numbered, 1)
            link(nc.vector.tensor_copy(number[:, :], number_i[:, :]))
            dve.wait_ge(win_loaded, 32)
            for k in range(2):
                key = win[:, k, 1:T + 1, k]
                nc.vector.tensor_tensor(same[:, k, :], key, win[:, k, 0:T, k], ALU.is_equal).then_inc(same_ready, 1)
                nc.vector.tensor_tensor(last[:, k, :], key, win[:, k, 2:T + 2, k], ALU.not_equal)
            dve.wait_ge(same_ready, 2)
            nc.vector.tensor_scalar(same[:, PENALTY, :], same[:, SAME_D, :], BIG, -BIG, ALU.mult,
                                    ALU.add).then_inc(penalties_ready, 1)
            nc.vector.tensor_scalar(away[:, 0, :], number[:, :], float(TRASH), None, ALU.add)
            nc.vector.tensor_scalar(away[:, 1, :], number[:, :], float(TRASH), None, ALU.add)
            nc.vector.tensor_scalar(away[:, 2, :], number[:, :], float(NH), None, ALU.add)
            link(nc.vector.tensor_scalar(small[:, :], win[:, 0, 1:T + 1, 0], float(NH), None, ALU.is_lt))
            link(nc.vector.tensor_tensor(last[:, 2, :], last[:, 0, :], small[:, :], ALU.mult))
            for n, (k, to) in enumerate(((0, OUT_D), (1, OUT_S), (0, OUT_HE))):
                link(nc.vector.tensor_tensor(tmp[:, n, :], win[:, k, 1:T + 1, k], away[:, n, :], ALU.subtract))
                link(nc.vector.tensor_tensor(tmp[:, n, :], tmp[:, n, :], last[:, n, :], ALU.mult))
                link(nc.vector.tensor_tensor(made[:, to, :], tmp[:, n, :], away[:, n, :], ALU.add))
            nc.vector.tensor_scalar(made[:, SRC_D, :], win[:, 0, 1:T + 1, 1], float(N - 1), None, ALU.min)
            nc.vector.tensor_scalar(made[:, DST_D, :], win[:, 0, 1:T + 1, 0], float(N - 1), None, ALU.min)
            nc.vector.tensor_scalar(made[:, HE_S, :], win[:, 1, 1:T + 1, 0], float(NH - 1), None, ALU.min)
            nc.vector.tensor_copy(made[:, WEIGHT, :], win[:, 0, 1:T + 1, 2]).then_inc(made_ready, 1)
            for k in range(2):
                nc.vector.tensor_tensor_scan(count[:, k, :], same[:, k, :], one[:, :], 0.0, ALU.mult, ALU.add)
                link(nc.vector.tensor_tensor_scan(goes_on[:, k, :], same[:, k, :], one[:, :], 1.0, ALU.mult,
                                                  ALU.mult))
            nc.vector.memset(carry[:, 0:1], 0.0).then_inc(counts_ready, 1)
            dve.wait_ge(ends_ready, 1)
            link(nc.vector.tensor_copy(whole[:, :], ends_turned[:, 1, :]))
            dve.wait_ge(counts_ready, 1)
            nc.vector.tensor_tensor_scan(carry[:, 1:P + 1], whole[:, :], ends_turned[:, 0, :], 0.0,
                                         ALU.mult, ALU.add).then_inc(carried, 1)
            dve.wait_ge(carry_turned_ready, 1)
            link(nc.vector.tensor_copy(carry_col[:, :], carry_turned[:, :]))
            for k in range(2):
                counted = nc.vector.scalar_tensor_tensor(out=made[:, CNT_D + k, :], in0=goes_on[:, k, :],
                                                         scalar=carry_col[:, k:k + 1], in1=count[:, k, :],
                                                         op0=ALU.mult, op1=ALU.add)
            counted.then_inc(made_ready, 1)
            for n in range(NCOL):
                dve.wait_ge(turned_ready, n + 1)
                link(nc.vector.tensor_copy(g.col[:, n, :].rearrange("p (h q) -> p h q", h=2),
                                           turned[:, n % 2, 0:2, 0:HALF]))
                nc.vector.tensor_copy(g.idx[:, n, :], g.col[:, n, :]).then_inc(turned_read, 1)
            dve.wait_ge(turned_read, NCOL)
            link(nc.vector.reciprocal(g.col[:, CNT_D:CNT_S + 1, :], g.col[:, CNT_D:CNT_S + 1, :]))

        @block.tensor
        def _(pe):
            pe.wait_ge(counts_ready, 1)
            nc.tensor.transpose(ends_turned[:, 0, :], count[:, :, T - 1], g.ident[:, :])
            nc.tensor.transpose(ends_turned[:, 1, :], goes_on[:, :, T - 1], g.ident[:, :]).then_inc(ends_ready, 1)
            pe.wait_ge(carried, 1)
            nc.tensor.transpose(carry_turned[:, :], carry[:, 0:P], g.ident[0:2, 0:2]).then_inc(carry_turned_ready, 1)
            pe.wait_ge(lines_loaded, 16 * NCOL)
            for n in range(NCOL):
                if n >= 2:
                    pe.wait_ge(turned_read, n - 1)
                for h in range(2):
                    t = nc.tensor.transpose(turned[:, n % 2, h, 0:HALF], lines[:, n, h, :], g.ident[0:HALF, 0:HALF])
                t.then_inc(turned_ready, 1)


def sum_segments(nc, g, name, table, flags, source, target, out, weight=None, relu_bias=None, w=None, scale=None):
    with ExitStack() as ctx:
        def sb(n, shape, dt):
            return ctx.enter_context(nc.sbuf_tensor(name + n, shape, dt))

        signal = signals(nc, ctx)

        def sem(n):
            return signal(name + n)

        same = sb("same", [P, 2, C], BF16)
        rows = sb("rows", [P, 2, U, D], F32)
        weighted = sb("weighted", [P, 2, U, D], F32)
        message = sb("message", [P, 2, C], F32)
        total = sb("total", [P, 2, C], F32)
        done = sb("done", [P, 2, U, D], F32)
        source_rows = sb("source_rows", [P, 2, U], I32)
        target_rows = sb("target_rows", [P, 2, U], I32)
        w_sb = sb("w", [D, D], F32)
        bias_sb = sb("bias", [D, 1], F32)
        turned = ctx.enter_context(nc.psum_tensor(name + "turned", [P, 2, C], F32))
        back = ctx.enter_context(nc.psum_tensor(name + "back", [P, 2, U, D], F32))

        flags_loaded = (sem("flags_loaded0"), sem("flags_loaded1"))
        sources_ready = sem("sources_ready")
        targets_ready = sem("targets_ready")
        gathered = (sem("gathered0"), sem("gathered1"))
        scattered = (sem("scattered0"), sem("scattered1"))
        weights_loaded = sem("weights_loaded")
        rows_weighted = sem("rows_weighted")
        message_turned = sem("message_turned")
        message_ready = sem("message_ready")
        summed = sem("summed")
        turned_back = sem("turned_back")
        rows_ready = sem("rows_ready")
        block = ctx.enter_context(nc.Block())
        n_loads = (w is not None) + (relu_bias is not None)

        @block.sync
        def _(sp):
            if w is not None:
                sp.dma_start(w_sb[:, :], w).then_inc(weights_loaded, 16)
            if relu_bias is not None:
                sp.dma_start(bias_sb[:, :], relu_bias.rearrange("(p a) -> p a", a=1)).then_inc(weights_loaded, 16)

            def step(c, i, par):
                after(sp, summed, c - 1)
                sp.dma_start(same[:, par, :], g.flags[flags:flags + 1, bass.ds(c * C, C)].to_broadcast([P, C])
                             ).then_inc(flags_loaded[par], 16)

            steps(sp, step, 0)

        @block.gpsimd
        def _(pool):
            def fetch(c, i, par):
                after(pool, rows_weighted if weight is not None else message_turned, c - 1)
                pool.wait_ge(sources_ready, c + 1)
                pool.nop(nofuse=True)
                for u in range(U):
                    nc.gpsimd.indirect_dma_start(
                        out=rows[:, par, u, :], out_offset=None, in_=table,
                        in_offset=bass.IndirectOffsetOnAxis(ap=source_rows[:, par, u:u + 1], axis=0)
                    ).then_inc(gathered[par], 16)

            def send(c, i, par):
                pool.wait_ge(targets_ready, c + 1)
                pool.wait_ge(rows_ready, c + 1)
                pool.nop(nofuse=True)
                for u in range(U):
                    nc.gpsimd.indirect_dma_start(
                        out=out, out_offset=bass.IndirectOffsetOnAxis(ap=target_rows[:, par, u:u + 1], axis=0),
                        in_=done[:, par, u, :], in_offset=None).then_inc(scattered[par], 16)

            def step(c, i, par):
                if now := chunk_before(c, i, par, 0):
                    fetch(*now)
                if was := chunk_before(c, i, par, 2):
                    send(*was)

            steps(pool, step, 2)
            pool.wait_ge(scattered[0], 16 * U * (NC // 2 + 1))
            pool.wait_ge(scattered[1], 16 * U * (NC // 2))

        @block.tensor
        def _(pe):
            if n_loads:
                pe.wait_ge(weights_loaded, 16 * n_loads)

            def turn(c, i, par):
                if weight is not None:
                    pe.wait_ge(rows_weighted, c + 1)
                else:
                    pe.wait_ge(gathered[par], 16 * U * (i + 1))
                after(pe, message_ready if relu_bias is not None else summed, c - 1)
                for u in range(U):
                    x = (rows if weight is None else weighted)[:, par, u, :]
                    t = nc.tensor.transpose(turned[:, par, u * P:u * P + P], x, g.ident[:, :])
                t.then_inc(message_turned, 1)

            def finish(c, i, par):
                pe.wait_ge(summed, c + 1)
                after(pe, rows_ready, c - 1)
                for u in range(U):
                    x = total[:, par, u * P:u * P + P]
                    if w is None:
                        t = nc.tensor.transpose(back[:, par, u, :], x, g.ident[:, :])
                    else:
                        t = nc.tensor.matmul(back[:, par, u, :], x, w_sb[:, :], start=True, stop=True)
                t.then_inc(turned_back, 1)

            def step(c, i, par):
                if now := chunk_before(c, i, par, 0):
                    turn(*now)
                if was := chunk_before(c, i, par, 1):
                    finish(*was)

            steps(pe, step, 1)

        @block.vector
        def _(dve):
            def weigh(c, i, par):
                dve.wait_ge(gathered[par], 16 * U * (i + 1))
                after(dve, message_turned, c - 1)
                for u in range(U):
                    t = nc.vector.tensor_scalar(weighted[:, par, u, :], rows[:, par, u, :],
                                                g.col[:, weight, bass.ds(c * U + u, 1)], None, ALU.mult)
                t.then_inc(rows_weighted, 1)

            def scan(c, i, par):
                dve.wait_ge(message_ready if relu_bias is not None else message_turned, c + 1)
                after(dve, turned_back, c - 1)
                after(dve, summed, c)
                x = message[:, par, :] if relu_bias is not None else turned[:, par, :]
                first = isinstance(c, int) and c == 0
                dve.wait_ge(flags_loaded[par], 16 * (i + 1))
                nc.vector.tensor_tensor_scan(total[:, par, :], same[:, par, :], x,
                                             0.0 if first else total[:, 1 - par, C - 1:C],
                                             ALU.mult, ALU.add).then_inc(summed, 1)

            def step(c, i, par):
                if now := chunk_before(c, i, par, 0):
                    if weight is not None:
                        weigh(*now)
                    scan(*now)

            steps(dve, step, 0)

        @block.scalar
        def _(act):
            def point_to_sources(c, i, par):
                after(act, gathered[par], 16 * U * i)
                nc.scalar.copy(source_rows[:, par, :], g.idx[:, source, bass.ds(c * U, U)]
                               ).then_inc(sources_ready, 1)

            def relu(c, i, par):
                act.wait_ge(message_turned, c + 1)
                after(act, summed, c - 1)
                nc.scalar.activation(message[:, par, :], turned[:, par, :], ACT.Relu,
                                     bias=bias_sb[:, 0:1]).then_inc(message_ready, 1)

            def copy(c, i, par):
                after(act, scattered[par], 16 * U * i)
                act.nop(nofuse=True)
                nc.scalar.copy(target_rows[:, par, :], g.idx[:, target, bass.ds(c * U, U)]
                               ).then_inc(targets_ready, 1)
                act.wait_ge(turned_back, c + 1)
                if scale is None:
                    nc.scalar.activation(done[:, par, :, :], back[:, par, :, :], ACT.Copy).then_inc(rows_ready, 1)
                else:
                    act.nop(nofuse=True)
                    for u in range(U):
                        t = nc.scalar.activation(done[:, par, u, :], back[:, par, u, :], ACT.Copy,
                                                 scale=g.col[:, scale, bass.ds(c * U + u, 1)])
                    t.then_inc(rows_ready, 1)

            def step(c, i, par):
                if now := chunk_before(c, i, par, 0):
                    point_to_sources(*now)
                if relu_bias is not None and isinstance(c, int) and c == 0:
                    act.wait_ge(weights_loaded, 16 * n_loads)
                if relu_bias is not None and (was := chunk_before(c, i, par, 1)):
                    relu(*was)
                if was := chunk_before(c, i, par, 2):
                    copy(*was)

            steps(act, step, 2)


def attend(nc, g, name, table, wq, bq, wk, bk, wv, bv, out):
    with ExitStack() as ctx:
        def sb(n, shape, dt=F32):
            return ctx.enter_context(nc.sbuf_tensor(name + n, shape, dt))

        signal = signals(nc, ctx)

        def sem(n):
            return signal(name + n)

        def ps(n, shape):
            return ctx.enter_context(nc.psum_tensor(name + n, shape, F32))

        rows = sb("rows", [P, 2, 2, U, D])
        x_src = sb("x_src", [P, 2, C])
        x_dst = sb("x_dst", [P, 2, C])
        penalty = sb("penalty", [P, 2, C], BF16)
        query = sb("query", [P, C])
        qk = sb("qk", [P, C])
        top = sb("top", [P, 2, C + 1])
        enter = sb("enter", [P, 2, C])
        keep = sb("keep", [P, 2, C])
        mass = sb("mass", [P, 2, C])
        message = sb("message", [P, C])
        total = sb("total", [P, 2, C])
        share = sb("share", [P, U * HEADS])
        done = sb("done", [P, 2, U, D])
        source_rows = sb("source_rows", [P, 2, 2, U], I32)
        target_rows = sb("target_rows", [P, 2, U], I32)
        w_sb = sb("w", [D, 3, D])
        b_sb = sb("b", [D, 3])
        bq_scaled = sb("bq_scaled", [D, 1])
        t_src = ps("t_src", [P, C])
        t_dst = ps("t_dst", [P, C])
        key = ps("key", [P, C])
        raw_query = ps("raw_query", [P, C])
        value = ps("value", [P, C])
        score = ps("score", [P, C])
        back = ps("back", [P, U, D])
        mass_back = ps("mass_back", [P, U * HEADS])

        weights_loaded = sem("weights_loaded")
        bias_scaled = sem("bias_scaled")
        penalties_loaded = (sem("penalties_loaded0"), sem("penalties_loaded1"))
        sources_ready = sem("sources_ready")
        targets_ready = sem("targets_ready")
        gathered = (sem("gathered0"), sem("gathered1"))
        scattered = (sem("scattered0"), sem("scattered1"))
        turned = sem("turned")
        turned_copied = sem("turned_copied")
        keys_ready = sem("keys_ready")
        values_ready = sem("values_ready")
        query_ready = sem("query_ready")
        qk_ready = sem("qk_ready")
        scored = sem("scored")
        first_top = sem("first_top")
        top_ready = sem("top_ready")
        enter_shifted = sem("enter_shifted")
        keep_step = sem("keep_step")
        enter_ready = sem("enter_ready")
        keep_ready = sem("keep_ready")
        mass_ready = sem("mass_ready")
        message_ready = sem("message_ready")
        total_ready = sem("total_ready")
        turned_back = sem("turned_back")
        share_step = sem("share_step")
        rows_ready = sem("rows_ready")
        block = ctx.enter_context(nc.Block())
        SCALE = HD ** -0.5
        LAG = 3

        @block.sync
        def _(sp):
            for n, (w, b) in enumerate(((wk, bk), (wv, bv), (wq, bq))):
                sp.dma_start(w_sb[:, n, :], w).then_inc(weights_loaded, 16)
                sp.dma_start(b_sb[:, n:n + 1], b.rearrange("(p a) -> p a", a=1)).then_inc(weights_loaded, 16)

            def step(c, i, par):
                after(sp, keep_step, 2 * c - 2)
                sp.dma_start(penalty[:, par, :],
                             g.flags[PENALTY:PENALTY + 1, bass.ds(c * C, C)].to_broadcast([P, C])
                             ).then_inc(penalties_loaded[par], 16)

            steps(sp, step, 0)

        @block.gpsimd
        def _(pool):
            def fetch(c, i, par):
                after(pool, turned, c - 1)
                pool.wait_ge(sources_ready, c + 1)
                pool.nop(nofuse=True)
                for k in range(2):
                    for u in range(U):
                        nc.gpsimd.indirect_dma_start(
                            out=rows[:, par, k, u, :], out_offset=None, in_=table,
                            in_offset=bass.IndirectOffsetOnAxis(ap=source_rows[:, par, k, u:u + 1], axis=0)
                        ).then_inc(gathered[par], 16)

            def send(c, i, par):
                pool.wait_ge(targets_ready, c + 1)
                pool.wait_ge(rows_ready, c + 1)
                pool.nop(nofuse=True)
                for u in range(U):
                    nc.gpsimd.indirect_dma_start(
                        out=out, out_offset=bass.IndirectOffsetOnAxis(ap=target_rows[:, par, u:u + 1], axis=0),
                        in_=done[:, par, u, :], in_offset=None).then_inc(scattered[par], 16)

            def step(c, i, par):
                if now := chunk_before(c, i, par, 0):
                    fetch(*now)
                if was := chunk_before(c, i, par, LAG):
                    send(*was)

            steps(pool, step, LAG)
            pool.wait_ge(scattered[0], 16 * U * (NC // 2 + 1))
            pool.wait_ge(scattered[1], 16 * U * (NC // 2))

        @block.tensor
        def _(pe):
            def turn(c, i, par):
                pe.wait_ge(gathered[par], 2 * U * 16 * (i + 1))
                after(pe, turned_copied, c)
                for k, to in enumerate((t_src, t_dst)):
                    for u in range(U):
                        t = nc.tensor.transpose(to[:, u * P:u * P + P], rows[:, par, k, u, :], g.ident[:, :])
                t.then_inc(turned, 1)

            def keys(c, i, par):
                pe.wait_ge(turned_copied, c + 1)
                after(pe, qk_ready, c)
                nc.tensor.matmul(raw_query[:, :], w_sb[:, 2, :], x_dst[:, par, :], start=True, stop=True)
                nc.tensor.matmul(key[:, :], w_sb[:, 0, :], x_src[:, par, :], start=True,
                                 stop=True).then_inc(keys_ready, 1)

            def rate(c, i, par):
                pe.wait_ge(qk_ready, c + 1)
                after(pe, enter_shifted, c)
                nc.tensor.matmul(score[:, :], g.heads[:, :], qk[:, :], start=True, stop=True).then_inc(scored, 1)

            def values(c, i, par):
                after(pe, message_ready, c)
                nc.tensor.matmul(value[:, :], w_sb[:, 1, :], x_src[:, par, :], start=True,
                                 stop=True).then_inc(values_ready, 1)

            def finish(c, i, par):
                pe.wait_ge(total_ready, c + 1)
                pe.wait_ge(mass_ready, c + 1)
                after(pe, rows_ready, c)
                for u in range(U):
                    nc.tensor.matmul(mass_back[:, u * HEADS:u * HEADS + HEADS], mass[:, par, u * P:u * P + P],
                                     g.ident[:, 0:D:HD], start=True, stop=True)
                for u in range(U):
                    t = nc.tensor.transpose(back[:, u, :], total[:, par, u * P:u * P + P], g.ident[:, :])
                t.then_inc(turned_back, 1)

            def step(c, i, par):
                if now := chunk_before(c, i, par, 0):
                    turn(*now)
                if isinstance(c, int) and c == 0:
                    pe.wait_ge(weights_loaded, 16 * 6)
                if was := chunk_before(c, i, par, 1):
                    rate(*was)
                    values(*was)
                if now := chunk_before(c, i, par, 0):
                    keys(*now)
                if was := chunk_before(c, i, par, 2):
                    finish(*was)

            steps(pe, step, 2)

        @block.scalar
        def _(act):
            def copy(c, i, par):
                act.wait_ge(turned, c + 1)
                after(act, values_ready, c - 1)
                nc.scalar.activation(x_dst[:, par, :], t_dst[:, :], ACT.Copy)
                nc.scalar.activation(x_src[:, par, :], t_src[:, :], ACT.Copy).then_inc(turned_copied, 1)

            def ask(c, i, par):
                act.wait_ge(keys_ready, c + 1)
                after(act, qk_ready, c)
                nc.scalar.activation(query[:, :], raw_query[:, :], ACT.Identity, bias=bq_scaled[:, 0:1],
                                     scale=SCALE).then_inc(query_ready, 1)

            def exps(c, i, par):
                act.wait_ge(enter_shifted, c + 1)
                nc.scalar.activation(enter[:, par, :], enter[:, par, :], ACT.Exp).then_inc(enter_ready, 1)
                act.wait_ge(keep_step, 2 * c + 2)
                nc.scalar.activation(keep[:, par, :], keep[:, par, :], ACT.Exp).then_inc(keep_ready, 1)

            def point_to_sources(c, i, par):
                after(act, gathered[par], 2 * U * 16 * i)
                nc.scalar.copy(source_rows[:, par, :, :], g.idx[:, SRC_D:DST_D + 1, bass.ds(c * U, U)]
                               ).then_inc(sources_ready, 1)

            def point_to_targets(c, i, par):
                after(act, scattered[par], 16 * U * i)
                nc.scalar.copy(target_rows[:, par, :], g.idx[:, OUT_D, bass.ds(c * U, U)]
                               ).then_inc(targets_ready, 1)

            def step(c, i, par):
                if now := chunk_before(c, i, par, 0):
                    point_to_sources(*now)
                if isinstance(c, int) and c == 0:
                    act.wait_ge(bias_scaled, 1)
                if was := chunk_before(c, i, par, 1):
                    copy(*was)
                    ask(*was)
                if was := chunk_before(c, i, par, 2):
                    exps(*was)
                if was := chunk_before(c, i, par, LAG):
                    point_to_targets(*was)

            steps(act, step, LAG)

        @block.vector
        def _(dve):
            def multiply(c, i, par):
                dve.wait_ge(query_ready, c + 1)
                after(dve, scored, c)
                nc.vector.scalar_tensor_tensor(out=qk[:, :], in0=key[:, :], scalar=b_sb[:, 0:1],
                                               in1=query[:, :], op0=ALU.add, op1=ALU.mult
                                               ).then_inc(qk_ready, 1)

            def shift(c, i, par):
                if isinstance(c, int) and c == 0:
                    nc.vector.memset(top[:, 0, 0:1], 0.0).then_inc(first_top, 1)
                else:
                    dve.wait_ge(top_ready, c)
                    nc.vector.tensor_copy(top[:, par, 0:1], top[:, 1 - par, C:C + 1]).then_inc(first_top, 1)
                dve.wait_ge(first_top, c + 1)
                dve.wait_ge(scored, c + 1)
                dve.wait_ge(penalties_loaded[par], 16 * (i + 1))
                nc.vector.tensor_tensor_scan(top[:, par, 1:C + 1], penalty[:, par, :], score[:, :], top[:, par, 0:1],
                                             ALU.add, ALU.max).then_inc(top_ready, 1)
                after(dve, total_ready, c - 1)
                dve.wait_ge(top_ready, c + 1)
                nc.vector.tensor_tensor(keep[:, par, :], top[:, par, 0:C], penalty[:, par, :], ALU.add).then_inc(keep_step, 1)
                nc.vector.tensor_tensor(enter[:, par, :], score[:, :], top[:, par, 1:C + 1], ALU.subtract
                                        ).then_inc(enter_shifted, 1)
                dve.wait_ge(keep_step, 2 * c + 1)
                nc.vector.tensor_tensor(keep[:, par, :], keep[:, par, :], top[:, par, 1:C + 1], ALU.subtract
                                        ).then_inc(keep_step, 1)

            def add_up(c, i, par):
                first = isinstance(c, int) and c == 0
                dve.wait_ge(enter_ready, c + 1)
                dve.wait_ge(values_ready, c + 1)
                after(dve, total_ready, c)
                nc.vector.scalar_tensor_tensor(out=message[:, :], in0=value[:, :], scalar=b_sb[:, 1:2],
                                               in1=enter[:, par, :], op0=ALU.add, op1=ALU.mult
                                               ).then_inc(message_ready, 1)
                dve.wait_ge(keep_ready, c + 1)
                after(dve, turned_back, c - 1)
                after(dve, mass_ready, c)
                nc.vector.tensor_tensor_scan(mass[:, par, :], keep[:, par, :], enter[:, par, :],
                                             0.0 if first else mass[:, 1 - par, C - 1:C],
                                             ALU.mult, ALU.add).then_inc(mass_ready, 1)
                dve.wait_ge(message_ready, c + 1)
                nc.vector.tensor_tensor_scan(total[:, par, :], keep[:, par, :], message[:, :],
                                             0.0 if first else total[:, 1 - par, C - 1:C],
                                             ALU.mult, ALU.add).then_inc(total_ready, 1)

            def divide(c, i, par):
                dve.wait_ge(turned_back, c + 1)
                after(dve, rows_ready, c)
                nc.vector.tensor_scalar(share[:, :], mass_back[:, :], 1e-16, None, ALU.add).then_inc(share_step, 1)
                dve.wait_ge(share_step, 2 * c + 1)
                nc.vector.reciprocal(share[:, :], share[:, :]).then_inc(share_step, 1)
                dve.wait_ge(share_step, 2 * c + 2)
                after(dve, scattered[par], 16 * U * i)
                nc.vector.tensor_tensor(done[:, par, :, :].rearrange("p u (h d) -> p (u h) d", h=HEADS),
                                        back[:, :, :].rearrange("p u (h d) -> p (u h) d", h=HEADS),
                                        share[:, :].rearrange("p (a b) -> p a b", b=1).to_broadcast(
                                            [P, U * HEADS, HD]), ALU.mult).then_inc(rows_ready, 1)

            dve.wait_ge(weights_loaded, 16 * 6)
            nc.vector.tensor_scalar(bq_scaled[:, :], b_sb[:, 2:3], SCALE, None, ALU.mult).then_inc(bias_scaled, 1)

            def step(c, i, par):
                if was := chunk_before(c, i, par, 1):
                    shift(*was)
                if now := chunk_before(c, i, par, 0):
                    multiply(*now)
                if was := chunk_before(c, i, par, 2):
                    divide(*was)
                if was := chunk_before(c, i, par, 1):
                    add_up(*was)

            steps(dve, step, 2)


ADD, TWICE, CONV, LAST, RELU = range(5)
RING = 10
DEPTH = 5


def group_steps(eng, step, lag):
    head = NG % RING + RING
    for n in range(head):
        step(n // RING, n % RING)
    with eng.Fori(1, (NG - head) // RING + 1) as i:
        for r in range(RING):
            step(i + (head % RING + r) // RING, (head % RING + r) % RING)
    for n in range(NG, NG + lag):
        step(n // RING, n % RING)


def group_before(q, m, lag):
    if isinstance(q, int) and not 0 <= RING * q + m - lag < NG:
        return None
    return (q, m - lag) if m >= lag else (q - 1, m + RING - lag)


def update_nodes(nc, g, name, kind, h, agg, out, bias=None, ws=None, gain=None, offset=None, outer=None):
    with ExitStack() as ctx:
        def sb(n, shape, dt=F32):
            return ctx.enter_context(nc.sbuf_tensor(name + n, shape, dt))

        signal = signals(nc, ctx)

        def sem(n):
            return signal(name + n)

        conv = kind in (CONV, LAST)
        R = RING if kind == CONV else DEPTH
        node = sb("node", [NP, R, G, D])
        agg_in = sb("agg_in", [NP, DEPTH, G, D])
        y = sb("y", [NP, DEPTH, G, D])
        z = sb("z", [NP, DEPTH, G, D]) if conv else None
        outer_in = sb("outer_in", [NP, DEPTH, G, D]) if kind == LAST else None
        result = sb("result", [NP, DEPTH, G, D])
        turned_sb = sb("turned_sb", [D, 2, G, P]) if conv else None
        w_sb = sb("w_sb", [D, D])
        if conv:
            bias_row = sb("bias_row", [P, 4, D])
            ones_row = sb("ones_row", [P, P])
        on_all = sb("on_all", [NP, 3, D])
        stats = sb("stats", [NP, G, 6])
        mean_var = sb("mean_var", [NP, 2, G, 2])
        var = sb("var", [NP, G])
        minus_half = sb("minus_half", [NP, G])
        negated = sb("negated", [NP, G])
        rstd = sb("rstd", [NP, 2, G])
        shift = sb("shift", [NP, 2, G])
        if conv:
            turned = ctx.enter_context(nc.psum_tensor(name + "turned", [D, 2, G, P], F32))
            product = ctx.enter_context(nc.psum_tensor(name + "product", [P, 2, G, D], F32))

        consts_loaded = sem("consts_loaded")
        first_rows_ready = sem("first_rows_ready")
        node_loaded = [sem(f"node_loaded{m}") for m in range(R)]
        agg_loaded = [sem(f"agg_loaded{m}") for m in range(DEPTH)]
        outer_loaded = [sem(f"outer_loaded{m}") for m in range(DEPTH)] if kind == LAST else None
        stored = [sem(f"stored{m}") for m in range(DEPTH)]
        bias_added = sem("bias_added")
        other_bias_added = sem("other_bias_added")
        turned_ready = sem("turned_ready")
        turned_copied = sem("turned_copied")
        product_ready = sem("product_ready")
        sum_ready = sem("sum_ready")
        activated = sem("activated")
        outer_added = sem("outer_added")
        stats_ready = sem("stats_ready")
        mean_var_ready = sem("mean_var_ready")
        halves_ready = sem("halves_ready")
        var_ready = sem("var_ready")
        root_ready = sem("root_ready")
        norm_ready = sem("norm_ready")
        normed = sem("normed")
        scaled = sem("scaled")
        offset_added = sem("offset_added")
        other_offset_added = sem("other_offset_added")
        result_ready = sem("result_ready")
        block = ctx.enter_context(nc.Block())

        parts = (slice(0, SPLIT), slice(SPLIT, NP))
        consts = [(w_sb[:, :], ws)] if conv else []
        if conv:
            consts += [(bias_row[0:1, j, :], bias.rearrange("(a f) -> a f", a=1)) for j in range(4)]
        for n, v in enumerate((None if conv else bias, gain, offset)):
            if v is not None:
                consts.append((on_all[:, n, :], v.rearrange("(a f) -> a f", a=1).to_broadcast([NP, D])))
        ADDED = 2 if conv else 1 if bias is not None else 0
        MEASURED = 3 if kind == LAST else ADDED
        NORMED = MEASURED + 1
        ACTIVATED = 4 if kind == CONV else 2
        STORED = 8

        def number(q, m):
            return RING * q + m

        def uses(q, m, ring):
            return q * (RING // ring) + m // ring + 1

        def of_group(table, s, grp):
            return table[0:N, :].rearrange("(p r) f -> p (r f)", r=RP)[s, bass.ds(grp * G * D, G * D)]

        BIAS_SPLIT = 6
        OFFSET_SPLIT = 3

        def row_of(n, tiles=G):
            return on_all[:, n:n + 1, :].to_broadcast([NP, tiles, D])

        @block.sync
        def _(sp):
            def load(q, m):
                grp = number(q, m)
                after(sp, {CONV: result_ready, LAST: turned_ready}.get(kind, sum_ready), grp + 1 - R)
                for s in parts:
                    sp.dma_start(node[s, m % R, :, :].rearrange("p a f -> p (a f)"), of_group(h, s, grp)
                                 ).then_inc(node_loaded[m % R], 16)
                after(sp, sum_ready, grp + 1 - DEPTH)
                for s in parts:
                    sp.dma_start(agg_in[s, m % DEPTH, :, :].rearrange("p a f -> p (a f)"), of_group(agg, s, grp)
                                 ).then_inc(agg_loaded[m % DEPTH], 16)
                if kind == LAST:
                    after(sp, outer_added, grp + 1 - DEPTH)
                    for s in parts:
                        sp.dma_start(outer_in[s, m % DEPTH, :, :].rearrange("p a f -> p (a f)"),
                                     of_group(outer, s, grp)).then_inc(outer_loaded[m % DEPTH], 16)

            def store(q, m):
                sp.wait_ge(result_ready if kind == CONV else normed, number(q, m) + 1)
                for s in parts:
                    sp.dma_start(of_group(out, s, number(q, m)),
                                 result[s, m % DEPTH, :, :].rearrange("p a f -> p (a f)")
                                 ).then_inc(stored[m % DEPTH], 16)

            def step(q, m):
                if now := group_before(q, m, 0):
                    load(*now)
                if isinstance(q, int) and q == 0 and m == 0:
                    if conv:
                        sp.wait_ge(first_rows_ready, 2)
                    for to, v in consts:
                        sp.dma_start(to, v).then_inc(consts_loaded, 16)
                if was := group_before(q, m, STORED):
                    store(*was)

            group_steps(sp, step, STORED)
            for m in range(DEPTH):
                sp.wait_ge(stored[m], 32 * len(range(m, NG, DEPTH)))

        @block.gpsimd
        def _(pool):
            nc.gpsimd.memset(minus_half[:, :], -0.5).then_inc(halves_ready, 1)
            pool.wait_ge(halves_ready, 1)
            if consts:
                pool.wait_ge(consts_loaded, 16 * len(consts))

            def add_bias(q, m):
                pool.wait_ge(agg_loaded[m % DEPTH], 32 * uses(q, m, DEPTH))
                part = agg_in[:, m % DEPTH, 0:BIAS_SPLIT, :]
                nc.gpsimd.tensor_tensor(part, part, row_of(0, BIAS_SPLIT), ALU.add).then_inc(bias_added, 1)

            def root(q, m):
                grp = number(q, m)
                pool.wait_ge(mean_var_ready, grp + 1)
                after(pool, normed, grp - 1)
                after(pool, norm_ready, grp)
                pool.nop(nofuse=True)
                nc.gpsimd.tensor_scalar(var[:, :], mean_var[:, m % 2, :, 1], EPS, None, ALU.add
                                        ).then_inc(var_ready, 1)
                nc.gpsimd.tensor_scalar(negated[:, :], mean_var[:, m % 2, :, 0], -1.0, None, ALU.mult
                                        ).then_inc(root_ready, 1)
                pool.wait_ge(var_ready, grp + 1)
                nc.gpsimd.tensor_tensor(rstd[:, m % 2, :], var[:, :], minus_half[:, :], ALU.pow
                                        ).then_inc(root_ready, 1)
                pool.wait_ge(root_ready, 2 * grp + 2)
                nc.gpsimd.tensor_tensor(shift[:, m % 2, :], negated[:, :], rstd[:, m % 2, :], ALU.mult
                                        ).then_inc(norm_ready, 1)

            def affine(q, m):
                grp = number(q, m)
                pool.wait_ge(normed, grp + 1)
                nc.gpsimd.tensor_tensor(z[:, m % DEPTH, :, :], z[:, m % DEPTH, :, :], row_of(1), ALU.mult
                                        ).then_inc(scaled, 1)
                pool.wait_ge(scaled, grp + 1)
                part = z[:, m % DEPTH, 0:OFFSET_SPLIT, :]
                nc.gpsimd.tensor_tensor(part, part, row_of(2, OFFSET_SPLIT), ALU.add).then_inc(offset_added, 1)

            def step(q, m):
                if bias is not None and not conv and (now := group_before(q, m, 0)):
                    add_bias(*now)
                if was := group_before(q, m, NORMED):
                    root(*was)
                if kind == CONV and (was := group_before(q, m, ACTIVATED)):
                    affine(*was)

            group_steps(pool, step, ACTIVATED if kind == CONV else NORMED)

        @block.tensor
        def _(pe):
            if not conv:
                return
            def turn(q, m):
                p = m % 2
                pe.wait_ge(node_loaded[m % R], 32 * uses(q, m, R))
                after(pe, turned_copied, number(q, m) - 1)
                for j in range(G):
                    t = nc.tensor.transpose(turned[:, p, j, 0:NP], node[:, m % R, j, :], g.ident[0:NP, 0:NP])
                t.then_inc(turned_ready, 1)

            def project(q, m):
                grp = number(q, m)
                p = m % 2
                pe.wait_ge(turned_copied, grp + 1)
                after(pe, sum_ready, grp - 1)
                for k in range(0, G, 4):
                    nc.tensor.matmul(product[0:NP, p, k:k + 4, :].rearrange("p a f -> p (a f)"),
                                     ones_row[:, 0:NP], bias_row[:, :, :].rearrange("p a f -> p (a f)"),
                                     start=True, stop=False, skip_group_check=True)
                    for j in range(k, k + 4):
                        t = nc.tensor.matmul(product[0:NP, p, j, :], turned_sb[:, p, j, 0:NP], w_sb[:, :],
                                             start=False, stop=j == k + 3, skip_group_check=True)
                t.then_inc(product_ready, 1)

            def step(q, m):
                if isinstance(q, int) and q == 0 and m == 1:
                    pe.wait_ge(consts_loaded, 16 * len(consts))
                    pe.wait_ge(first_rows_ready, 3)
                if was := group_before(q, m, 1):
                    project(*was)
                if now := group_before(q, m, 0):
                    turn(*now)

            group_steps(pe, step, 1)

        @block.scalar
        def _(act):
            def copy(q, m):
                grp = number(q, m)
                act.wait_ge(turned_ready, grp + 1)
                after(act, product_ready, grp - 1)
                nc.scalar.activation(turned_sb[:, m % 2, :, 0:NP], turned[:, m % 2, :, 0:NP],
                                     ACT.Copy).then_inc(turned_copied, 1)

            def normalize(q, m):
                grp = number(q, m)
                act.wait_ge(norm_ready, grp + 1)
                if kind == CONV:
                    after(act, result_ready, grp + 1 - DEPTH)
                    to = z[:, m % DEPTH, :, :]
                else:
                    after(act, stored[m % DEPTH], 32 * (uses(q, m, DEPTH) - 1))
                    to = result[:, m % DEPTH, :, :]
                x = (z if kind == LAST else y)[:, m % DEPTH, :, :]
                for j in range(G):
                    t = nc.scalar.activation(to[:, j, :], x[:, j, :], ACT.Identity,
                                             bias=shift[:, m % 2, j:j + 1], scale=rstd[:, m % 2, j:j + 1])
                t.then_inc(normed, 1)

            def gelu(q, m):
                act.wait_ge(offset_added if kind == CONV else sum_ready, number(q, m) + 1)
                if kind == CONV:
                    act.wait_ge(other_offset_added, number(q, m) + 1)
                x = (z if kind == CONV else y)[:, m % DEPTH, :, :]
                nc.scalar.activation(x, x, ACT.Gelu).then_inc(activated, 1)

            def step(q, m):
                if conv and (now := group_before(q, m, 0)):
                    copy(*now)
                if kind == LAST and (was := group_before(q, m, ACTIVATED)):
                    gelu(*was)
                if was := group_before(q, m, NORMED):
                    normalize(*was)
                if kind == CONV and (was := group_before(q, m, ACTIVATED)):
                    gelu(*was)

            group_steps(act, step, max(NORMED, ACTIVATED))

        @block.vector
        def _(dve):
            if conv:
                nc.vector.memset(bias_row[:, :, :], 0.0).then_inc(first_rows_ready, 1)
                nc.vector.memset(ones_row[:, :], 0.0).then_inc(first_rows_ready, 1)
                dve.wait_ge(first_rows_ready, 2)
                nc.vector.memset(ones_row[0:1, :], 1.0).then_inc(first_rows_ready, 1)
            if consts:
                dve.wait_ge(consts_loaded, 16 * len(consts))

            def bias_rest(q, m):
                dve.wait_ge(agg_loaded[m % DEPTH], 32 * uses(q, m, DEPTH))
                part = agg_in[:, m % DEPTH, BIAS_SPLIT:G, :]
                nc.vector.tensor_tensor(part, part, row_of(0, G - BIAS_SPLIT), ALU.add
                                        ).then_inc(other_bias_added, 1)

            def add(q, m):
                grp = number(q, m)
                if conv:
                    dve.wait_ge(product_ready, grp + 1)
                else:
                    dve.wait_ge(node_loaded[m % R], 32 * uses(q, m, R))
                if bias is not None and not conv:
                    dve.wait_ge(bias_added, grp + 1)
                    dve.wait_ge(other_bias_added, grp + 1)
                else:
                    dve.wait_ge(agg_loaded[m % DEPTH], 32 * uses(q, m, DEPTH))
                after(dve, outer_added if kind == LAST else normed, grp + 1 - DEPTH)
                to = y[:, m % DEPTH, :, :]
                a = agg_in[:, m % DEPTH, :, :]
                if conv:
                    ins = nc.vector.tensor_tensor(to, product[0:NP, m % 2, :, :], a, ALU.add)
                elif kind == ADD:
                    ins = nc.vector.tensor_tensor(to, node[:, m % R, :, :], a, ALU.add)
                elif kind == TWICE:
                    ins = nc.vector.scalar_tensor_tensor(out=to, in0=node[:, m % R, :, :], scalar=2.0,
                                                         in1=a, op0=ALU.mult, op1=ALU.add)
                else:
                    ins = nc.vector.scalar_tensor_tensor(out=to, in0=a, scalar=0.0,
                                                         in1=node[:, m % R, :, :], op0=ALU.max, op1=ALU.add)
                ins.then_inc(sum_ready, 1)

            def add_outer(q, m):
                grp = number(q, m)
                dve.wait_ge(activated, grp + 1)
                dve.wait_ge(outer_loaded[m % DEPTH], 32 * uses(q, m, DEPTH))
                after(dve, normed, grp + 1 - DEPTH)
                nc.vector.tensor_tensor(z[:, m % DEPTH, :, :], y[:, m % DEPTH, :, :], outer_in[:, m % DEPTH, :, :],
                                        ALU.add).then_inc(outer_added, 1)

            def measure(q, m, n):
                grp = number(q, m)
                if n == 0:
                    dve.wait_ge(outer_added if kind == LAST else sum_ready, grp + 1)
                    after(dve, mean_var_ready, grp)
                if n == G:
                    after(dve, norm_ready, grp - 1)
                    dve.wait_ge(stats_ready, grp + 1)
                    dve.nop(nofuse=True)
                if n < G:
                    x = (z if kind == LAST else y)[:, m % DEPTH, n, :]
                    ins = nc.vector.bn_stats(stats[:, n, :], x)
                    if n == G - 1:
                        ins.then_inc(stats_ready, 1)
                else:
                    ins = nc.vector.bn_aggr(mean_var[:, m % 2, n - G, :], stats[:, n - G, :])
                    if n == 2 * G - 1:
                        ins.then_inc(mean_var_ready, 1)

            def offset_rest(q, m):
                grp = number(q, m)
                dve.wait_ge(scaled, grp + 1)
                part = z[:, m % DEPTH, OFFSET_SPLIT:G, :]
                nc.vector.tensor_tensor(part, part, row_of(2, G - OFFSET_SPLIT), ALU.add
                                        ).then_inc(other_offset_added, 1)

            def keep_on(q, m):
                grp = number(q, m)
                dve.wait_ge(activated, grp + 1)
                after(dve, stored[m % DEPTH], 32 * (uses(q, m, DEPTH) - 1))
                nc.vector.tensor_tensor(result[:, m % DEPTH, :, :], node[:, m % R, :, :], z[:, m % DEPTH, :, :],
                                        ALU.add).then_inc(result_ready, 1)

            def step(q, m):
                if bias is not None and not conv and (now := group_before(q, m, 0)):
                    bias_rest(*now)
                if was := group_before(q, m, ADDED):
                    add(*was)
                if kind == LAST and (was := group_before(q, m, MEASURED)):
                    add_outer(*was)
                if was := group_before(q, m, MEASURED):
                    for n in range(2 * G):
                        measure(*was, n)
                if kind == CONV and (was := group_before(q, m, ACTIVATED + 1)):
                    keep_on(*was)
                if kind == CONV and (was := group_before(q, m, ACTIVATED)):
                    offset_rest(*was)

            group_steps(dve, step, ACTIVATED + 1 if kind == CONV else MEASURED)


def build(nc, x, src, dst, edge_weight, w1, b1, w2, b2, wq, bq, wk, bk, wv, bv, ws, bs, ln_g, ln_b, w3, b3, out):
    def dram(name, shape, dt=F32):
        return nc.dram_tensor(name, shape, dt).ap()

    g = Program()
    g.agg_s = dram("agg_s", [TRASH + EP, D])
    g.agg_d = dram("agg_d", [TRASH + EP, D])
    g.he = dram("he", [NH + EP, D])
    by_low = [dram(f"by_low{k}", [EP, 4]) for k in range(2)]
    by_key = [dram(f"by_key{k}", [EP + 2, 4]) for k in range(2)]
    cols = dram("cols", [NCOL, EP])
    g.flags = dram("flags", [3, EP], BF16)
    h = [dram(f"h{n}", [N, D]) for n in range(3)]

    with ExitStack() as ctx:
        constants(nc, ctx, g)
        with (
            nc.sbuf_tensor("pay0", [P, T, 4], F32) as pay0,
            nc.sbuf_tensor("pay1", [P, T, 4], F32) as pay1,
            nc.sbuf_tensor("digit", [P, 4, T], F32) as digit,
            nc.sbuf_tensor("border", [P, 4, T], F32) as border,
            nc.psum_tensor("counts", [P, 4, 512], F32) as counts,
        ):
            count_digits(nc, g, dst, src, edge_weight, pay0, digit, border, counts)
            rank_pass(nc, g, 0, (digit[:, 0, :], digit[:, 2, :]), (pay0, pay0), counts, by_low, 0, g.agg_s[0:N, :],
                      next_border=(border[:, 1, :], border[:, 3, :]))
            second_digit(nc, g, by_low, (digit[:, 1, :], digit[:, 3, :]), (pay0, pay1))
            rank_pass(nc, g, 1, (digit[:, 1, :], digit[:, 3, :]), (pay0, pay1), counts, by_key, 1, g.agg_d[0:N, :])
        describe(nc, g, by_key, cols)

        sum_segments(nc, g, "a", x, SAME_D, SRC_D, OUT_HE, g.he, w=w1, scale=CNT_D)
        sum_segments(nc, g, "b", g.he[0:NH, :], SAME_S, HE_S, OUT_S, g.agg_s, scale=CNT_S)
        sum_segments(nc, g, "c", g.agg_s[0:N, :], SAME_D, SRC_D, OUT_HE, g.he, relu_bias=b1, w=w2, scale=CNT_D)
        sum_segments(nc, g, "d", g.he[0:NH, :], SAME_S, HE_S, OUT_S, g.agg_s, scale=CNT_S)
        update_nodes(nc, g, "e", ADD, x, g.agg_s, h[0], bias=b2)

        sum_segments(nc, g, "f", h[0], SAME_D, SRC_D, OUT_D, g.agg_d)
        update_nodes(nc, g, "g", TWICE, h[0], g.agg_d, h[1])

        at = 1
        for n in range(LAYERS):
            attend(nc, g, f"h{n}", h[at], wq[n], bq[n], wk[n], bk[n], wv[n], bv[n], g.agg_d)
            to = 2 if at == 0 else 0
            if n < LAYERS - 1:
                update_nodes(nc, g, f"i{n}", CONV, h[at], g.agg_d, h[to], bias=bs[n], ws=ws[n], gain=ln_g[n],
                             offset=ln_b[n])
            else:
                update_nodes(nc, g, f"i{n}", LAST, h[at], g.agg_d, h[to], bias=bs[n], ws=ws[n], outer=h[1])
            at = to

        sum_segments(nc, g, "j", h[at], SAME_D, SRC_D, OUT_D, g.agg_d, weight=WEIGHT, w=w3)
        update_nodes(nc, g, "k", RELU, h[at], g.agg_d, out, bias=b3)


_INS = ["x", "src", "dst", "edge_weight", "L0_gnn_W1", "L0_gnn_b1", "L0_gnn_W2", "L0_gnn_b2", "L2_gnn_Wq",
        "L2_gnn_bq", "L2_gnn_Wk", "L2_gnn_bk", "L2_gnn_Wv", "L2_gnn_bv", "L2_gnn_Ws", "L2_gnn_bs", "L2_gnn_ln_g",
        "L2_gnn_ln_b", "L3_gnn_weight", "L3_gnn_bias"]


def kernel(**inputs):
    import numpy as np
    import concourse.bacc as bacc
    from concourse.bass_utils import run_bass_kernel_spmd

    nc = bacc.Bacc("TRN2", target_bir_lowering=False, num_devices=1)
    arrays, args = {}, []
    for name in _INS:
        a = np.ascontiguousarray(inputs[name])
        arrays[f"in_{name}"] = a
        args.append(nc.dram_tensor(f"in_{name}", a.shape, mybir.dt.from_np(a.dtype), kind="ExternalInput").ap())
    args.append(nc.dram_tensor("out", (N, D), F32, kind="ExternalOutput").ap())
    build(nc, *args)
    r = run_bass_kernel_spmd(nc, [arrays], core_ids=[0])
    return r.results[0]["out"]
```
